# Optimizing a Trainium2 kernel written in Bass

```python
import numpy as np
import jax
import jax.numpy as jnp

def _softmax(x, axis=-1):
    return jax.nn.softmax(x, axis=axis)

def _gelu(x):
    return jax.nn.gelu(x, approximate=True)

def _silu(x):
    return jax.nn.silu(x)

def _sigmoid(x):
    return jax.nn.sigmoid(x)

def _layernorm(x, axis=-1, eps=1e-05):
    m = jnp.mean(x, axis=axis, keepdims=True)
    v = jnp.var(x, axis=axis, keepdims=True)
    return (x - m) / jnp.sqrt(v + eps)

def _scatter_add(tgt, idx, src, axis=0):
    return tgt.at[idx].add(src)

def _segment_sum(src, seg, n):
    return jax.ops.segment_sum(src, seg, n)
kernel_name = 'mk_seq_postln_d1_jaxref_r8_516b1a'

def setup_inputs(seed: int=0):
    np.random.seed(seed)
    _w = jnp.asarray

    def _L0_attn_setup():
        import jax, jax.numpy as jnp
        import numpy as np
        BATCH, SEQ, D_MODEL = (4, 256, 128)
        D_STATE, D_CONV, EXPAND, HEADDIM = (64, 4, 2, 64)
        D_INNER = EXPAND * D_MODEL
        NHEADS = D_INNER // HEADDIM
        CONV_DIM = D_INNER + 2 * D_STATE
        D_IN_PROJ = 2 * D_INNER + 2 * D_STATE + NHEADS
        EPS = 1e-05

        def mamba2(X, W_in, conv_w, conv_b, dt_bias, A_log, D, norm_w, W_out):
            b, l, _ = X.shape
            zxbcdt = X @ W_in.T
            z, xBC, dt = jnp.split(zxbcdt, [D_INNER, D_INNER + CONV_DIM], axis=-1)
            dt = jax.nn.softplus(dt + dt_bias)
            xBC_t = xBC.transpose(0, 2, 1)
            ker = conv_w[:, None, :]
            xBC_c = jax.lax.conv_general_dilated(xBC_t, ker, window_strides=(1,), padding=[(D_CONV - 1, 0)], feature_group_count=CONV_DIM)
            xBC = jax.nn.silu(xBC_c.transpose(0, 2, 1) + conv_b)
            x, Bm, Cm = jnp.split(xBC, [D_INNER, D_INNER + D_STATE], axis=-1)
            xh = x.reshape(b, l, NHEADS, HEADDIM)
            A = -jnp.exp(A_log)
            dA = jnp.exp(dt * A)
            dBx = jnp.einsum('blh,bln,blhp->blhpn', dt, Bm, xh)

            def step(h, inp):
                dA_t, dBx_t, C_t = inp
                h = h * dA_t[:, :, None, None] + dBx_t
                y = jnp.einsum('bhpn,bn->bhp', h, C_t)
                return (h, y)
            h0 = jnp.zeros((b, NHEADS, HEADDIM, D_STATE), X.dtype)
            _, ys = jax.lax.scan(step, h0, (dA.transpose(1, 0, 2), dBx.transpose(1, 0, 2, 3, 4), Cm.transpose(1, 0, 2)))
            y = ys.transpose(1, 0, 2, 3) + D[None, None, :, None] * xh
            y = y.reshape(b, l, D_INNER)
            y = y * jax.nn.silu(z)
            y = y * jax.lax.rsqrt(jnp.mean(y * y, axis=-1, keepdims=True) + EPS) * norm_w
            return y @ W_out.T
        key = jax.random.key(seed)
        ks = jax.random.split(key, 6)
        s = 0.02
        return {'X': jax.random.normal(ks[0], (BATCH, SEQ, D_MODEL), jnp.float32), 'W_in': jax.random.normal(ks[1], (D_IN_PROJ, D_MODEL), jnp.float32) * s, 'conv_w': jax.random.normal(ks[2], (CONV_DIM, D_CONV), jnp.float32) * s, 'conv_b': jnp.zeros((CONV_DIM,), jnp.float32), 'dt_bias': jax.random.uniform(ks[3], (NHEADS,), jnp.float32), 'A_log': jnp.log(jax.random.uniform(ks[4], (NHEADS,), jnp.float32, minval=1.0, maxval=16.0)), 'D': jnp.ones((NHEADS,), jnp.float32), 'norm_w': jnp.ones((D_INNER,), jnp.float32), 'W_out': jax.random.normal(ks[5], (D_MODEL, D_INNER), jnp.float32) * s}
    _L0_attn_in = _L0_attn_setup()

    def _L0_ffn_setup():
        import jax, jax.numpy as jnp
        import numpy as np
        B, S, D, H, E, K, F = (1, 128, 128, 16, 8, 2, 512)

        def layernorm(x, g, b, eps=1e-05):
            m = x.mean(-1, keepdims=True)
            v = ((x - m) ** 2).mean(-1, keepdims=True)
            return (x - m) * jax.lax.rsqrt(v + eps) * g + b
        key = jax.random.key(seed)
        ks = jax.random.split(key, 8)
        n = lambda k, shape, sc: jax.random.normal(k, shape, dtype=jnp.float32) * sc
        return {'x': n(ks[0], (B, S, D), 1.0), 'w_qkv': n(ks[1], (D, 3 * D), D ** (-0.5)), 'w_o': n(ks[2], (D, D), D ** (-0.5)), 'g1': jnp.ones((D,), jnp.float32), 'b1': jnp.zeros((D,), jnp.float32), 'wg': n(ks[3], (D, E), D ** (-0.5)), 'w1': n(ks[4], (E, D, F), D ** (-0.5)), 'bb1': jnp.zeros((E, F), jnp.float32), 'w2': n(ks[5], (E, F, D), F ** (-0.5)), 'bb2': jnp.zeros((E, D), jnp.float32), 'g2': jnp.ones((D,), jnp.float32), 'b2': jnp.zeros((D,), jnp.float32)}
    _L0_ffn_in = _L0_ffn_setup()
    _d = {'L0_attn_X': _L0_attn_in['X'], 'L0_attn_W_in': _L0_attn_in['W_in'], 'L0_attn_conv_w': _L0_attn_in['conv_w'], 'L0_attn_conv_b': _L0_attn_in['conv_b'], 'L0_attn_dt_bias': _L0_attn_in['dt_bias'], 'L0_attn_A_log': _L0_attn_in['A_log'], 'L0_attn_D': _L0_attn_in['D'], 'L0_attn_norm_w': _L0_attn_in['norm_w'], 'L0_attn_W_out': _L0_attn_in['W_out'], 'L0_ffn_w_qkv': _L0_ffn_in['w_qkv'], 'L0_ffn_w_o': _L0_ffn_in['w_o'], 'L0_ffn_g1': _L0_ffn_in['g1'], 'L0_ffn_b1': _L0_ffn_in['b1'], 'L0_ffn_wg': _L0_ffn_in['wg'], 'L0_ffn_w1': _L0_ffn_in['w1'], 'L0_ffn_bb1': _L0_ffn_in['bb1'], 'L0_ffn_w2': _L0_ffn_in['w2'], 'L0_ffn_bb2': _L0_ffn_in['bb2'], 'L0_ffn_g2': _L0_ffn_in['g2'], 'L0_ffn_b2': _L0_ffn_in['b2']}
    _x0 = _d['L0_attn_X']
    _d['L0_attn_X'] = jax.random.normal(jax.random.fold_in(jax.random.key(seed), 1), (8, 512, 128), dtype=_x0.dtype)
    del _x0
    return _d

def reference(L0_attn_X, L0_attn_W_in, L0_attn_conv_w, L0_attn_conv_b, L0_attn_dt_bias, L0_attn_A_log, L0_attn_D, L0_attn_norm_w, L0_attn_W_out, L0_ffn_w_qkv, L0_ffn_w_o, L0_ffn_g1, L0_ffn_b1, L0_ffn_wg, L0_ffn_w1, L0_ffn_bb1, L0_ffn_w2, L0_ffn_bb2, L0_ffn_g2, L0_ffn_b2):

    def _L0_attn_ref(X, W_in, conv_w, conv_b, dt_bias, A_log, D, norm_w, W_out):
        import jax, jax.numpy as jnp
        import numpy as np
        BATCH, SEQ, D_MODEL = (4, 256, 128)
        D_STATE, D_CONV, EXPAND, HEADDIM = (64, 4, 2, 64)
        D_INNER = EXPAND * D_MODEL
        NHEADS = D_INNER // HEADDIM
        CONV_DIM = D_INNER + 2 * D_STATE
        D_IN_PROJ = 2 * D_INNER + 2 * D_STATE + NHEADS
        EPS = 1e-05

        def mamba2(X, W_in, conv_w, conv_b, dt_bias, A_log, D, norm_w, W_out):
            b, l, _ = X.shape
            zxbcdt = X @ W_in.T
            z, xBC, dt = jnp.split(zxbcdt, [D_INNER, D_INNER + CONV_DIM], axis=-1)
            dt = jax.nn.softplus(dt + dt_bias)
            xBC_t = xBC.transpose(0, 2, 1)
            ker = conv_w[:, None, :]
            xBC_c = jax.lax.conv_general_dilated(xBC_t, ker, window_strides=(1,), padding=[(D_CONV - 1, 0)], feature_group_count=CONV_DIM)
            xBC = jax.nn.silu(xBC_c.transpose(0, 2, 1) + conv_b)
            x, Bm, Cm = jnp.split(xBC, [D_INNER, D_INNER + D_STATE], axis=-1)
            xh = x.reshape(b, l, NHEADS, HEADDIM)
            A = -jnp.exp(A_log)
            dA = jnp.exp(dt * A)
            dBx = jnp.einsum('blh,bln,blhp->blhpn', dt, Bm, xh)

            def step(h, inp):
                dA_t, dBx_t, C_t = inp
                h = h * dA_t[:, :, None, None] + dBx_t
                y = jnp.einsum('bhpn,bn->bhp', h, C_t)
                return (h, y)
            h0 = jnp.zeros((b, NHEADS, HEADDIM, D_STATE), X.dtype)
            _, ys = jax.lax.scan(step, h0, (dA.transpose(1, 0, 2), dBx.transpose(1, 0, 2, 3, 4), Cm.transpose(1, 0, 2)))
            y = ys.transpose(1, 0, 2, 3) + D[None, None, :, None] * xh
            y = y.reshape(b, l, D_INNER)
            y = y * jax.nn.silu(z)
            y = y * jax.lax.rsqrt(jnp.mean(y * y, axis=-1, keepdims=True) + EPS) * norm_w
            return y @ W_out.T
        return mamba2(X, W_in, conv_w, conv_b, dt_bias, A_log, D, norm_w, W_out) + X

    def _L0_ffn_ref(x, w_qkv, w_o, g1, b1, wg, w1, bb1, w2, bb2, g2, b2):
        import jax, jax.numpy as jnp
        import numpy as np
        B, S, D, H, E, K, F = (1, 128, 128, 16, 8, 2, 512)

        def layernorm(x, g, b, eps=1e-05):
            m = x.mean(-1, keepdims=True)
            v = ((x - m) ** 2).mean(-1, keepdims=True)
            return (x - m) * jax.lax.rsqrt(v + eps) * g + b
        b, s, d = x.shape
        hd = d // H
        qkv = x @ w_qkv
        q, k, v = jnp.split(qkv, 3, axis=-1)
        to_heads = lambda t: t.reshape(b, s, H, hd).transpose(0, 2, 1, 3)
        q, k, v = (to_heads(q), to_heads(k), to_heads(v))
        scores = jnp.einsum('bhqd,bhkd->bhqk', q, k) / jnp.sqrt(jnp.float32(hd))
        causal = jnp.tril(jnp.ones((s, s), bool))
        scores = jnp.where(causal, scores, jnp.finfo(scores.dtype).min)
        attn = jax.nn.softmax(scores, axis=-1)
        o = jnp.einsum('bhqk,bhkd->bhqd', attn, v)
        o = o.transpose(0, 2, 1, 3).reshape(b, s, d) @ w_o
        h = layernorm(x + o, g1, b1)
        probs = jax.nn.softmax(h @ wg, axis=-1)
        topv, topi = jax.lax.top_k(probs, K)
        topv = topv / topv.sum(-1, keepdims=True)
        w = (topv[..., None] * jax.nn.one_hot(topi, E, dtype=h.dtype)).sum(-2)
        h1 = jax.nn.gelu(jnp.einsum('bsd,edf->ebsf', h, w1) + bb1[:, None, None, :])
        y = jnp.einsum('ebsf,efd->ebsd', h1, w2) + bb2[:, None, None, :]
        moe = jnp.einsum('ebsd,bse->bsd', y, w)
        return layernorm(h + moe, g2, b2)
    x = L0_attn_X
    x = _layernorm(x + _L0_attn_ref(x, L0_attn_W_in, L0_attn_conv_w, L0_attn_conv_b, L0_attn_dt_bias, L0_attn_A_log, L0_attn_D, L0_attn_norm_w, L0_attn_W_out), axis=-1)
    x = _layernorm(x + _L0_ffn_ref(x, L0_ffn_w_qkv, L0_ffn_w_o, L0_ffn_g1, L0_ffn_b1, L0_ffn_wg, L0_ffn_w1, L0_ffn_bb1, L0_ffn_w2, L0_ffn_bb2, L0_ffn_g2, L0_ffn_b2), axis=-1)
    return x

_drawn_inputs = setup_inputs


def setup_inputs(seed=0):
    import zlib

    import numpy as np

    out = dict(_drawn_inputs(seed))
    spreads = {'L0_attn_conv_b': (0.0, 0.1),
     'L0_attn_D': (1.0, 0.6),
     'L0_attn_norm_w': (1.0, 0.2),
     'L0_ffn_g1': (1.0, 0.2),
     'L0_ffn_b1': (0.0, 0.1),
     'L0_ffn_bb1': (0.0, 0.347),
     'L0_ffn_bb2': (0.0, 0.1),
     'L0_ffn_g2': (1.0, 0.2),
     'L0_ffn_b2': (0.0, 0.1)}
    factors = {'L0_attn_dt_bias': 8.0, 'L0_attn_A_log': 8.0}
    for name, (base, spread) in spreads.items():
        noise = np.random.default_rng([zlib.crc32(name.encode()), seed]).standard_normal(out[name].shape)
        drawn = base * np.exp(spread * noise) if base else spread * noise
        out[name] = jnp.asarray(drawn.astype(out[name].dtype))
    for name, factor in factors.items():
        out[name] = (out[name] * factor).astype(out[name].dtype)
    return out
```

```python
import concourse.bass as bass
from concourse import mybir
from contextlib import ExitStack

F32 = mybir.dt.float32
BF16 = mybir.dt.bfloat16
U32 = mybir.dt.uint32
ALU = mybir.AluOpType
ACT = mybir.ActivationFunctionType
AX = mybir.AxisListType

P = 128
BATCH, SEQ, D = 8, 512, 128
TILES = SEQ // P
EPS = 1e-5

DI, NS, MH, HD, TAPS = 256, 64, 4, 64, 4
CONV = DI + 2 * NS
PROJ = 2 * DI + 2 * NS + MH
CH = CONV // P


class Row:

    def __init__(self, it, p):
        self.it, self.p = it, p

    def __call__(self, per, k):
        return self.it * (2 * per) + (self.p * per + k)


def end_stage(nc, sems):
    nc.clear_and_free_semaphores(sems)
    nc.all_engine_barrier()


def wait_apart(eng, sem, value, passed):
    eng.wait_ge(sem, value)
    eng.sem_inc(passed, 1)


class Chain:

    def __init__(self, eng, sem, per):
        self.eng, self.sem, self.per = eng, sem, per

    def begin(self, row):
        self.row, self.n = row, 0

    def add(self, ins):
        self.n += 1
        ins.then_inc(self.sem, 1)

    def wait(self):
        self.eng.wait_ge(self.sem, self.row(self.per, self.n))

    def wait_apart(self, passed):
        wait_apart(self.eng, self.sem, self.row(self.per, self.n), passed)

    def end(self):
        assert self.n == self.per, (self.n, self.per)


def over_partitions(row_ap, n=P):
    return bass.AP(tensor=row_ap.tensor, offset=row_ap.offset, ap=[[0, n]] + [list(x) for x in row_ap.ap])


def mamba_layer(nc, X, W_in, conv_w, conv_b, dt_bias, A_log, Dskip, norm_w, W_out, x1_dram):
    sems = []
    with ExitStack() as ctx:
        def sb(name, shape, dt=F32):
            return ctx.enter_context(nc.sbuf_tensor(name, shape, dt))

        def sem(name):
            sems.append(nc.alloc_semaphore(name))
            return sems[-1]

        win = sb("win", [P, PROJ // P, D])
        win_dt = sb("win_dt", [MH, D])
        winT = sb("winT", [P, PROJ])
        wout = sb("wout", [P, DI])
        woutT = sb("woutT", [P, 2, D])
        cw = sb("cw", [P, CH, TAPS])
        cb = sb("cb", [P, CH])
        nw = sb("nw", [P, 2])
        dtb = sb("dtb", [P, MH])
        a_log = sb("a_log", [P, MH])
        a_neg = sb("a_neg", [P, MH])
        dskip = sb("dskip", [P, MH])
        ident = sb("ident", [P, P])
        ones = sb("ones", [P, P])
        upto = sb("upto", [P, P])
        after = sb("after", [P, P])
        minus_half = sb("minus_half", [P, TILES])
        xin = [sb(f"xin{p}", [P, TILES, D]) for p in range(2)]
        x2 = sb("x2", [P, TILES, D])
        xT = sb("xT", [P, SEQ])
        acc = sb("acc", [P, CH, SEQ])
        xc = sb("xc", [P, 2, SEQ])
        bc = sb("bc", [P, SEQ])
        cz = sb("cz", [P, SEQ])
        zs = sb("zs", [P, TILES, DI])
        btok = sb("btok", [P, TILES, NS])
        u = sb("u", [P, TILES, MH])
        absu = sb("absu", [P, TILES, MH])
        eu = sb("eu", [P, TILES, MH])
        one_e = sb("one_e", [P, TILES, MH])
        lnu = sb("lnu", [P, TILES, MH])
        den = sb("den", [P, TILES, MH])
        dt = sb("dt", [P, TILES, MH])
        a = sb("a", [P, TILES, MH])
        ecs = sb("ecs", [P, TILES, MH])
        etot = sb("etot", [NS, TILES, MH])
        xdt = sb("xdt", [P, TILES, DI])
        dx = sb("dx", [P, TILES, DI])
        ra = [sb(f"ra{k}", [P, MH, P]) for k in range(2)]
        decay = [sb(f"decay{k}", [P, MH, P]) for k in range(2)]
        gm = sb("gm", [P, TILES, P])
        mm = [sb(f"mm{k}", [P, MH, P]) for k in range(2)]
        xw = sb("xw", [P, TILES, DI])
        hs = sb("hs", [P, TILES, DI])
        t1 = sb("t1", [P, TILES, DI])
        y = sb("y", [P, TILES, DI])
        sq = sb("sq", [P, DI])
        ss = sb("ss", [P, TILES])
        rstd = sb("rstd", [P, TILES])
        yT = sb("yT", [P, 2, SEQ])
        r = sb("r", [P, TILES, D])
        bst = sb("bst", [P, TILES, 6])
        mv = sb("mv", [P, TILES, 2])
        rstd2 = sb("rstd2", [P, TILES])
        x1 = [sb(f"x1o{p}", [P, TILES, D]) for p in range(2)]

        ps = ctx.enter_context(nc.psum_tensor("psA", [P, 8, 512], F32))

        def bank(k, n=1):
            return ps[:, k:k + n, :].rearrange("p k n -> p (k n)")

        w_in_sem = sem("weights_loaded")
        consts = sem("constants_made")
        setup_ps = sem("setup_transposed")
        setup_sb = sem("setup_copied")
        x_in = [sem(f"x_loaded{p}") for p in range(2)]
        x_used = [sem(f"x_used{p}") for p in range(2)]
        x1_used = [sem(f"x1_stored{p}") for p in range(2)]
        xT_ps, xT_sb, conv_ps, dt_ps, z_ps = sem("xT_ps"), sem("xT_sb"), sem("conv_ps"), sem("dt_ps"), sem("z_ps")
        tap0, conv_done, silu = sem("tap0"), sem("conv_done"), sem("silu")
        c_moved, u_ready, ln_ready, a_ready = sem("c_moved"), sem("u_ready"), sem("ln_ready"), sem("a_ready")
        xtr_ps, bctr_ps, btok_ready = sem("xtr_ps"), sem("bctr_ps"), sem("btok_ready")
        xdt_ready, dx_ready = sem("xdt_ready"), sem("dx_ready")
        cs_ps, ecs_ready = sem("cs_ps"), sem("ecs_ready")
        ra_ready, seg_ps, decay_ready, m_ready, xw_ready = sem("ra_ready"), sem("seg_ps"), sem("decay_ready"), sem("m_ready"), sem("xw_ready")
        g_ps, gm_ready, hn_ps, h_ready = sem("g_ps"), sem("gm_ready"), sem("hn_ps"), sem("h_ready")
        intra_ps, inter_ps = sem("intra_ps"), sem("inter_ps")
        y_ready, ss_ready, rstd_ready = sem("y_ready"), sem("ss_ready"), sem("rstd_ready")
        yT_ps, yT_sb, o_ps = sem("yT_ps"), sem("yT_sb"), sem("o_ps")
        x2_ready, r_ready, var_ready, rstd2_ready, x1_ready = sem("x2_ready"), sem("r_ready"), sem("var_ready"), sem("rstd2_ready"), sem("x1_ready")
        dve_own, act_own, pool_own = sem("dve_own"), sem("act_own"), sem("pool_own")

        sp_passed, pool_passed, dve_passed = sem("sp_passed_a"), sem("pool_passed_a"), sem("dve_passed_a")
        block = ctx.enter_context(nc.Block())
        x_rows = X.rearrange("b (t p) d -> b p t d", p=P)
        x1_rows = x1_dram.rearrange("b (t p) d -> b p t d", p=P)
        def xw_step(pool, row, c):
            if c == 0:
                pool.wait_ge(xdt_ready, row(1, 1))
            pool.wait_ge(decay_ready, row(4, c + 1))
            nc.gpsimd.tensor_tensor(xw[:, c, :].rearrange("p (h d) -> p h d", h=MH),
                                    xdt[:, c, :].rearrange("p (h d) -> p h d", h=MH),
                                    decay[c % 2][:, :, P - 1:P].broadcast_to([P, MH, HD]),
                                    ALU.mult).then_inc(xw_ready, 1)

        def seg(pe, row, c):
            pe.wait_ge(ra_ready, row(4, c + 1))
            if c >= 2:
                pe.wait_ge(decay_ready, row(4, c - 1))
            else:
                pe.wait_ge(yT_sb, row(1, 0))
            nc.tensor.matmul(bank(6 + c % 2), after[:, :], ra[c % 2][:, :, :].rearrange("p h n -> p (h n)"),
                             start=True, stop=True).then_inc(seg_ps, 1)

        def intra(pe, row, c):
            pe.wait_ge(m_ready, row(4, c + 1))
            if c == 0:
                pe.wait_ge(dx_ready, row(1, 1))
            for h in range(MH):
                ins = nc.tensor.matmul(bank(0, 2)[:, c * DI + h * HD:c * DI + (h + 1) * HD], mm[c % 2][:, h, :],
                                       xdt[:, c, h * HD:(h + 1) * HD], start=True, stop=True)
            ins.then_inc(intra_ps, 1)

        @block.sync
        def _(sp):
            sp.dma_start(win[:, :, :], W_in[0:PROJ - MH, :].rearrange("(c p) d -> p c d", p=P)).then_inc(w_in_sem, 16)
            sp.dma_start(win_dt[:, :], W_in[PROJ - MH:PROJ, :]).then_inc(w_in_sem, 16)
            sp.dma_start(wout[:, :], W_out).then_inc(w_in_sem, 16)
            sp.dma_start(nw[:, :], norm_w.rearrange("(k p) -> p k", p=P), allow_slow_non_contiguous=True).then_inc(w_in_sem, 16)
            sp.dma_start(cw[:, :, :], conv_w.rearrange("(c p) k -> p c k", p=P)).then_inc(w_in_sem, 16)
            sp.dma_start(cb[:, :], conv_b.rearrange("(c p) -> p c", p=P), allow_slow_non_contiguous=True).then_inc(w_in_sem, 16)
            sp.dma_start(dtb[:, :], over_partitions(dt_bias)).then_inc(w_in_sem, 16)
            sp.dma_start(a_log[:, :], over_partitions(A_log)).then_inc(w_in_sem, 16)
            sp.dma_start(dskip[:, :], over_partitions(Dskip)).then_inc(w_in_sem, 16)
            with sp.Fori(0, BATCH // 2) as it:
                for p in range(2):
                    row = Row(it, p)
                    sp.wait_ge(x_used[p], it * 2)
                    sp.dma_start(xin[p][:, :, :], x_rows[it * 2 + p]).then_inc(x_in[p], 16)
                for p in range(2):
                    row = Row(it, p)
                    wait_apart(sp, silu, row(3, 2), sp_passed)
                    sp.wait_ge(inter_ps, row(3, 0))
                    sp.wait_ge(g_ps, row(1, 0))
                    sp.dma_start(cz[0:NS, :], bc[NS:P, :]).then_inc(c_moved, 16)
                    sp.wait_ge(x1_ready, row(1, 1))
                    sp.dma_start(x1_rows[it * 2 + p], x1[p][:, :, :]).then_inc(x1_used[p], 16)
            for p in range(2):
                sp.wait_ge(x1_used[p], 16 * (BATCH // 2))

        @block.gpsimd
        def _(pool):
            nc.gpsimd.memset(ones[:, :], 1.0).then_inc(consts, 1)
            nc.gpsimd.memset(minus_half[:, :], -0.5).then_inc(consts, 1)
            nc.gpsimd.memset(cz[:, :], 0.0).then_inc(consts, 1)
            nc.gpsimd.memset(hs[:, :, :], 0.0).then_inc(consts, 1)
            pool.wait_ge(consts, 4)
            nc.gpsimd.affine_select(out=upto[:, :], in_=ones[:, :], compare_op=ALU.is_ge, fill=0.0, base=0,
                                    pattern=[[1, P]], channel_multiplier=-1).then_inc(consts, 1)
            nc.gpsimd.affine_select(out=after[:, :], in_=ones[:, :], compare_op=ALU.is_gt, fill=0.0, base=0,
                                    pattern=[[-1, P]], channel_multiplier=1).then_inc(consts, 1)
            nc.gpsimd.affine_select(out=ident[:, :], in_=ones[:, :], compare_op=ALU.is_equal, fill=0.0, base=0,
                                    pattern=[[-1, P]], channel_multiplier=1).then_inc(consts, 1)
            own = Chain(pool, pool_own, 2)
            with pool.Fori(0, BATCH // 2) as it:
                for p in range(2):
                    row = Row(it, p)
                    own.begin(row)
                    pool.wait_ge(x_in[p], it * 16 + 16)
                    pool.wait_ge(r_ready, row(1, 0))
                    nc.gpsimd.tensor_tensor(x2[:, :, :], xin[p][:, :, :], xin[p][:, :, :], ALU.add).then_inc(x2_ready, 1)
                    pool.wait_ge(x2_ready, row(1, 1))
                    pool.sem_inc(x_used[p], 1)
                    for c in range(TILES):
                        if c == 0:
                            pool.wait_ge(a_ready, row(1, 1))
                        pool.wait_ge(seg_ps, row(4, max(c - 1, 0)))
                        nc.gpsimd.tensor_tensor(ra[c % 2][:, :, :], upto[:, :].unsqueeze(1).broadcast_to([P, MH, P]),
                                                a[:, c, :].unsqueeze(2).broadcast_to([P, MH, P]),
                                                ALU.mult).then_inc(ra_ready, 1)
                        if c >= 1:
                            xw_step(pool, row, c - 1)
                    wait_apart(pool, ss_ready, row(4, 4), pool_passed)
                    own.add(nc.gpsimd.tensor_scalar(rstd[:, :], ss[:, :], 1.0 / DI, EPS, ALU.mult, ALU.add))
                    own.wait()
                    nc.gpsimd.tensor_tensor(rstd[:, :], rstd[:, :], minus_half[:, :], ALU.pow).then_inc(rstd_ready, 1)
                    wait_apart(pool, var_ready, row(1, 1), pool_passed)
                    own.add(nc.gpsimd.tensor_scalar(rstd2[:, :], mv[:, :, 1], EPS, None, ALU.add))
                    own.wait()
                    nc.gpsimd.tensor_tensor(rstd2[:, :], rstd2[:, :], minus_half[:, :], ALU.pow).then_inc(rstd2_ready, 1)
                    own.end()

        @block.scalar
        def _(act):
            act.wait_ge(w_in_sem, 16 * 9)
            nc.scalar.activation(a_neg[:, :], a_log[:, :], ACT.Exp).then_inc(setup_sb, 1)
            with act.Fori(0, BATCH // 2) as it:
                for p in range(2):
                    row = Row(it, p)
                    act.wait_ge(xT_ps, row(1, 1))
                    act.wait_ge(z_ps, row(1, 0))
                    nc.scalar.activation(xT[:, :], bank(3), ACT.Copy).then_inc(xT_sb, 1)
                    for c in range(CH):
                        act.wait_ge(conv_ps, row(3, c + 1))
                        act.wait_ge(silu, row(3, 0))
                        nc.scalar.activation(acc[:, c, :], bank(c), ACT.Identity, bias=cb[:, c:c + 1],
                                             scale=cw[:, c, TAPS - 1:TAPS]).then_inc(tap0, 1)
                    act.wait_ge(u_ready, row(3, 2))
                    nc.scalar.activation(eu[:, :, :], absu[:, :, :], ACT.Exp, scale=-1.0).then_inc(ln_ready, 1)
                    act.wait_ge(u_ready, row(3, 3))
                    nc.scalar.activation(lnu[:, :, :], one_e[:, :, :], ACT.Ln).then_inc(ln_ready, 1)
                    act.wait_ge(conv_done, row(3, 2))
                    act.wait_ge(xtr_ps, row(1, 0))
                    nc.scalar.activation(xc[:, :, :], acc[:, 0:2, :], ACT.Silu).then_inc(silu, 1)
                    act.wait_ge(conv_done, row(3, 3))
                    act.wait_ge(c_moved, row(16, 0))
                    act.wait_ge(bctr_ps, row(1, 0))
                    act.wait_ge(g_ps, row(1, 0))
                    nc.scalar.activation(bc[:, :], acc[:, 2, :], ACT.Silu).then_inc(silu, 1)
                    act.wait_ge(z_ps, row(1, 1))
                    act.wait_ge(y_ready, row(1, 0))
                    nc.scalar.activation(zs[:, :, :].rearrange("p t n -> p (t n)"), bank(4, 2), ACT.Silu).then_inc(silu, 1)
                    act.wait_ge(bctr_ps, row(1, 1))
                    act.wait_ge(hn_ps, row(3, 0))
                    nc.scalar.activation(btok[:, :, :], bank(2).rearrange("p (t n) -> p t n", t=TILES)[:, :, 0:NS],
                                         ACT.Copy).then_inc(btok_ready, 1)
                    act.wait_ge(cs_ps, row(1, 1))
                    nc.scalar.activation(ecs[:, :, :].rearrange("p t h -> p (t h)"), bank(3)[:, 16:32], ACT.Exp).then_inc(act_own, 1)
                    nc.scalar.activation(etot[:, :, :].rearrange("p t h -> p (t h)"), bank(3)[0:NS, 32:48], ACT.Exp).then_inc(ecs_ready, 1)
                    for c in range(TILES):
                        act.wait_ge(seg_ps, row(4, c + 1))
                        act.wait_ge(m_ready, row(4, max(c - 1, 0)))
                        act.wait_ge(xw_ready, row(3, max(c - 1, 0)))
                        nc.scalar.activation(decay[c % 2][:, :, :].rearrange("p h n -> p (h n)"), bank(6 + c % 2),
                                             ACT.Exp).then_inc(decay_ready, 1)
                    act.wait_ge(y_ready, row(1, 1))
                    for t in range(TILES):
                        if t >= 1:
                            act.wait_ge(ss_ready, row(4, t))
                        nc.scalar.activation(sq[:, :], y[:, t, :], ACT.Square, accum_out=ss[:, t:t + 1]).then_inc(ss_ready, 1)
                    act.wait_ge(yT_ps, row(1, 1))
                    nc.scalar.activation(yT[:, :, :].rearrange("p k n -> p (k n)"), bank(6, 2), ACT.Copy).then_inc(yT_sb, 1)

        @block.vector
        def _(dve):
            dve.wait_ge(setup_ps, 1)
            nc.vector.tensor_copy(winT[:, :], bank(0, 2)[:, 0:PROJ]).then_inc(setup_sb, 1)
            dve.wait_ge(w_in_sem, 16 * 9)
            for k in range(2):
                nc.vector.tensor_scalar(woutT[:, k, :], bank(2)[:, k * P:(k + 1) * P], nw[:, k:k + 1], None,
                                        ALU.mult).then_inc(setup_sb, 1)
            dve.wait_ge(setup_sb, 4)
            nc.vector.tensor_scalar(a_neg[:, :], a_neg[:, :], -1.0, None, ALU.mult).then_inc(setup_sb, 1)
            dve.wait_ge(setup_sb, 5)
            own = Chain(dve, dve_own, 22)
            with dve.Fori(0, BATCH // 2) as it:
                for p in range(2):
                    row = Row(it, p)
                    own.begin(row)
                    dve.wait_ge(dt_ps, row(1, 1))
                    nc.vector.tensor_tensor(u[:, :, :], bank(3)[:, 0:16].rearrange("p (t h) -> p t h", t=TILES),
                                            dtb[:, :].unsqueeze(1).broadcast_to([P, TILES, MH]), ALU.add).then_inc(u_ready, 1)
                    dve.wait_ge(u_ready, row(3, 1))
                    nc.vector.scalar_tensor_tensor(out=absu[:, :, :], in0=u[:, :, :], scalar=-1.0, in1=u[:, :, :],
                                                   op0=ALU.mult, op1=ALU.max).then_inc(u_ready, 1)
                    for c in range(CH):
                        dve.wait_ge(tap0, row(3, c + 1))
                        for k in range(TAPS - 1):
                            s = TAPS - 1 - k
                            if k:
                                own.wait()
                            ins = nc.vector.scalar_tensor_tensor(out=acc[:, c, s:SEQ], in0=bank(c)[:, 0:SEQ - s],
                                                                 scalar=cw[:, c, k:k + 1], in1=acc[:, c, s:SEQ],
                                                                 op0=ALU.mult, op1=ALU.add)
                            if k < TAPS - 2:
                                own.add(ins)
                            else:
                                ins.then_inc(conv_done, 1)
                        if c == 0:
                            dve.wait_ge(ln_ready, row(2, 1))
                            nc.vector.tensor_scalar(one_e[:, :, :], eu[:, :, :], 1.0, None, ALU.add).then_inc(u_ready, 1)
                    dve.wait_ge(u_ready, row(3, 3))
                    own.add(nc.vector.tensor_scalar(den[:, :, :], one_e[:, :, :], -1.0, 1e-30, ALU.add, ALU.max))
                    own.wait()
                    own.add(nc.vector.reciprocal(den[:, :, :], den[:, :, :]))
                    own.wait()
                    dve.wait_ge(ln_ready, row(2, 2))
                    own.add(nc.vector.tensor_tensor(lnu[:, :, :], lnu[:, :, :], den[:, :, :], ALU.mult))
                    own.wait()
                    own.add(nc.vector.tensor_scalar(den[:, :, :], one_e[:, :, :], 1.0, None, ALU.is_equal))
                    own.wait()
                    own.add(nc.vector.tensor_tensor(lnu[:, :, :], lnu[:, :, :], den[:, :, :], ALU.add))
                    own.wait()
                    own.add(nc.vector.tensor_tensor(lnu[:, :, :], lnu[:, :, :], eu[:, :, :], ALU.mult))
                    own.wait()
                    dve.wait_ge(ra_ready, row(4, 0))
                    own.add(nc.vector.scalar_tensor_tensor(out=dt[:, :, :], in0=u[:, :, :], scalar=0.0, in1=lnu[:, :, :],
                                                           op0=ALU.max, op1=ALU.add))
                    own.wait()
                    nc.vector.scalar_tensor_tensor(out=a[:, :, :], in0=dt[:, :, :], scalar=1.0,
                                                   in1=a_neg[:, :].unsqueeze(1).broadcast_to([P, TILES, MH]),
                                                   op0=ALU.mult, op1=ALU.mult).then_inc(a_ready, 1)
                    dve.wait_ge(xtr_ps, row(1, 1))
                    xtok = bank(0, 2).rearrange("p (t h d) -> p t h d", t=TILES, h=MH)
                    dve.wait_ge(intra_ps, row(4, 0))
                    dve.wait_ge(xw_ready, row(3, 0))
                    nc.vector.tensor_tensor(xdt[:, :, :].rearrange("p t (h d) -> p (t h) d", h=MH),
                                            bank(0, 2).rearrange("p (g d) -> p g d", d=HD),
                                            dt[:, :, :].rearrange("p t h -> p (t h)").unsqueeze(2).broadcast_to([P, TILES * MH, HD]),
                                            ALU.mult).then_inc(xdt_ready, 1)
                    nc.vector.tensor_tensor(dx[:, :, :].rearrange("p t (h d) -> p t h d", h=MH), xtok,
                                            dskip[:, :].unsqueeze(1).unsqueeze(3).broadcast_to([P, TILES, MH, HD]),
                                            ALU.mult).then_inc(dx_ready, 1)
                    dve.wait_ge(g_ps, row(1, 1))
                    nc.vector.tensor_tensor(gm[:, :, :], bank(3).rearrange("p (t n) -> p t n", t=TILES),
                                            upto[:, :].unsqueeze(1).broadcast_to([P, TILES, P]), ALU.mult).then_inc(gm_ready, 1)
                    dve.wait_ge(gm_ready, row(1, 1))
                    for c in range(TILES):
                        dve.wait_ge(decay_ready, row(4, c + 1))
                        dve.wait_ge(intra_ps, row(4, max(c - 1, 0)))
                        nc.vector.tensor_tensor(mm[c % 2][:, :, :], decay[c % 2][:, :, :],
                                                gm[:, c, :].unsqueeze(1).broadcast_to([P, MH, P]), ALU.mult).then_inc(m_ready, 1)
                    dve.wait_ge(hn_ps, row(3, 3))
                    dve.wait_ge(ecs_ready, row(1, 1))
                    dve.wait_ge(act_own, row(1, 1))
                    dve.wait_ge(inter_ps, row(3, 0))
                    nc.vector.tensor_copy(hs[0:NS, 1, :], bank(2)[0:NS, 0:DI]).then_inc(h_ready, 1)
                    for c in range(1, TILES - 1):
                        dve.wait_ge(h_ready, row(3, c))
                        own.add(nc.vector.tensor_tensor(hs[0:NS, c + 1, :].rearrange("p (h d) -> p h d", h=MH),
                                                        hs[0:NS, c, :].rearrange("p (h d) -> p h d", h=MH),
                                                        etot[:, c, :].unsqueeze(2).broadcast_to([NS, MH, HD]), ALU.mult))
                        own.wait()
                        src = bank(2)[0:NS, DI:2 * DI] if c == 1 else bank(3)[0:NS, 0:DI]
                        nc.vector.tensor_tensor(hs[0:NS, c + 1, :], hs[0:NS, c + 1, :], src, ALU.add).then_inc(h_ready, 1)
                    dve.wait_ge(intra_ps, row(4, 4))
                    own.add(nc.vector.tensor_tensor(y[:, :, :].rearrange("p t n -> p (t n)"), bank(0, 2),
                                                    dx[:, :, :].rearrange("p t n -> p (t n)"), ALU.add))
                    dve.wait_ge(inter_ps, row(3, 3))
                    own.add(nc.vector.tensor_tensor(t1[:, 1:TILES, :].rearrange("p t (h d) -> p (t h) d", h=MH),
                                                    bank(4, 2)[:, DI:TILES * DI].rearrange("p (g d) -> p g d", d=HD),
                                                    ecs[:, 1:TILES, :].rearrange("p t h -> p (t h)").unsqueeze(2).broadcast_to([P, 3 * MH, HD]),
                                                    ALU.mult))
                    own.wait()
                    own.add(nc.vector.tensor_tensor(y[:, 1:TILES, :], y[:, 1:TILES, :], t1[:, 1:TILES, :], ALU.add))
                    own.wait()
                    dve.wait_ge(silu, row(3, 3))
                    nc.vector.tensor_tensor(y[:, :, :], y[:, :, :], zs[:, :, :], ALU.mult).then_inc(y_ready, 1)
                    dve.wait_ge(o_ps, row(1, 1))
                    dve.wait_ge(rstd_ready, row(1, 1))
                    dve.wait_ge(x2_ready, row(1, 1))
                    for t in range(TILES):
                        ins = nc.vector.scalar_tensor_tensor(out=r[:, t, :], in0=bank(2)[:, t * P:(t + 1) * P],
                                                             scalar=rstd[:, t:t + 1], in1=x2[:, t, :],
                                                             op0=ALU.mult, op1=ALU.add)
                        if t == TILES - 1:
                            ins.then_inc(r_ready, 1)
                        else:
                            own.add(ins)
                    own.wait()
                    dve.wait_ge(r_ready, row(1, 1))
                    for t in range(TILES):
                        ins = nc.vector.bn_stats(bst[:, t, :], r[:, t, :])
                    own.add(ins)
                    own.wait_apart(dve_passed)
                    for t in range(TILES):
                        ins = nc.vector.bn_aggr(mv[:, t, :], bst[:, t, :])
                    ins.then_inc(var_ready, 1)
                    dve.wait_ge(var_ready, row(1, 1))
                    dve.wait_ge(rstd2_ready, row(1, 1))
                    dve.wait_ge(x1_used[p], it * 16)
                    for t in range(TILES):
                        ins = nc.vector.tensor_scalar(x1[p][:, t, :], r[:, t, :], mv[:, t, 0:1], rstd2[:, t:t + 1],
                                                      ALU.subtract, ALU.mult)
                    ins.then_inc(x1_ready, 1)
                    own.end()

        @block.tensor
        def _(pe):
            pe.wait_ge(w_in_sem, 16 * 9)
            pe.wait_ge(consts, 7)
            for c in range(PROJ // P):
                nc.tensor.transpose(bank(0, 2)[:, c * P:(c + 1) * P], win[:, c, :], ident[:, :])
            nc.tensor.transpose(bank(1)[:, P:P + MH], win_dt[:, :], ident[0:MH, 0:MH])
            for k in range(2):
                ins = nc.tensor.transpose(bank(2)[:, k * P:(k + 1) * P], wout[:, k * P:(k + 1) * P], ident[:, :])
            ins.then_inc(setup_ps, 1)
            pe.wait_ge(setup_sb, 5)
            with pe.Fori(0, BATCH // 2) as it:
                for p in range(2):
                    row = Row(it, p)
                    pe.wait_ge(x_in[p], it * 16 + 16)
                    pe.wait_ge(h_ready, row(3, 0))
                    for t in range(TILES):
                        ins = nc.tensor.transpose(bank(3)[:, t * P:(t + 1) * P], xin[p][:, t, :], ident[:, :])
                    ins.then_inc(xT_ps, 1)
                    pe.wait_ge(xT_ps, row(1, 1))
                    pe.sem_inc(x_used[p], 1)
                    pe.wait_ge(xT_sb, row(1, 1))
                    for t in range(TILES):
                        ins = nc.tensor.matmul(bank(3)[:, t * MH:(t + 1) * MH], xT[:, t * P:(t + 1) * P],
                                               winT[:, PROJ - MH:PROJ], start=True, stop=True)
                    ins.then_inc(dt_ps, 1)
                    pe.wait_ge(y_ready, row(1, 0))
                    for c in range(CH):
                        if c == 2:
                            pe.wait_ge(x1_ready, row(1, 0))
                        nc.tensor.matmul(bank(c), winT[:, DI + c * P:DI + (c + 1) * P], xT[:, :],
                                         start=True, stop=True).then_inc(conv_ps, 1)
                    for t in range(TILES):
                        ins = nc.tensor.matmul(bank(4, 2)[:, t * DI:(t + 1) * DI], xT[:, t * P:(t + 1) * P],
                                               winT[:, 0:DI], start=True, stop=True)
                    ins.then_inc(z_ps, 1)
                    pe.wait_ge(a_ready, row(1, 1))
                    nc.tensor.matmul(bank(3)[:, 16:32], upto[:, :], a[:, :, :].rearrange("p t h -> p (t h)"),
                                     start=True, stop=True)
                    nc.tensor.matmul(bank(3)[0:NS, 32:48], ones[:, 0:NS], a[:, :, :].rearrange("p t h -> p (t h)"),
                                     start=True, stop=True).then_inc(cs_ps, 1)
                    for c in range(2):
                        seg(pe, row, c)
                    pe.wait_ge(silu, row(3, 1))
                    pe.wait_ge(conv_done, row(3, 3))
                    for t in range(TILES):
                        for k in range(2):
                            ins = nc.tensor.transpose(bank(0, 2)[:, t * DI + k * P:t * DI + (k + 1) * P],
                                                      xc[:, k, t * P:(t + 1) * P], ident[:, :])
                    ins.then_inc(xtr_ps, 1)
                    pe.wait_ge(silu, row(3, 2))
                    for t in range(TILES):
                        ins = nc.tensor.transpose(bank(2)[:, t * P:(t + 1) * P], bc[:, t * P:(t + 1) * P], ident[:, :])
                    ins.then_inc(bctr_ps, 1)
                    pe.wait_ge(c_moved, row(16, 16))
                    pe.wait_ge(ecs_ready, row(1, 1))
                    for t in range(TILES):
                        ins = nc.tensor.matmul(bank(3)[:, t * P:(t + 1) * P], bc[:, t * P:(t + 1) * P],
                                               cz[:, t * P:(t + 1) * P], start=True, stop=True)
                    ins.then_inc(g_ps, 1)
                    pe.wait_ge(btok_ready, row(1, 1))
                    for c in range(2):
                        pe.wait_ge(xw_ready, row(3, c + 1))
                        nc.tensor.matmul(bank(2)[0:NS, c * DI:(c + 1) * DI], btok[:, c, :], xw[:, c, :],
                                         start=True, stop=True).then_inc(hn_ps, 1)
                        seg(pe, row, c + 2)
                        intra(pe, row, c)
                    pe.wait_ge(gm_ready, row(1, 1))
                    pe.wait_ge(xw_ready, row(3, 3))
                    nc.tensor.matmul(bank(3)[0:NS, 0:DI], btok[:, 2, :], xw[:, 2, :],
                                     start=True, stop=True).then_inc(hn_ps, 1)
                    for c in range(2, TILES):
                        intra(pe, row, c)
                    pe.wait_ge(silu, row(3, 3))
                    for c in range(1, TILES):
                        pe.wait_ge(h_ready, row(3, c))
                        nc.tensor.matmul(bank(4, 2)[:, c * DI:(c + 1) * DI], cz[:, c * P:(c + 1) * P], hs[:, c, :],
                                         start=True, stop=True).then_inc(inter_ps, 1)
                    pe.wait_ge(y_ready, row(1, 1))
                    pe.wait_ge(decay_ready, row(4, 4))
                    for t in range(TILES):
                        for k in range(2):
                            ins = nc.tensor.transpose(bank(6 + k)[:, t * P:(t + 1) * P], y[:, t, k * P:(k + 1) * P], ident[:, :])
                    ins.then_inc(yT_ps, 1)
                    pe.wait_ge(yT_sb, row(1, 1))
                    for t in range(TILES):
                        for k in range(2):
                            ins = nc.tensor.matmul(bank(2)[:, t * P:(t + 1) * P], yT[:, k, t * P:(t + 1) * P],
                                                   woutT[:, k, :], start=(k == 0), stop=(k == 1))
                    ins.then_inc(o_ps, 1)
    end_stage(nc, sems)


AH, DH = 16, 8
PARTS = 3
QK_ROWS = PARTS * PARTS * DH
MAX_ROWS = QK_ROWS + PARTS
GROUPS = AH // 4
VW = 32


def qkv_projection(nc, x1_dram, w_qkv, q_parts, k_parts, v_dram):
    sems = []
    with ExitStack() as ctx:
        def sb(name, shape, dt=F32):
            return ctx.enter_context(nc.sbuf_tensor(name, shape, dt))

        def pair(name, shape, dt=F32):
            return [sb(f"{name}{p}", shape, dt) for p in range(2)]

        def sem(name):
            sems.append(nc.alloc_semaphore(name))
            return sems[-1]

        wqkv = sb("wqkv", [P, 3 * D])
        wqk = sb("wqk", [P, 2, DH, AH])
        ones = sb("ones_b", [P, P])
        ident = sb("ident_b", [P, P])
        x1 = pair("x1_b", [P, TILES, D])
        xT = pair("xT_b", [P, SEQ])
        part = {n: pair(f"{n}part", [P, PARTS, SEQ], BF16) for n in "qk"}
        rest = {n: pair(f"{n}rest", [P, SEQ]) for n in "qk"}
        v = pair("v_b", [P, TILES, D])
        ps = ctx.enter_context(nc.psum_tensor("psB0", [P, 8, 512], F32))
        w_loaded, consts, w_ordered = sem("wqkv_loaded"), sem("qkv_constants"), sem("wqk_ordered")
        x_loaded = [sem(f"x1_loaded{p}") for p in range(2)]
        stored = [sem(f"qkv_stored{p}") for p in range(2)]
        xT_ps, xT_sb = sem("x1T_ps"), sem("x1T_sb")
        proj_ps = sem("proj_ps")
        first_part, rest_ready, third_part, second_part = sem("first_part"), sem("rest_ready"), sem("third_part"), sem("second_part")
        v_sb = sem("v_sb")
        pool_passed = sem("pool_passed_b")
        block = ctx.enter_context(nc.Block())
        x1_rows = x1_dram.rearrange("b (t p) d -> b p t d", p=P)
        v_rows = v_dram.rearrange("b (t p) d -> b p t d", p=P)
        SCALE = {"q": DH ** -0.5, "k": 1.0}

        @block.sync
        def _(sp):
            sp.dma_start(wqkv[:, :], w_qkv).then_inc(w_loaded, 16)
            with sp.Fori(0, BATCH // 2) as it:
                for p in range(2):
                    sp.wait_ge(xT_ps, it * 2)
                    sp.dma_start(x1[p][:, :, :], x1_rows[it * 2 + p]).then_inc(x_loaded[p], 16)
                for p in range(2):
                    row = Row(it, p)
                    for n, (name, dst) in enumerate((("q", q_parts), ("k", k_parts))):
                        sp.wait_ge(third_part, row(2, n + 1))
                        sp.dma_start(dst[it * 2 + p].rearrange("s c n -> c s n"), part[name][p][:, :, :]).then_inc(stored[p], 16)
                    sp.wait_ge(v_sb, row(1, 1))
                    sp.dma_start(v_rows[it * 2 + p], v[p][:, :, :]).then_inc(stored[p], 16)
            for p in range(2):
                sp.wait_ge(stored[p], 48 * (BATCH // 2))

        @block.gpsimd
        def _(pool):
            nc.gpsimd.memset(ones[:, :], 1.0).then_inc(consts, 1)
            pool.wait_ge(consts, 1)
            nc.gpsimd.affine_select(out=ident[:, :], in_=ones[:, :], compare_op=ALU.is_equal, fill=0.0, base=0,
                                    pattern=[[-1, P]], channel_multiplier=1).then_inc(consts, 1)
            with pool.Fori(0, BATCH // 2) as it:
                for p in range(2):
                    row = Row(it, p)
                    for n, name in enumerate("qk"):
                        wait_apart(pool, rest_ready, row(2, n + 1), pool_passed)
                        nc.gpsimd.tensor_copy(part[name][p][:, 1, :], rest[name][p][:, :]).then_inc(second_part, 1)
                        pool.wait_ge(second_part, row(2, n + 1))
                        nc.gpsimd.tensor_tensor(part[name][p][:, 2, :], rest[name][p][:, :], part[name][p][:, 1, :],
                                                ALU.subtract).then_inc(third_part, 1)

        @block.scalar
        def _(act):
            with act.Fori(0, BATCH // 2) as it:
                for p in range(2):
                    row = Row(it, p)
                    act.wait_ge(xT_ps, row(1, 1))
                    act.wait_ge(proj_ps, it * 6)
                    nc.scalar.activation(xT[p][:, :], ps[:, 4 * p, :], ACT.Copy).then_inc(xT_sb, 1)
                    act.wait_ge(stored[p], it * 48)
                    for n, name in enumerate("qk"):
                        act.wait_ge(proj_ps, row(3, n + 1))
                        nc.scalar.activation(part[name][p][:, 0, :], ps[:, 4 * p + 1 + n, :], ACT.Copy,
                                             scale=SCALE[name]).then_inc(first_part, 1)
                    act.wait_ge(proj_ps, row(3, 3))
                    nc.scalar.activation(v[p][:, :, :].rearrange("p t n -> p (t n)"), ps[:, 4 * p + 3, :], ACT.Copy).then_inc(v_sb, 1)

        @block.vector
        def _(dve):
            dve.wait_ge(w_loaded, 16)
            for n in range(2):
                nc.vector.tensor_copy(wqk[:, n, :, :], wqkv[:, n * D:(n + 1) * D].rearrange("p (h d) -> p d h", d=DH)).then_inc(w_ordered, 1)
            with dve.Fori(0, BATCH // 2) as it:
                for p in range(2):
                    row = Row(it, p)
                    dve.wait_ge(third_part, it * 4)
                    for n, name in enumerate("qk"):
                        dve.wait_ge(first_part, row(2, n + 1))
                        nc.vector.scalar_tensor_tensor(out=rest[name][p][:, :], in0=ps[:, 4 * p + 1 + n, :], scalar=SCALE[name],
                                                       in1=part[name][p][:, 0, :], op0=ALU.mult, op1=ALU.subtract).then_inc(rest_ready, 1)

        @block.tensor
        def _(pe):
            pe.wait_ge(w_loaded, 16)
            pe.wait_ge(consts, 2)
            pe.wait_ge(w_ordered, 2)
            with pe.Fori(0, BATCH // 2) as it:
                for p in range(2):
                    row = Row(it, p)
                    pe.wait_ge(x_loaded[p], it * 16 + 16)
                    pe.wait_ge(xT_sb, it * 2)
                    for t in range(TILES):
                        ins = nc.tensor.transpose(ps[:, 4 * p, t * P:(t + 1) * P], x1[p][:, t, :], ident[:, :])
                    ins.then_inc(xT_ps, 1)
                    pe.wait_ge(xT_sb, row(1, 1))
                    pe.wait_ge(rest_ready, it * 4)
                    pe.wait_ge(v_sb, it * 2)
                    for n in range(2):
                        nc.tensor.matmul(ps[:, 4 * p + 1 + n, :], wqk[:, n, :, :].rearrange("p d h -> p (d h)"), xT[p][:, :],
                                         start=True, stop=True).then_inc(proj_ps, 1)
                    for t in range(TILES):
                        ins = nc.tensor.matmul(ps[:, 4 * p + 3, t * P:(t + 1) * P], xT[p][:, t * P:(t + 1) * P],
                                               wqkv[:, 2 * D:3 * D], start=True, stop=True)
                    ins.then_inc(proj_ps, 1)
    end_stage(nc, sems)


MAX_UNITS = [(qt, 4 * g + h, n) for g in range(GROUPS) for qt, n in ((0, 4), (1, 2), (2, 1), (3, 1)) for h in range(0, 4, n)]
EXP_UNITS = [(g, kt, h, n) for g in range(GROUPS) for kt, n in ((0, 2), (1, 2), (2, 4), (3, 4)) for h in range(0, 4, n)]
NMAX, NEXP, STEPS = len(MAX_UNITS), len(EXP_UNITS), GROUPS * TILES


LAG = 2
PBUF = 4
MAX_SHARE = [4] * 5 + [3] * 8 + [0] * 3


def schedule():
    extra = {2: [("last heads", GROUPS - 1), ("spread v", 0)], 3: [("last out", 0)], 4: [("last norm", 0)],
             5: [("last normalise", 0)], 6: [("heads", 0), ("last gain", 0)], 10: [("heads", 1)],
             12: [("max rows", 0)], 14: [("heads", 2)]}
    out, done = [], 0
    for step in range(STEPS):
        units = [u for u, (g, k, _, _) in enumerate(EXP_UNITS) if (g, k) == divmod(step, TILES)]
        n = MAX_SHARE[step]
        for i, u in enumerate(units):
            out.append(("exp", u))
            m = n // len(units) + (i < n % len(units))
            out += [("max", done + j) for j in range(m)]
            done += m
        out.append(("pv", step - LAG) if step >= LAG else ("last pv", STEPS - LAG + step))
        if step % TILES == TILES - 1:
            out.append(("group", step // TILES))
        out += extra.get(step, [])
    assert done == NMAX
    return out


SCHEDULE = schedule()


def repeated(ap, n):
    return bass.AP(tensor=ap.tensor, offset=ap.offset, ap=[[0, n]] + [list(x) for x in ap.ap])


def attention_layer(nc, x1_dram, q_parts, k_parts, v_dram, w_o, g1, b1, h_dram):
    sems = []
    with ExitStack() as ctx:
        def sb(name, shape, dt=F32):
            return ctx.enter_context(nc.sbuf_tensor(name, shape, dt))

        def pair(name, shape, dt=F32):
            return [sb(f"{name}{p}", shape, dt) for p in range(2)]

        def sem(name):
            sems.append(nc.alloc_semaphore(name))
            return sems[-1]

        wo = sb("wo", [P, D])
        g1b = sb("g1b", [P, D])
        b1b = sb("b1b", [P, D])
        ones = sb("ones_c", [P, P])
        ident = sb("ident_c", [P, P])
        ident16 = sb("ident16", [P, P], BF16)
        hide = sb("hide", [P, P], BF16)
        minus_half = sb("minus_half_c", [P, TILES])
        qx = pair("qx", [96, AH, SEQ], BF16)
        kx = pair("kx", [96, AH, SEQ], BF16)
        kones = sb("kones", [PARTS, SEQ], BF16)
        vtok = pair("vtok", [P, TILES, D])
        vx = pair("vx", [P, TILES, AH, VW])
        mx = sb("mx", [P, AH, TILES])
        mparts = sb("mparts", [AH * TILES, PARTS, P], BF16)
        mrest = sb("mrest", [TILES * AH, P])
        pb = [sb(f"pb{k}", [P, 4, SEQ]) for k in range(PBUF)]
        oT = sb("oT", [P, SEQ])
        rc = sb("rc", [P, TILES, 4, 1])
        otok = sb("otok", [P, TILES, D])
        oT2 = sb("oT2", [P, SEQ])
        x1r = sb("x1r", [P, TILES, D])
        r = sb("r_c", [P, TILES, D])
        bst = sb("bst_c", [P, TILES, 6])
        mv = sb("mv_c", [P, TILES, 2])
        rstd = sb("rstd_c", [P, TILES])
        nrm = sb("nrm", [P, TILES, D])
        h1 = sb("h1", [P, TILES, D])
        h = sb("h_c", [P, TILES, D])

        ps = ctx.enter_context(nc.psum_tensor("psB", [P, 8, 512], F32))
        S_BANK, E_BANK, PV_BANK, MISC = 0, 2, 6, 7

        w_loaded, consts, vx_made = sem("wo_loaded"), sem("att_constants"), sem("vx_made")
        kones_made, kones_loaded = sem("kones_made"), sem("kones_loaded")
        qk_loaded, v_loaded, vx_ready = [[sem(f"qk_loaded{p}_{g}") for g in range(GROUPS)] for p in range(2)], [sem(f"v_loaded{p}") for p in range(2)], sem("vx_ready")
        s_ps, mx_ready = sem("s_ps"), sem("mx_ready")
        mxT_ps, mpart_ready, mrows = sem("mxT_ps"), sem("mpart_ready"), [sem(f"mrows{p}") for p in range(2)]
        e_ps, exp_ready, masked, pv_ps = sem("e_ps"), sem("exp_ready"), sem("masked"), sem("pv_ps")
        oT_sb, oTt_ps, otok_ready = sem("oT_sb"), sem("oTt_ps"), sem("otok_ready")
        oT2_ps, oT2_sb, o_ps, x1r_loaded = sem("oT2_ps"), sem("oT2_sb"), sem("att_o_ps"), sem("x1r_loaded")
        r_ready, var_ready, rstd_ready, nrm_ready = sem("att_r"), sem("att_var"), sem("att_rstd"), sem("att_nrm")
        gain_done, h_ready, h_stored = sem("gain_done"), sem("att_h_ready"), sem("h_stored")
        dve_own = sem("dve_own_c")

        pool_passed, dve_passed, pe_passed = sem("pool_passed_c"), sem("dve_passed_c"), sem("pe_passed_c")
        block = ctx.enter_context(nc.Block())
        x1_rows = x1_dram.rearrange("b (t p) d -> b p t d", p=P)
        h_rows = h_dram.rearrange("b (t p) d -> b p t d", p=P)
        v_rows = v_dram.rearrange("b (t p) d -> b p t d", p=P)

        def rows(eng, body):
            body(0, 0, True, False)
            with eng.Fori(0, BATCH // 2 - 1) as it:
                body(it, 1, False, False)
                body(it, 2, False, False)
            body(BATCH // 2 - 1, 1, False, True)

        def times(it, p):
            return it + p // 2 + 1

        QK_LOADS = 2 * PARTS * 16

        def load_group(sp, it, p, g):
            q, src, heads = p % 2, it * 2 + p, slice(4 * g, 4 * g + 4)
            for s in range(PARTS):
                at = s * PARTS * DH
                sp.dma_start(qx[q][at:at + PARTS * DH, heads, :],
                             q_parts[src].rearrange("j (d h) n -> (j d) h n", d=DH)[:, heads, :]).then_inc(qk_loaded[q][g], 16)
                k = k_parts[src, s].rearrange("(d h) n -> d h n", d=DH)[:, heads, :]
                sp.dma_start(kx[q][at:at + PARTS * DH, heads, :], repeated(k, PARTS)).then_inc(qk_loaded[q][g], 16)

        def load_v(sp, it, p):
            sp.dma_start(vtok[p % 2][:, :, :], v_rows[it * 2 + p]).then_inc(v_loaded[p % 2], 16)

        def store_max(sp, it, p):
            row, q = Row(it, p), p % 2
            sp.wait_ge(mpart_ready, row(4, 4))
            for s in range(PARTS):
                sp.dma_start(qx[q][QK_ROWS + s:QK_ROWS + s + 1, :, :].rearrange("p h (t n) -> p (h t) n", n=P),
                             mparts[:, s, :]).then_inc(mrows[q], 16)

        @block.sync
        def _(sp):
            for g in range(GROUPS):
                load_group(sp, 0, 0, g)
            load_v(sp, 0, 0)
            sp.dma_start(wo[:, :], w_o).then_inc(w_loaded, 16)
            sp.dma_start(g1b[:, :], over_partitions(g1)).then_inc(w_loaded, 16)
            sp.dma_start(b1b[:, :], over_partitions(b1)).then_inc(w_loaded, 16)
            sp.wait_ge(kones_made, 1)
            for q in range(2):
                sp.dma_start(kx[q][QK_ROWS:MAX_ROWS, :, :], kones[:, :].unsqueeze(1).broadcast_to([PARTS, AH, SEQ])).then_inc(kones_loaded, 16)
            for g in range(GROUPS):
                load_group(sp, 0, 1, g)
            load_v(sp, 0, 1)
            store_max(sp, 0, 0)

            def body(it, p, first, loads, last):
                row = Row(it, p)
                if not first:
                    sp.wait_ge(r_ready, Row(it, p - 1)(1, 0))
                    sp.dma_start(x1r[:, :, :], x1_rows[it * 2 + p - 1]).then_inc(x1r_loaded, 16)
                if loads:
                    sp.wait_ge(vx_ready, row(1, 1))
                    load_v(sp, it, p + 2)
                for g in range(GROUPS):
                    if g == GROUPS - 1 and not last:
                        store_max(sp, it, p + 1)
                    if loads:
                        sp.wait_ge(e_ps, row(NEXP, (g + 1) * NEXP // GROUPS))
                        load_group(sp, it, p + 2, g)
            body(0, 0, True, True, False)
            with sp.Fori(0, BATCH // 2 - 2) as it:
                body(it, 1, False, True, False)
                body(it, 2, False, True, False)
            last = BATCH // 2 - 1
            body(last, -1, False, True, False)
            body(last, 0, False, False, False)
            body(last, 1, False, False, True)
            sp.wait_ge(r_ready, BATCH - 1)
            sp.dma_start(x1r[:, :, :], x1_rows[BATCH - 1]).then_inc(x1r_loaded, 16)

        def spread_v(pool, it, p):
            row, q = Row(it, p), p % 2
            wait_apart(pool, v_loaded[q], times(it, p) * 16, pool_passed)
            nc.gpsimd.tensor_copy(vx[q][:, :, :, 0:DH], vtok[q][:, :, :].rearrange("p t (h d) -> p t h d", d=DH)).then_inc(vx_ready, 1)

        @block.gpsimd
        def _(pool):
            nc.gpsimd.memset(ones[:, :], 1.0).then_inc(consts, 1)
            nc.gpsimd.memset(minus_half[:, :], -0.5).then_inc(consts, 1)
            nc.gpsimd.memset(hide[:, :], -3e38).then_inc(consts, 1)
            pool.wait_ge(consts, 3)
            nc.gpsimd.affine_select(out=ident[:, :], in_=ones[:, :], compare_op=ALU.is_equal, fill=0.0, base=0,
                                    pattern=[[-1, P]], channel_multiplier=1).then_inc(consts, 1)
            nc.gpsimd.affine_select(out=ident16[:, :], in_=ones[:, :], compare_op=ALU.is_equal, fill=0.0, base=0,
                                    pattern=[[-1, P]], channel_multiplier=1).then_inc(consts, 1)
            nc.gpsimd.affine_select(out=hide[:, :], in_=hide[:, :], compare_op=ALU.is_gt, fill=0.0, base=0,
                                    pattern=[[1, P]], channel_multiplier=-1).then_inc(consts, 1)
            pool.wait_ge(vx_made, 2)
            spread_v(pool, 0, 0)

            def norm(it, p):
                row = Row(it, p)
                wait_apart(pool, var_ready, row(1, 1), pool_passed)
                nc.gpsimd.tensor_scalar(rstd[:, :], mv[:, :, 1], EPS, None, ALU.add).then_inc(rstd_ready, 1)
                pool.wait_ge(rstd_ready, row(2, 1))
                nc.gpsimd.tensor_tensor(rstd[:, :], rstd[:, :], minus_half[:, :], ALU.pow).then_inc(rstd_ready, 1)

            def gain(it, p):
                row = Row(it, p)
                pool.wait_ge(nrm_ready, row(1, 1))
                nc.gpsimd.tensor_tensor(h1[:, :, :], nrm[:, :, :], g1b[:, :].unsqueeze(1).broadcast_to([P, TILES, D]),
                                        ALU.mult).then_inc(gain_done, 1)
                pool.wait_ge(gain_done, row(1, 1))
                pool.wait_ge(h_stored, row(16, 0))
                nc.gpsimd.tensor_tensor(h[:, :, :], h1[:, :, :], b1b[:, :].unsqueeze(1).broadcast_to([P, TILES, D]),
                                        ALU.add).then_inc(h_ready, 1)
                pool.wait_ge(h_ready, row(1, 1))
                pool.dma_start(h_rows[it * 2 + p], h[:, :, :]).then_inc(h_stored, 16)

            def body(it, p, first, last):
                row = Row(it, p)
                for what, n in SCHEDULE:
                    if what == "exp":
                        g, kt, h0, heads = EXP_UNITS[n]
                        if h0 + heads == 4:
                            step = g * TILES + kt
                            wait_apart(pool, exp_ready, row(NEXP, n + 2), pool_passed)
                            nc.gpsimd.affine_select(out=pb[step % PBUF][:, :, 0:P], in_=pb[step % PBUF][:, :, 0:P],
                                                    compare_op=ALU.is_ge, fill=0.0, base=0,
                                                    pattern=[[0, 4], [1, P]], channel_multiplier=-1).then_inc(masked, 1)
                    elif what == "spread v" and not last:
                        if not first:
                            pool.wait_ge(pv_ps, row(STEPS, 0))
                        spread_v(pool, it, p + 1)
                    elif what == "last norm" and not first:
                        norm(it, p - 1)
                    elif what == "last gain" and not first:
                        gain(it, p - 1)
            rows(pool, body)
            norm(BATCH // 2 - 1, 1)
            gain(BATCH // 2 - 1, 1)
            pool.wait_ge(h_stored, 16 * BATCH)

        @block.scalar
        def _(act):
            act.sem_inc(exp_ready, 1)

            def exp_unit(row, u):
                g, kt, h0, heads = EXP_UNITS[u]
                step, width = g * TILES + kt, SEQ - kt * P
                stride = 512 if width > 256 else width
                src = ps[:, E_BANK + 2 * (u % 2):E_BANK + 2 * (u % 2) + 2, :].rearrange("p k n -> p (k n)")
                src = src[:, 0:heads * stride].rearrange("p (h n) -> p h n", n=stride)[:, :, 0:width]
                act.wait_ge(e_ps, row(NEXP, u + 1))
                used = row(STEPS, step + 1 - PBUF)
                if not (isinstance(used, int) and used <= 0):
                    act.wait_ge(pv_ps, used)
                nc.scalar.activation(pb[step % PBUF][:, h0:h0 + heads, 0:width], src, ACT.Exp).then_inc(exp_ready, 1)

            def oT_copy(row, g):
                act.wait_ge(pv_ps, row(STEPS, TILES * g + TILES))
                act.wait_ge(oTt_ps, row(GROUPS, g))
                nc.scalar.activation(oT[:, :], ps[:, PV_BANK, :], ACT.Copy).then_inc(oT_sb, 1)

            def oT2_copy(row):
                act.wait_ge(oT2_ps, row(1, 1))
                act.wait_ge(o_ps, row(1, 0))
                nc.scalar.activation(oT2[:, :], ps[:, MISC, :], ACT.Copy).then_inc(oT2_sb, 1)

            def body(it, p, first, last):
                row, before = Row(it, p), Row(it, p - 1)
                for what, n in SCHEDULE:
                    if what == "exp":
                        exp_unit(row, n)
                    elif what == "pv" and n % TILES == TILES - 1:
                        oT_copy(row, n // TILES)
                    elif what == "last pv" and n == STEPS - 1 and not first:
                        oT_copy(before, GROUPS - 1)
                    elif what == "last out" and not first:
                        oT2_copy(before)
            rows(act, body)
            end = Row(BATCH // 2 - 1, 1)
            oT_copy(end, GROUPS - 1)
            oT2_copy(end)

        @block.vector
        def _(dve):
            nc.vector.memset(kones[:, :], 1.0).then_inc(kones_made, 1)
            for q in range(2):
                nc.vector.memset(vx[q][:, :, :, :], 0.0).then_inc(vx_made, 1)
            dve.wait_ge(vx_made, 2)
            for q in range(2):
                nc.vector.memset(vx[q][:, :, :, DH:DH + 1], 1.0).then_inc(vx_made, 1)

            def max_unit(row, u):
                qt, h0, heads = MAX_UNITS[u]
                width = (qt + 1) * P
                dve.wait_ge(s_ps, row(NMAX, u + 1))
                nc.vector.tensor_reduce(mx[:, h0:h0 + heads, qt],
                                        ps[:, S_BANK + u % 2, 0:heads * width].rearrange("p (h n) -> p h n", n=width),
                                        AX.X, ALU.max).then_inc(mx_ready, 1)

            def max_rows(row, it, p):
                q = p % 2
                src = ps[0:TILES * AH, MISC, 0:P]
                dve.wait_ge(mxT_ps, row(1, 1))
                if not (isinstance(it, int) and times(it, p - 1) <= 0):
                    dve.wait_ge(mrows[1 - q], times(it, p - 1) * 16 * PARTS)
                nc.vector.tensor_scalar(mparts[:, 0, :], src, -1.0, None, ALU.mult).then_inc(mpart_ready, 1)
                dve.wait_ge(mpart_ready, row(4, 1))
                nc.vector.scalar_tensor_tensor(out=mrest[:, :], in0=src, scalar=-1.0, in1=mparts[:, 0, :],
                                               op0=ALU.mult, op1=ALU.subtract).then_inc(mpart_ready, 1)
                dve.wait_ge(mpart_ready, row(4, 2))
                nc.vector.tensor_copy(mparts[:, 1, :], mrest[:, :]).then_inc(mpart_ready, 1)
                dve.wait_ge(mpart_ready, row(4, 3))
                nc.vector.tensor_tensor(mparts[:, 2, :], mrest[:, :], mparts[:, 1, :], ALU.subtract).then_inc(mpart_ready, 1)

            def heads(row, g):
                src = ps[:, MISC, :].rearrange("p (t r n) -> p t r n", t=TILES, r=4)
                dve.wait_ge(oTt_ps, row(GROUPS, g + 1))
                dve.wait_ge(otok_ready, row(2 * GROUPS, 2 * g))
                nc.vector.reciprocal(rc[:, :, :, :], src[:, :, :, DH:DH + 1]).then_inc(otok_ready, 1)
                dve.wait_ge(otok_ready, row(2 * GROUPS, 2 * g + 1))
                if g == 0:
                    dve.wait_ge(oT2_ps, row(1, 0))
                nc.vector.tensor_tensor(otok[:, :, g * 32:(g + 1) * 32].rearrange("p t (r d) -> p t r d", r=4),
                                        src[:, :, :, 0:DH], rc[:, :, :, :].broadcast_to([P, TILES, 4, DH]),
                                        ALU.mult).then_inc(otok_ready, 1)

            def residual(row):
                dve.wait_ge(o_ps, row(1, 1))
                dve.wait_ge(x1r_loaded, row(16, 16))
                dve.wait_ge(nrm_ready, row(1, 0))
                nc.vector.tensor_tensor(r[:, :, :].rearrange("p t n -> p (t n)"), ps[:, MISC, :],
                                        x1r[:, :, :].rearrange("p t n -> p (t n)"), ALU.add).then_inc(r_ready, 1)
                dve.wait_ge(r_ready, row(1, 1))
                for t in range(TILES):
                    ins = nc.vector.bn_stats(bst[:, t, :], r[:, t, :])
                ins.then_inc(dve_own, 1)
                dve.wait_ge(rstd_ready, row(2, 0))
                wait_apart(dve, dve_own, row(1, 1), dve_passed)
                for t in range(TILES):
                    ins = nc.vector.bn_aggr(mv[:, t, :], bst[:, t, :])
                ins.then_inc(var_ready, 1)

            def normalise(row):
                dve.wait_ge(var_ready, row(1, 1))
                dve.wait_ge(rstd_ready, row(2, 2))
                dve.wait_ge(gain_done, row(1, 0))
                for t in range(TILES):
                    ins = nc.vector.tensor_scalar(nrm[:, t, :], r[:, t, :], mv[:, t, 0:1], rstd[:, t:t + 1],
                                                  ALU.subtract, ALU.mult)
                ins.then_inc(nrm_ready, 1)

            for u in range(NMAX):
                max_unit(Row(0, 0), u)
            max_rows(Row(0, 0), 0, 0)

            def body(it, p, first, last):
                row, before, after = Row(it, p), Row(it, p - 1), Row(it, p + 1)
                for what, n in SCHEDULE:
                    if what == "max" and not last:
                        max_unit(after, n)
                    elif what == "max rows" and not last:
                        max_rows(after, it, p + 1)
                    elif what == "heads":
                        heads(row, n)
                    elif what == "last heads" and not first:
                        heads(before, n)
                    elif what == "last norm" and not first:
                        residual(before)
                    elif what == "last normalise" and not first:
                        normalise(before)
            rows(dve, body)
            end = Row(BATCH // 2 - 1, 1)
            heads(end, GROUPS - 1)
            residual(end)
            normalise(end)

        @block.tensor
        def _(pe):
            pe.wait_ge(consts, 6)

            def max_unit(row, it, p, u):
                qt, h0, heads = MAX_UNITS[u]
                q, width = p % 2, (qt + 1) * P
                if u % (NMAX // GROUPS) == 0:
                    pe.wait_ge(qk_loaded[q][h0 // 4], times(it, p) * QK_LOADS)
                n = row(NMAX, u - 1)
                if not isinstance(n, int) or n > 0:
                    pe.wait_ge(mx_ready, n)
                for j in range(heads):
                    out = ps[:, S_BANK + u % 2, j * width:(j + 1) * width]
                    nc.tensor.matmul(out, qx[q][0:QK_ROWS, h0 + j, qt * P:(qt + 1) * P],
                                     kx[q][0:QK_ROWS, h0 + j, 0:width], start=True, stop=False)
                    ins = nc.tensor.matmul(out[:, qt * P:width], ident16[:, :], hide[:, :], start=False, stop=True)
                ins.then_inc(s_ps, 1)

            def max_rows(row):
                wait_apart(pe, mx_ready, row(NMAX, NMAX), pe_passed)
                nc.tensor.transpose(ps[0:TILES * AH, MISC, 0:P], mx[:, :, :].rearrange("p h t -> p (h t)"),
                                    ident[:, :]).then_inc(mxT_ps, 1)

            def exp_unit(row, it, p, u):
                g, kt, h0, heads = EXP_UNITS[u]
                q, width = p % 2, SEQ - kt * P
                stride = 512 if width > 256 else width
                if u == 0:
                    pe.wait_ge(mrows[q], times(it, p) * 16 * PARTS)
                pe.wait_ge(exp_ready, row(NEXP, u))
                for j in range(heads):
                    at = (E_BANK + 2 * (u % 2)) * 512 + j * stride
                    ins = nc.tensor.matmul(ps[:, at // 512, at % 512:at % 512 + width],
                                           kx[q][0:MAX_ROWS, 4 * g + h0 + j, kt * P:(kt + 1) * P],
                                           qx[q][0:MAX_ROWS, 4 * g + h0 + j, kt * P:SEQ], start=True, stop=True)
                ins.then_inc(e_ps, 1)

            def pv(row, it, p, step):
                g, kt = divmod(step, TILES)
                q, width = p % 2, SEQ - kt * P
                if step == 0:
                    pe.wait_ge(vx_ready, row(1, 1))
                if kt == 0:
                    pe.wait_ge(oT_sb, row(GROUPS, g))
                pe.wait_ge(masked, row(STEPS, step + 1))
                for j in range(4):
                    ins = nc.tensor.matmul(ps[32 * j:32 * (j + 1), PV_BANK, kt * P:SEQ], vx[q][:, kt, 4 * g + j, :],
                                           pb[step % PBUF][:, j, 0:width], start=(kt == 0), stop=(kt == TILES - 1))
                ins.then_inc(pv_ps, 1)

            def heads(row, g):
                pe.wait_ge(oT_sb, row(GROUPS, g + 1))
                pe.wait_ge(otok_ready, row(2 * GROUPS, 2 * g))
                for t in range(TILES):
                    ins = nc.tensor.transpose(ps[:, MISC, t * P:(t + 1) * P], oT[:, t * P:(t + 1) * P], ident[:, :])
                ins.then_inc(oTt_ps, 1)

            def out_proj(row):
                pe.wait_ge(otok_ready, row(2 * GROUPS, 2 * GROUPS))
                for t in range(TILES):
                    ins = nc.tensor.transpose(ps[:, MISC, t * P:(t + 1) * P], otok[:, t, :], ident[:, :])
                ins.then_inc(oT2_ps, 1)

            def out_proj2(row):
                pe.wait_ge(oT2_sb, row(1, 1))
                for t in range(TILES):
                    ins = nc.tensor.matmul(ps[:, MISC, t * P:(t + 1) * P], oT2[:, t * P:(t + 1) * P], wo[:, :],
                                           start=True, stop=True)
                ins.then_inc(o_ps, 1)

            for u in range(NMAX):
                max_unit(Row(0, 0), 0, 0, u)
            max_rows(Row(0, 0))
            pe.wait_ge(w_loaded, 48)
            pe.wait_ge(kones_loaded, 32)
            pe.wait_ge(vx_made, 4)

            def body(it, p, first, last):
                row, before, after = Row(it, p), Row(it, p - 1), Row(it, p + 1)
                for what, n in SCHEDULE:
                    if what == "exp":
                        exp_unit(row, it, p, n)
                    elif what == "max" and not last:
                        max_unit(after, it, p + 1, n)
                    elif what == "max rows" and not last:
                        pe.wait_ge(otok_ready, row(2 * GROUPS, 2 * 2))
                        max_rows(after)
                    elif what == "pv":
                        pv(row, it, p, n)
                    elif what == "last pv" and not first:
                        pv(before, it, p - 1, n)
                    elif what == "heads":
                        if n == 0:
                            if not first:
                                pe.wait_ge(r_ready, before(1, 1))
                        elif n == 2 and not last:
                            pe.wait_ge(mpart_ready, after(4, 2))
                        heads(row, n)
                    elif what == "last heads" and not first:
                        heads(before, n)
                    elif what == "last out" and not first:
                        out_proj(before)
                    elif what == "last norm" and not first:
                        out_proj2(before)
            rows(pe, body)
            end = Row(BATCH // 2 - 1, 1)
            for n in range(STEPS - LAG, STEPS):
                pv(end, BATCH // 2 - 1, 1, n)
            heads(end, GROUPS - 1)
            out_proj(end)
            out_proj2(end)
    end_stage(nc, sems)


E, TOPK, F = 8, 2, 512
FC = F // P
TOKENS = BATCH * SEQ
ALL_TILES = TOKENS // P
REGION = TOKENS + P
SLOTS = E * REGION + P
PAY = D + 1
RESULTS = TOPK * TOKENS
NOWHERE = 1 << 20
SLOT_TILES = RESULTS // P + E
ROUTE_STEPS = 29


def route(nc, h_dram, wg, slots, gates, count):
    sems = []
    with ExitStack() as ctx:
        def sb(name, shape, dt=F32):
            return ctx.enter_context(nc.sbuf_tensor(name, shape, dt))

        def pair(name, shape, dt=F32):
            return [sb(f"{name}{p}", shape, dt) for p in range(2)]

        def sem(name):
            sems.append(nc.alloc_semaphore(name))
            return sems[-1]

        wgs = sb("wgs", [P, E])
        ones = sb("ones_r", [P, P])
        ident = sb("ident_r", [P, P])
        before = sb("before", [P, P])
        rank = sb("rank", [P, E])
        region = sb("region", [P, E])
        fill_at = sb("fill_at", [P, E])
        fill_idx = sb("fill_idx", [P, E], U32)
        filler = sb("filler", [P, PAY])
        rows_of = sb("rows_of", [P, TOPK, ALL_TILES], U32)
        pay = [pair(f"pay{k}_", [P, TILES, PAY]) for k in range(TOPK)]
        hT = pair("hT_r", [P, SEQ])
        lg = sb("lg", [P, TILES, E])
        lg2 = sb("lg2", [P, TILES, E])
        m = [sb(f"m{k}", [P, TILES, 1]) for k in range(TOPK)]
        key = sb("key", [P, TILES, E])
        kmax = sb("kmax", [P, TILES, 1])
        sel = pair("sel", [P, TOPK, TILES, E])
        cnt = pair("cnt", [P, TILES, E])
        ex = sb("ex", [P, TILES])
        den = sb("den_r", [P, TILES])
        base = sb("base", [P, TILES, E])
        pos = sb("pos", [P, TILES, E])
        pick = sb("pick", [P, TILES, E])
        at = sb("at", [P, TILES])
        idx = [pair(f"idx{k}_", [P, TILES], U32) for k in range(TOPK)]
        ps = ctx.enter_context(nc.psum_tensor("psR", [P, 8, 512], F32))
        w_loaded, consts = sem("wg_loaded"), sem("route_constants")
        h_loaded = [sem(f"h_loaded{p}") for p in range(2)]
        scattered = [sem(f"scattered{p}") for p in range(2)]
        hT_ps, hT_sb, lg_ps, diff_ready, exp_ready = sem("hT_ps"), sem("hT_sb"), sem("lg_ps"), sem("diff_ready"), sem("rexp_ready")
        cnt_ready, pos_ps, idx_ready, fill_ready, filled = sem("cnt_ready"), sem("pos_ps"), sem("idx_ready"), sem("fill_ready"), sem("filled")
        dve_own = sem("dve_own_r")
        pool_passed, sp_passed = sem("pool_passed_r"), sem("sp_passed_r")
        block = ctx.enter_context(nc.Block())
        h_rows = h_dram.rearrange("b (t p) d -> b p t d", p=P)

        @block.sync
        def _(sp):
            sp.dma_start(wgs[:, :], wg).then_inc(w_loaded, 16)
            with sp.Fori(0, BATCH // 2) as it:
                for p in range(2):
                    wait_apart(sp, hT_ps, it * 2, sp_passed)
                    sp.wait_ge(scattered[p], it * (16 * TOPK * TILES))
                    for k in range(TOPK):
                        sp.dma_start(pay[k][p][:, :, 0:D], h_rows[it * 2 + p]).then_inc(h_loaded[p], 16)

        @block.gpsimd
        def _(pool):
            nc.gpsimd.memset(ones[:, :], 1.0).then_inc(consts, 1)
            nc.gpsimd.memset(filler[:, :], 0.0).then_inc(consts, 1)
            pool.wait_ge(consts, 2)
            nc.gpsimd.affine_select(out=ident[:, :], in_=ones[:, :], compare_op=ALU.is_equal, fill=0.0, base=0,
                                    pattern=[[-1, P]], channel_multiplier=1).then_inc(consts, 1)
            nc.gpsimd.affine_select(out=before[:, :], in_=ones[:, :], compare_op=ALU.is_gt, fill=0.0, base=0,
                                    pattern=[[1, P]], channel_multiplier=-1).then_inc(consts, 1)
            nc.gpsimd.iota(rank[:, :], pattern=[[-1, E]], base=E, channel_multiplier=0,
                           allow_small_or_imprecise_dtypes=True).then_inc(consts, 1)
            nc.gpsimd.iota(region[:, :], pattern=[[REGION, E]], base=0, channel_multiplier=0,
                           allow_small_or_imprecise_dtypes=True).then_inc(consts, 1)
            nc.gpsimd.iota(fill_at[:, :], pattern=[[REGION, E]], base=0, channel_multiplier=1,
                           allow_small_or_imprecise_dtypes=True).then_inc(consts, 1)
            nc.gpsimd.iota(rows_of[:, :, :], pattern=[[TOKENS, TOPK], [P, ALL_TILES]], base=0,
                           channel_multiplier=1).then_inc(consts, 1)
            nc.gpsimd.iota(filler[:, D:PAY].bitcast(U32), pattern=[[0, 1]], base=NOWHERE, channel_multiplier=0).then_inc(consts, 1)
            with pool.Fori(0, BATCH // 2) as it:
                for p in range(2):
                    row = Row(it, p)
                    for k in range(TOPK):
                        wait_apart(pool, idx_ready, row(TOPK, k + 1), pool_passed)
                        for t in range(TILES):
                            nc.gpsimd.indirect_dma_start(out=slots, out_offset=bass.IndirectOffsetOnAxis(ap=idx[k][p][:, t:t + 1], axis=0),
                                                         in_=pay[k][p][:, t, :], in_offset=None, bounds_check=SLOTS - 1,
                                                         oob_is_err=False).then_inc(scattered[p], 16)
            pool.wait_ge(fill_ready, 1)
            pool.dma_start(slots[E * REGION:SLOTS, :], filler[:, :]).then_inc(filled, 16)
            for e in range(E):
                nc.gpsimd.indirect_dma_start(out=slots, out_offset=bass.IndirectOffsetOnAxis(ap=fill_idx[:, e:e + 1], axis=0),
                                             in_=filler[:, :], in_offset=None, bounds_check=SLOTS - 1,
                                             oob_is_err=False).then_inc(filled, 16)
            for p in range(2):
                pool.wait_ge(scattered[p], 16 * TOPK * TILES * (BATCH // 2))
            pool.wait_ge(filled, 16 * (E + 1))

        @block.scalar
        def _(act):
            with act.Fori(0, BATCH // 2) as it:
                for p in range(2):
                    row = Row(it, p)
                    act.wait_ge(hT_ps, row(1, 1))
                    act.wait_ge(lg_ps, it * 2)
                    nc.scalar.activation(hT[p][:, :], ps[:, p, :], ACT.Copy).then_inc(hT_sb, 1)
                    act.wait_ge(diff_ready, row(1, 1))
                    nc.scalar.activation(ex[:, :], den[:, :], ACT.Exp).then_inc(exp_ready, 1)

        @block.vector
        def _(dve):
            nc.vector.memset(count[:, :], 0.0).then_inc(dve_own, 1)
            dve.wait_ge(dve_own, 1)
            dve.wait_ge(consts, 9)
            own = Chain(dve, dve_own, ROUTE_STEPS)
            with dve.Fori(0, BATCH // 2) as it:
                for p in range(2):
                    row = Row(it, p)
                    own.begin(lambda per, k, row=row: row(per, k) + 1)

                    def step(ins):
                        own.add(ins)
                        own.wait()

                    def bc(x, n=E):
                        return x.broadcast_to([P, TILES, n])
                    tiles = bass.ds(it * (2 * TILES) + p * TILES, TILES)
                    dve.wait_ge(scattered[p], it * (16 * TOPK * TILES))
                    for k in range(TOPK):
                        step(nc.vector.tensor_copy(pay[k][p][:, :, D:PAY].bitcast(U32), rows_of[:, k, tiles].unsqueeze(2)))
                    dve.wait_ge(lg_ps, row(1, 1))
                    step(nc.vector.tensor_copy(lg[:, :, :].rearrange("p t e -> p (t e)"), ps[:, 2 + p, 0:TILES * E]))
                    dve.wait_ge(pos_ps, it * 2)
                    src = lg
                    for k in range(TOPK):
                        step(nc.vector.tensor_reduce(m[k][:, :, :], src[:, :, :], AX.X, ALU.max))
                        step(nc.vector.tensor_tensor(key[:, :, :], src[:, :, :], bc(m[k][:, :, :]), ALU.is_equal))
                        step(nc.vector.tensor_tensor(key[:, :, :], key[:, :, :], rank[:, :].unsqueeze(1).broadcast_to([P, TILES, E]), ALU.mult))
                        step(nc.vector.tensor_reduce(kmax[:, :, :], key[:, :, :], AX.X, ALU.max))
                        step(nc.vector.tensor_tensor(sel[p][:, k, :, :], key[:, :, :], bc(kmax[:, :, :]), ALU.is_equal))
                        if k == 0:
                            step(nc.vector.scalar_tensor_tensor(out=lg2[:, :, :], in0=sel[p][:, 0, :, :], scalar=-3e38,
                                                                in1=lg[:, :, :], op0=ALU.mult, op1=ALU.add))
                            src = lg2
                    nc.vector.tensor_tensor(cnt[p][:, :, :], sel[p][:, 0, :, :], sel[p][:, 1, :, :], ALU.add).then_inc(cnt_ready, 1)
                    nc.vector.tensor_tensor(den[:, :], m[1][:, :, 0], m[0][:, :, 0], ALU.subtract).then_inc(diff_ready, 1)
                    dve.wait_ge(exp_ready, row(1, 1))
                    step(nc.vector.tensor_scalar(den[:, :], ex[:, :], 1.0, None, ALU.add))
                    step(nc.vector.reciprocal(den[:, :], den[:, :]))
                    step(nc.vector.tensor_copy(gates[:, 0, tiles], den[:, :]))
                    step(nc.vector.tensor_tensor(gates[:, 1, tiles], den[:, :], ex[:, :], ALU.mult))
                    dve.wait_ge(pos_ps, row(1, 1))
                    step(nc.vector.tensor_copy(base[:, 0, :], count[:, :]))
                    for t in range(1, TILES):
                        step(nc.vector.tensor_tensor(base[:, t, :], ps[:, 6 + p, (t - 1) * E:t * E], base[:, t - 1, :], ALU.add))
                    step(nc.vector.tensor_tensor(count[:, :], ps[:, 6 + p, (TILES - 1) * E:TILES * E], base[:, TILES - 1, :], ALU.add))
                    step(nc.vector.tensor_tensor(pos[:, :, :], ps[:, 4 + p, 0:TILES * E].rearrange("p (t e) -> p t e", e=E), base[:, :, :], ALU.add))
                    step(nc.vector.tensor_tensor(pos[:, :, :], pos[:, :, :], region[:, :].unsqueeze(1).broadcast_to([P, TILES, E]), ALU.add))
                    for k in range(TOPK):
                        step(nc.vector.tensor_tensor(pick[:, :, :], sel[p][:, k, :, :], pos[:, :, :], ALU.mult))
                        step(nc.vector.tensor_reduce(at[:, :], pick[:, :, :], AX.X, ALU.add))
                        nc.vector.tensor_copy(idx[k][p][:, :], at[:, :]).then_inc(idx_ready, 1)
                        dve.wait_ge(idx_ready, row(TOPK, k + 1))
                    own.end()
            nc.vector.tensor_tensor(fill_at[:, :], fill_at[:, :], count[:, :], ALU.add).then_inc(dve_own, 1)
            dve.wait_ge(dve_own, 2 + ROUTE_STEPS * BATCH)
            nc.vector.tensor_copy(fill_idx[:, :], fill_at[:, :]).then_inc(fill_ready, 1)

        @block.tensor
        def _(pe):
            pe.wait_ge(w_loaded, 16)
            pe.wait_ge(consts, 9)
            with pe.Fori(0, BATCH // 2) as it:
                for p in range(2):
                    row = Row(it, p)
                    pe.wait_ge(h_loaded[p], it * (16 * TOPK) + 16 * TOPK)
                    pe.wait_ge(hT_sb, it * 2)
                    for t in range(TILES):
                        ins = nc.tensor.transpose(ps[:, p, t * P:(t + 1) * P], pay[0][p][:, t, 0:D], ident[:, :])
                    ins.then_inc(hT_ps, 1)
                    pe.wait_ge(hT_sb, row(1, 1))
                    pe.wait_ge(cnt_ready, it * 2)
                    for t in range(TILES):
                        ins = nc.tensor.matmul(ps[:, 2 + p, t * E:(t + 1) * E], hT[p][:, t * P:(t + 1) * P], wgs[:, :],
                                               start=True, stop=True)
                    ins.then_inc(lg_ps, 1)
                    pe.wait_ge(cnt_ready, row(1, 1))
                    pe.wait_ge(idx_ready, it * (2 * TOPK))
                    nc.tensor.matmul(ps[:, 4 + p, 0:TILES * E], before[:, :], cnt[p][:, :, :].rearrange("p t e -> p (t e)"),
                                     start=True, stop=True)
                    nc.tensor.matmul(ps[:, 6 + p, 0:TILES * E], ones[:, :], cnt[p][:, :, :].rearrange("p t e -> p (t e)"),
                                     start=True, stop=True).then_inc(pos_ps, 1)
    end_stage(nc, sems)


def plan_tiles(nc, count, table):
    sems = []
    with ExitStack() as ctx:
        def sb(name, shape, dt=F32):
            return ctx.enter_context(nc.sbuf_tensor(name, shape, dt))

        def sem(name):
            sems.append(nc.alloc_semaphore(name))
            return sems[-1]

        own, made = sem("plan_steps"), sem("plan_constants")
        J, M = SLOT_TILES, TOKENS // P
        full = sb("full", [1, E, M])
        passed = sb("passed", [1, E, M])
        need = sb("need", [1, E, 1])
        upto = sb("upto_p", [1, E + 1])
        number = sb("number", [1, J])
        ids = sb("ids", [1, E])
        cmp = sb("cmp", [1, J, E])
        ex = sb("ex_p", [1, J, 1])
        st = sb("st_p", [1, J, 1])
        live = sb("live", [1, J, 1])
        row = sb("row_p", [1, J, 1])
        block = ctx.enter_context(nc.Block())

        @block.gpsimd
        def _(pool):
            nc.gpsimd.iota(full[:, :, :], pattern=[[0, E], [P, M]], base=0, channel_multiplier=0,
                           allow_small_or_imprecise_dtypes=True).then_inc(made, 1)
            nc.gpsimd.iota(number[:, :], pattern=[[1, J]], base=0, channel_multiplier=0,
                           allow_small_or_imprecise_dtypes=True).then_inc(made, 1)
            nc.gpsimd.iota(ids[:, :], pattern=[[1, E]], base=0, channel_multiplier=0,
                           allow_small_or_imprecise_dtypes=True).then_inc(made, 1)

        @block.vector
        def _(dve):
            n = [0]

            def step(ins):
                n[0] += 1
                ins.then_inc(own, 1)
                dve.wait_ge(own, n[0])
            v = nc.vector
            dve.wait_ge(made, 3)
            step(v.tensor_tensor(passed[:, :, :], count[0:1, :].unsqueeze(2).broadcast_to([1, E, M]), full[:, :, :], ALU.is_gt))
            step(v.tensor_reduce(need[:, :, :], passed[:, :, :], AX.X, ALU.add))
            step(v.memset(upto[:, 0:1], 0.0))
            for e in range(E):
                step(v.tensor_tensor(upto[:, e + 1:e + 2], upto[:, e:e + 1], need[:, e, :], ALU.add))
            num = number[:, :].unsqueeze(2).broadcast_to([1, J, E])
            step(v.tensor_tensor(cmp[:, :, :], upto[:, 1:E + 1].unsqueeze(1).broadcast_to([1, J, E]), num, ALU.is_le))
            step(v.tensor_reduce(ex[:, :, :], cmp[:, :, :], AX.X, ALU.add))
            step(v.tensor_tensor(cmp[:, :, :], ids[:, :].unsqueeze(1).broadcast_to([1, J, E]), ex[:, :, :].broadcast_to([1, J, E]), ALU.is_equal))
            step(v.tensor_tensor(cmp[:, :, :], cmp[:, :, :], upto[:, 0:E].unsqueeze(1).broadcast_to([1, J, E]), ALU.mult))
            step(v.tensor_reduce(st[:, :, :], cmp[:, :, :], AX.X, ALU.add))
            step(v.tensor_scalar(live[:, :, :], ex[:, :, :], float(E), float(P), ALU.is_lt, ALU.mult))
            step(v.tensor_tensor(row[:, :, 0], number[:, :], st[:, :, 0], ALU.subtract))
            step(v.tensor_tensor(row[:, :, :], row[:, :, :], live[:, :, :], ALU.mult))
            step(v.scalar_tensor_tensor(out=row[:, :, :], in0=ex[:, :, :], scalar=float(REGION), in1=row[:, :, :],
                                        op0=ALU.mult, op1=ALU.add))
            step(v.tensor_copy(table[:, 0, :], row[:, :, 0]))
            step(v.tensor_scalar(ex[:, :, :], ex[:, :, :], float(E - 1), None, ALU.min))
            step(v.tensor_scalar(table[:, 1, :], ex[:, :, 0], float(D + FC), None, ALU.mult))
            step(v.tensor_scalar(table[:, 2, :], ex[:, :, 0], float(F), None, ALU.mult))
    end_stage(nc, sems)


RING = 4
BIAS = D + FC


class Tile:

    def __init__(self, it, p):
        self.it, self.p = it, p
        self.j = it * RING + p
        self.turn = it + p // RING
        self.ring, self.pair = p % RING, p % 2

    def shift(self, d):
        if isinstance(self.it, int) and not 0 <= self.j + d < SLOT_TILES:
            return None
        return Tile(self.it, self.p + d)

    def done(self, before=0):
        if isinstance(self.it, int) and self.j + 1 - before <= 0:
            return None
        return self.it * RING + (self.p + 1 - before)


def all_tiles(eng, body):
    for p in range(RING):
        body(Tile(0, p))
    with eng.Fori(1, SLOT_TILES // RING - 1) as it:
        for p in range(RING):
            body(Tile(it, p))
    for p in range(RING):
        body(Tile(SLOT_TILES // RING - 1, p))


def experts(nc, slots, w1, bb1, w2, bb2, table, results):
    sems = []
    with ExitStack() as ctx:
        def sb(name, shape, dt=F32):
            return ctx.enter_context(nc.sbuf_tensor(name, shape, dt))

        def ring(name, n, shape, dt=F32):
            return [sb(f"{name}{p}", shape, dt) for p in range(n)]

        def sem(name):
            sems.append(nc.alloc_semaphore(name))
            return sems[-1]

        w1s = sb("w1s", [P, E * F])
        w2s = sb("w2s", [P, E * F])
        b1s = sb("b1s", [E * FC, P])
        biases = sb("biases", [P, E, BIAS])
        ones = sb("ones_e", [P, P])
        ident = sb("ident_e", [P, P])
        hin = ring("hin", RING, [P, PAY])
        dest = ring("dest", RING, [P, 1], U32)
        y = ring("y_e", RING, [P, D])
        w1t = ring("w1t", 2, [P, F])
        hT = ring("hT_e", 2, [P, P])
        pre = ring("pre", 2, [P, FC, P])
        gT = ring("gT", 2, [P, FC, P])
        ps = ctx.enter_context(nc.psum_tensor("psE", [P, 8, 512], F32))
        HT_BANK, UP_BANK, Y_BANK = 0, 2, 4
        w_loaded, consts = sem("moe_weights"), sem("moe_constants")
        b1_ps, b1_ready = sem("b1_ps"), sem("b1_ready")
        h_loaded = [sem(f"slots_loaded{p}") for p in range(RING)]
        stored = [sem(f"results_stored{p}") for p in range(RING)]
        hT_ps, hT_sb, w1_ready, up_ps, pre_ready, g_ready = sem("ehT_ps"), sem("ehT_sb"), sem("w1_ready"), sem("up_ps"), sem("pre_ready"), sem("g_ready")
        y_ps, y_ready, dest_ready = sem("y_ps"), sem("ey_ready"), sem("dest_ready")
        pool_passed = sem("pool_passed_e")
        block = ctx.enter_context(nc.Block())
        WEIGHT_LOADS = 2 * E + 2

        def offset(eng, row, tile, bound):
            cell = table[0:1, row, tile.j:tile.j + 1] if isinstance(tile.j, int) else table[0:1, row, bass.ds(tile.j, 1)]
            return eng.value_load(cell, min_val=0, max_val=bound)

        def wait(eng, sem, value):
            if value is not None:
                eng.wait_ge(sem, value)

        @block.sync
        def _(sp):
            def load(tile):
                at = offset(sp, 0, tile, SLOTS - P)
                wait(sp, hT_ps, tile.done(RING))
                wait(sp, dest_ready, tile.done(RING))
                sp.dma_start(hin[tile.ring][:, :], slots[bass.ds(at, P), :]).then_inc(h_loaded[tile.ring], 16)

            for p in range(RING - 1):
                load(Tile(0, p))
            sp.dma_start(b1s[:, :], bb1.rearrange("e (c p) -> (e c) p", p=P)).then_inc(w_loaded, 16)
            sp.dma_start(biases[:, :, 0:D], over_partitions(bb2)).then_inc(w_loaded, 16)
            for e in range(E):
                sp.dma_start(w1s[:, e * F:(e + 1) * F], w1[e]).then_inc(w_loaded, 16)
                sp.dma_start(w2s[:, e * F:(e + 1) * F].rearrange("p (c d) -> p c d", c=FC),
                             w2[e].rearrange("(c p) d -> p c d", p=P)).then_inc(w_loaded, 16)

            def body(tile):
                if tile.shift(RING - 1):
                    load(tile.shift(RING - 1))
            all_tiles(sp, body)

        @block.gpsimd
        def _(pool):
            nc.gpsimd.memset(ones[:, :], 1.0).then_inc(consts, 1)
            pool.wait_ge(consts, 1)
            nc.gpsimd.affine_select(out=ident[:, :], in_=ones[:, :], compare_op=ALU.is_equal, fill=0.0, base=0,
                                    pattern=[[-1, P]], channel_multiplier=1).then_inc(consts, 1)

            def body(tile):
                wait_apart(pool, y_ready, tile.done(), pool_passed)
                nc.gpsimd.indirect_dma_start(out=results, out_offset=bass.IndirectOffsetOnAxis(ap=dest[tile.ring][:, 0:1], axis=0),
                                             in_=y[tile.ring][:, :], in_offset=None, bounds_check=RESULTS - 1,
                                             oob_is_err=False).then_inc(stored[tile.ring], 16)
            all_tiles(pool, body)
            for q in range(RING):
                pool.wait_ge(stored[q], 16 * (SLOT_TILES // RING))

        @block.scalar
        def _(act):
            def weights(tile):
                at = offset(act, 2, tile, (E - 1) * F)
                wait(act, up_ps, tile.done(2))
                nc.scalar.activation(w1t[tile.pair][:, :], w1s[:, bass.ds(at, F)], ACT.Copy).then_inc(w1_ready, 1)

            def turned(tile):
                act.wait_ge(hT_ps, tile.done())
                wait(act, up_ps, tile.done(2))
                nc.scalar.activation(hT[tile.pair][:, :], ps[:, HT_BANK + tile.pair, 0:P], ACT.Copy).then_inc(hT_sb, 1)

            def gelu(tile):
                act.wait_ge(pre_ready, tile.done())
                wait(act, y_ps, tile.done(2))
                nc.scalar.activation(gT[tile.pair][:, :, :], pre[tile.pair][:, :, :], ACT.Gelu_apprx_tanh).then_inc(g_ready, 1)

            act.wait_ge(w_loaded, 16 * WEIGHT_LOADS)
            for p in range(2):
                weights(Tile(0, p))
                turned(Tile(0, p))

            def body(tile):
                gelu(tile)
                if tile.shift(2):
                    weights(tile.shift(2))
                    turned(tile.shift(2))
            all_tiles(act, body)

        @block.vector
        def _(dve):
            dve.wait_ge(w_loaded, 16 * WEIGHT_LOADS)
            dve.wait_ge(b1_ps, 1)
            nc.vector.tensor_copy(biases[:, :, D:BIAS], ps[:, Y_BANK, 0:E * FC].rearrange("p (e c) -> p e c", c=FC)).then_inc(b1_ready, 1)
            dve.wait_ge(b1_ready, 1)
            flat = biases[:, :, :].rearrange("p e n -> p (e n)")

            def rows(tile):
                dve.wait_ge(h_loaded[tile.ring], (tile.turn + 1) * 16)
                dve.wait_ge(stored[tile.ring], tile.turn * 16)
                nc.vector.tensor_copy(dest[tile.ring][:, :], hin[tile.ring][:, D:PAY].bitcast(U32)).then_inc(dest_ready, 1)

            def bias(tile, at):
                dve.wait_ge(up_ps, tile.done())
                wait(dve, g_ready, tile.done(2))
                nc.vector.tensor_tensor(pre[tile.pair][:, :, :], ps[:, UP_BANK + tile.pair, :].rearrange("p (c n) -> p c n", c=FC),
                                        flat[:, bass.ds(at + D, FC)].unsqueeze(2).broadcast_to([P, FC, P]),
                                        ALU.add).then_inc(pre_ready, 1)

            def result(tile, at):
                dve.wait_ge(y_ps, tile.done())
                dve.wait_ge(dest_ready, tile.done())
                nc.vector.tensor_tensor(y[tile.ring][:, :], ps[:, Y_BANK + tile.pair, 0:D], flat[:, bass.ds(at, D)],
                                        ALU.add).then_inc(y_ready, 1)

            def body(tile):
                at = offset(dve, 1, tile, (E - 1) * BIAS)
                rows(tile)
                bias(tile, at)
                before = tile.shift(-1)
                if before:
                    result(before, offset(dve, 1, before, (E - 1) * BIAS))
            all_tiles(dve, body)
            last = Tile(SLOT_TILES // RING - 1, RING - 1)
            result(last, offset(dve, 1, last, (E - 1) * BIAS))

        @block.tensor
        def _(pe):
            pe.wait_ge(w_loaded, 16 * WEIGHT_LOADS)
            pe.wait_ge(consts, 2)
            nc.tensor.transpose(ps[:, Y_BANK, 0:E * FC], b1s[:, :], ident[0:E * FC, 0:E * FC]).then_inc(b1_ps, 1)
            pe.wait_ge(b1_ready, 1)

            def turn(tile):
                pe.wait_ge(h_loaded[tile.ring], (tile.turn + 1) * 16)
                wait(pe, hT_sb, tile.done(2))
                nc.tensor.transpose(ps[:, HT_BANK + tile.pair, 0:P], hin[tile.ring][:, 0:D], ident[:, :]).then_inc(hT_ps, 1)

            def up(tile):
                pe.wait_ge(hT_sb, tile.done())
                pe.wait_ge(w1_ready, tile.done())
                wait(pe, pre_ready, tile.done(2))
                for c in range(FC):
                    ins = nc.tensor.matmul(ps[:, UP_BANK + tile.pair, c * P:(c + 1) * P], w1t[tile.pair][:, c * P:(c + 1) * P],
                                           hT[tile.pair][:, :], start=True, stop=True)
                ins.then_inc(up_ps, 1)

            def down(tile, at):
                pe.wait_ge(g_ready, tile.done())
                wait(pe, y_ready, tile.done(2))
                for c in range(FC):
                    ins = nc.tensor.matmul(ps[:, Y_BANK + tile.pair, 0:D], gT[tile.pair][:, c, :], w2s[:, bass.ds(at + c * D, D)],
                                           start=(c == 0), stop=(c == FC - 1))
                ins.then_inc(y_ps, 1)

            turn(Tile(0, 0))
            turn(Tile(0, 1))
            up(Tile(0, 0))

            def body(tile):
                at = offset(pe, 2, tile, (E - 1) * F)
                if tile.shift(1):
                    up(tile.shift(1))
                if tile.shift(2):
                    turn(tile.shift(2))
                down(tile, at)
            all_tiles(pe, body)
    end_stage(nc, sems)


def last_norms(nc, x1_dram, h_dram, results, gates, g2, b2, out):
    sems = []
    with ExitStack() as ctx:
        def sb(name, shape, dt=F32):
            return ctx.enter_context(nc.sbuf_tensor(name, shape, dt))

        def pair(name, shape, dt=F32):
            return [sb(f"{name}{p}", shape, dt) for p in range(2)]

        def sem(name):
            sems.append(nc.alloc_semaphore(name))
            return sems[-1]
        g2b, b2b = sb("g2b", [P, D]), sb("b2b", [P, D])
        minus_half = sb("minus_half_l", [P, TILES])
        x1, h = pair("x1_l", [P, TILES, D]), pair("h_l", [P, TILES, D])
        ys = pair("ys", [P, TOPK, TILES, D])
        s = [pair(f"s{k}_", [P, TILES, D]) for k in range(TOPK)]
        bst, mv, rs = [[sb(f"{n}{k}_l", sh) for k in range(2)] for n, sh in (("bst", [P, TILES, 6]), ("mv", [P, TILES, 2]), ("rs", [P, TILES]))]
        n1, n2, n3 = sb("n1", [P, TILES, D]), sb("n2", [P, TILES, D]), sb("n3", [P, TILES, D])
        r = sb("r_l", [P, TILES, D])
        o = pair("o_l", [P, TILES, D])
        loaded = [sem(f"last_loaded{p}") for p in range(2)]
        stored = [sem(f"out_stored{p}") for p in range(2)]
        w_loaded, consts = sem("g2_loaded"), sem("last_constants")
        var_ready, rstd_ready, n1_ready, gain_ready = sem("lvar_ready"), sem("lrstd_ready"), sem("ln1_ready"), sem("lgain_ready")
        o_ready, dve_own = sem("o_ready"), sem("dve_own_l")
        pool_passed, dve_passed = sem("pool_passed_l"), sem("dve_passed_l")
        block = ctx.enter_context(nc.Block())

        def by_tile(x):
            return x.rearrange("b (t p) d -> b p t d", p=P)

        @block.sync
        def _(sp):
            sp.dma_start(g2b[:, :], over_partitions(g2)).then_inc(w_loaded, 16)
            sp.dma_start(b2b[:, :], over_partitions(b2)).then_inc(w_loaded, 16)
            res = results.rearrange("(k b t p) d -> k b p t d", k=TOPK, b=BATCH, p=P)
            with sp.Fori(0, BATCH // 2) as it:
                for p in range(2):
                    sp.wait_ge(o_ready, it * 2)
                    b = it * 2 + p
                    sp.dma_start(h[p][:, :, :], by_tile(h_dram)[b]).then_inc(loaded[p], 16)
                    for k in range(TOPK):
                        sp.dma_start(ys[p][:, k, :, :], res[k, b]).then_inc(loaded[p], 16)
                    sp.dma_start(x1[p][:, :, :], by_tile(x1_dram)[b]).then_inc(loaded[p], 16)
                for p in range(2):
                    sp.wait_ge(o_ready, Row(it, p)(1, 1))
                    sp.dma_start(by_tile(out)[it * 2 + p], o[p][:, :, :]).then_inc(stored[p], 16)
            for p in range(2):
                sp.wait_ge(stored[p], 16 * (BATCH // 2))

        @block.gpsimd
        def _(pool):
            nc.gpsimd.memset(minus_half[:, :], -0.5).then_inc(consts, 1)
            pool.wait_ge(consts, 1)
            pool.wait_ge(w_loaded, 32)
            with pool.Fori(0, BATCH // 2) as it:
                for p in range(2):
                    row = Row(it, p)
                    for k in range(2):
                        wait_apart(pool, var_ready, row(2, k + 1), pool_passed)
                        nc.gpsimd.tensor_scalar(rs[k][:, :], mv[k][:, :, 1], EPS, None, ALU.add).then_inc(rstd_ready, 1)
                        pool.wait_ge(rstd_ready, row(4, 2 * k + 1))
                        nc.gpsimd.tensor_tensor(rs[k][:, :], rs[k][:, :], minus_half[:, :], ALU.pow).then_inc(rstd_ready, 1)
                        if k == 0:
                            pool.wait_ge(n1_ready, row(1, 1))
                            nc.gpsimd.tensor_tensor(n2[:, :, :], n1[:, :, :], g2b[:, :].unsqueeze(1).broadcast_to([P, TILES, D]),
                                                    ALU.mult).then_inc(gain_ready, 1)
                            pool.wait_ge(gain_ready, row(2, 1))
                            nc.gpsimd.tensor_tensor(n3[:, :, :], n2[:, :, :], b2b[:, :].unsqueeze(1).broadcast_to([P, TILES, D]),
                                                    ALU.add).then_inc(gain_ready, 1)

        @block.vector
        def _(dve):
            own = Chain(dve, dve_own, 5)
            with dve.Fori(0, BATCH // 2) as it:
                for p in range(2):
                    row = Row(it, p)
                    own.begin(row)
                    dve.wait_ge(loaded[p], it * (16 * (TOPK + 2)) + 16 * (TOPK + 2))
                    src = h[p]
                    for k in range(TOPK):
                        for t in range(TILES):
                            ins = nc.vector.scalar_tensor_tensor(out=s[k][p][:, t, :], in0=ys[p][:, k, t, :],
                                                                 scalar=gates[:, k, bass.ds(it * (2 * TILES) + (p * TILES + t), 1)],
                                                                 in1=src[:, t, :], op0=ALU.mult, op1=ALU.add)
                        own.add(ins)
                        own.wait()
                        src = s[k][p]

                    def moments(x, k):
                        for t in range(TILES):
                            ins = nc.vector.bn_stats(bst[k][:, t, :], x[:, t, :])
                        own.add(ins)
                        own.wait_apart(dve_passed)
                        for t in range(TILES):
                            ins = nc.vector.bn_aggr(mv[k][:, t, :], bst[k][:, t, :])
                        ins.then_inc(var_ready, 1)
                        dve.wait_ge(var_ready, row(2, k + 1))
                        dve.wait_ge(rstd_ready, row(4, 2 * k + 2))
                    moments(src, 0)
                    for t in range(TILES):
                        ins = nc.vector.tensor_scalar(n1[:, t, :], src[:, t, :], mv[0][:, t, 0:1], rs[0][:, t:t + 1],
                                                      ALU.subtract, ALU.mult)
                    ins.then_inc(n1_ready, 1)
                    dve.wait_ge(gain_ready, row(2, 2))
                    own.add(nc.vector.tensor_tensor(r[:, :, :], n3[:, :, :], x1[p][:, :, :], ALU.add))
                    own.wait()
                    moments(r, 1)
                    dve.wait_ge(stored[p], it * 16)
                    for t in range(TILES):
                        ins = nc.vector.tensor_scalar(o[p][:, t, :], r[:, t, :], mv[1][:, t, 0:1], rs[1][:, t:t + 1],
                                                      ALU.subtract, ALU.mult)
                    ins.then_inc(o_ready, 1)
                    own.end()
    end_stage(nc, sems)


def layer(nc, X, W_in, conv_w, conv_b, dt_bias, A_log, Dskip, norm_w, W_out,
          w_qkv, w_o, g1, b1, wg, w1, bb1, w2, bb2, g2, b2, out):
    def dram(name, shape, dt=F32):
        return nc.dram_tensor(name, shape, dt, kind="Internal").ap()

    x1 = dram("x1_rows", (BATCH, SEQ, D))
    q_parts = dram("q_parts", (BATCH, PARTS, D, SEQ), BF16)
    k_parts = dram("k_parts", (BATCH, PARTS, D, SEQ), BF16)
    v = dram("v_rows", (BATCH, SEQ, D))
    h = dram("h_rows", (BATCH, SEQ, D))
    slots = dram("slots", (SLOTS, PAY))
    results = dram("results", (RESULTS, D))

    mamba_layer(nc, X, W_in, conv_w, conv_b, dt_bias, A_log, Dskip, norm_w, W_out, x1)
    qkv_projection(nc, x1, w_qkv, q_parts, k_parts, v)
    attention_layer(nc, x1, q_parts, k_parts, v, w_o, g1, b1, h)
    with nc.sbuf_tensor("gates", [P, TOPK, ALL_TILES], F32) as gates, \
            nc.sbuf_tensor("count", [P, E], F32) as count, \
            nc.sbuf_tensor("table", [1, 3, SLOT_TILES], U32) as table:
        route(nc, h, wg, slots, gates, count)
        plan_tiles(nc, count, table)
        experts(nc, slots, w1, bb1, w2, bb2, table, results)
        last_norms(nc, x1, h, results, gates, g2, b2, out)


INPUTS = ["L0_attn_X", "L0_attn_W_in", "L0_attn_conv_w", "L0_attn_conv_b", "L0_attn_dt_bias", "L0_attn_A_log",
          "L0_attn_D", "L0_attn_norm_w", "L0_attn_W_out", "L0_ffn_w_qkv", "L0_ffn_w_o", "L0_ffn_g1", "L0_ffn_b1",
          "L0_ffn_wg", "L0_ffn_w1", "L0_ffn_bb1", "L0_ffn_w2", "L0_ffn_bb2", "L0_ffn_g2", "L0_ffn_b2"]


def kernel(**inputs):
    import numpy as np
    import concourse.bacc as bacc
    from concourse.bass_utils import run_bass_kernel_spmd

    nc = bacc.Bacc("TRN2", target_bir_lowering=False, num_devices=1)
    arrays, args = {}, []
    for name in INPUTS:
        a = np.ascontiguousarray(inputs[name])
        arrays[f"in_{name}"] = a
        args.append(nc.dram_tensor(f"in_{name}", a.shape, mybir.dt.from_np(a.dtype), kind="ExternalInput").ap())
    out = nc.dram_tensor("out_rows", (BATCH, SEQ, D), F32, kind="ExternalOutput").ap()
    layer(nc, *args, out)
    result = run_bass_kernel_spmd(nc, [arrays], core_ids=[0])
    return result.results[0]["out_rows"]
```

```python
import concourse.bass as bass
from concourse import mybir
from contextlib import ExitStack

F32 = mybir.dt.float32
BF16 = mybir.dt.bfloat16
U32 = mybir.dt.uint32
ALU = mybir.AluOpType
ACT = mybir.ActivationFunctionType
AX = mybir.AxisListType

P = 128
BATCH, SEQ, D = 8, 512, 128
TILES = SEQ // P
EPS = 1e-5

DI, NS, MH, HD, TAPS = 256, 64, 4, 64, 4
CONV = DI + 2 * NS
PROJ = 2 * DI + 2 * NS + MH
CH = CONV // P


class Row:

    def __init__(self, it, p):
        self.it, self.p = it, p

    def __call__(self, per, k):
        return self.it * (2 * per) + (self.p * per + k)


def all_rows(eng, body):
    body(0, 0, True, False)
    with eng.Fori(0, BATCH // 2 - 1) as it:
        body(it, 1, False, False)
        body(it, 2, False, False)
    body(BATCH // 2 - 1, 1, False, True)


def end_stage(nc, sems):
    nc.clear_and_free_semaphores(sems)
    nc.all_engine_barrier()


def wait_apart(eng, sem, value, passed):
    eng.wait_ge(sem, value)
    eng.sem_inc(passed, 1)


class Chain:

    def __init__(self, eng, sem, per):
        self.eng, self.sem, self.per = eng, sem, per

    def begin(self, row):
        self.row, self.n = row, 0

    def add(self, ins):
        self.n += 1
        ins.then_inc(self.sem, 1)

    def wait(self):
        self.eng.wait_ge(self.sem, self.row(self.per, self.n))

    def wait_apart(self, passed):
        wait_apart(self.eng, self.sem, self.row(self.per, self.n), passed)

    def end(self):
        assert self.n == self.per, (self.n, self.per)


def over_partitions(row_ap, n=P):
    return bass.AP(tensor=row_ap.tensor, offset=row_ap.offset, ap=[[0, n]] + [list(x) for x in row_ap.ap])


def mamba_layer(nc, X, W_in, conv_w, conv_b, dt_bias, A_log, Dskip, norm_w, W_out, x1_dram):
    sems = []
    with ExitStack() as ctx:
        def sb(name, shape, dt=F32):
            return ctx.enter_context(nc.sbuf_tensor(name, shape, dt))

        def sem(name):
            sems.append(nc.alloc_semaphore(name))
            return sems[-1]

        win = sb("win", [P, PROJ // P, D])
        win_dt = sb("win_dt", [MH, D])
        winT = sb("winT", [P, PROJ])
        wout = sb("wout", [P, DI])
        woutT = sb("woutT", [P, 2, D])
        cw = sb("cw", [P, CH, TAPS])
        cb = sb("cb", [P, CH])
        nw = sb("nw", [P, 2])
        dtb = sb("dtb", [P, MH])
        a_log = sb("a_log", [P, MH])
        a_neg = sb("a_neg", [P, MH])
        dskip = sb("dskip", [P, MH])
        ident = sb("ident", [P, P])
        ones = sb("ones", [P, P])
        upto = sb("upto", [P, P])
        after = sb("after", [P, P])
        minus_half = sb("minus_half", [P, TILES])
        xin = [sb(f"xin{p}", [P, TILES, D]) for p in range(2)]
        x2 = sb("x2", [P, TILES, D])
        xT = sb("xT", [P, SEQ])
        acc = sb("acc", [P, CH, SEQ])
        xc = [sb(f"xc{p}", [P, 2, SEQ]) for p in range(2)]
        bc = [sb(f"bc{p}", [P, SEQ]) for p in range(2)]
        cz = [sb(f"cz{p}", [P, SEQ]) for p in range(2)]
        zs = [sb(f"zs{p}", [P, TILES, DI]) for p in range(2)]
        btok = sb("btok", [P, TILES, NS])
        u = sb("u", [P, TILES, MH])
        absu = sb("absu", [P, TILES, MH])
        eu = sb("eu", [P, TILES, MH])
        one_e = sb("one_e", [P, TILES, MH])
        lnu = sb("lnu", [P, TILES, MH])
        den = sb("den", [P, TILES, MH])
        dt = sb("dt", [P, TILES, MH])
        a = sb("a", [P, TILES, MH])
        ecs = sb("ecs", [P, TILES, MH])
        etot = sb("etot", [NS, TILES, MH])
        xdt = sb("xdt", [P, TILES, DI])
        dx = sb("dx", [P, TILES, DI])
        ra = [sb(f"ra{k}", [P, MH, P]) for k in range(2)]
        decay = [sb(f"decay{k}", [P, MH, P]) for k in range(2)]
        gm = sb("gm", [P, TILES, P])
        mm = [sb(f"mm{k}", [P, MH, P]) for k in range(2)]
        xw = sb("xw", [P, TILES, DI])
        hs = sb("hs", [P, TILES, DI])
        t1 = sb("t1", [P, TILES, DI])
        y = sb("y", [P, TILES, DI])
        sq = sb("sq", [P, DI])
        ss = sb("ss", [P, TILES])
        rstd = sb("rstd", [P, TILES])
        yT = sb("yT", [P, 2, SEQ])
        r = sb("r", [P, TILES, D])
        bst = sb("bst", [P, TILES, 6])
        mv = sb("mv", [P, TILES, 2])
        rstd2 = sb("rstd2", [P, TILES])
        x1 = [sb(f"x1o{p}", [P, TILES, D]) for p in range(2)]

        ps = ctx.enter_context(nc.psum_tensor("psA", [P, 8, 512], F32))

        def bank(k, n=1):
            return ps[:, k:k + n, :].rearrange("p k n -> p (k n)")

        w_in_sem = sem("weights_loaded")
        consts = sem("constants_made")
        setup_ps = sem("setup_transposed")
        setup_sb = sem("setup_copied")
        x_in = [sem(f"x_loaded{p}") for p in range(2)]
        x1_used = [sem(f"x1_stored{p}") for p in range(2)]
        xT_ps, xT_sb, conv_ps, dt_ps, z_ps = sem("xT_ps"), sem("xT_sb"), sem("conv_ps"), sem("dt_ps"), sem("z_ps")
        tap0, conv_done, silu = sem("tap0"), sem("conv_done"), sem("silu")
        c_moved, u_ready, ln_ready, a_ready = [sem(f"c_moved{p}") for p in range(2)], sem("u_ready"), sem("ln_ready"), sem("a_ready")
        xtr_ps, bctr_ps, btok_ready = sem("xtr_ps"), sem("bctr_ps"), sem("btok_ready")
        xdt_ready, dx_ready = sem("xdt_ready"), sem("dx_ready")
        cs_ps, ecs_ready = sem("cs_ps"), sem("ecs_ready")
        ra_ready, seg_ps, decay_ready, m_ready, xw_ready = sem("ra_ready"), sem("seg_ps"), sem("decay_ready"), sem("m_ready"), sem("xw_ready")
        g_ps, gm_ready, hn_ps, h_ready = sem("g_ps"), sem("gm_ready"), sem("hn_ps"), sem("h_ready")
        intra_ps, inter_ps = sem("intra_ps"), sem("inter_ps")
        y_ready, ss_ready, rstd_ready = sem("y_ready"), sem("ss_ready"), sem("rstd_ready")
        yT_ps, yT_sb, o_ps = sem("yT_ps"), sem("yT_sb"), sem("o_ps")
        x2_ready, r_ready, var_ready, rstd2_ready, x1_ready = sem("x2_ready"), sem("r_ready"), sem("var_ready"), sem("rstd2_ready"), sem("x1_ready")
        front_own, scan_own, tail_own, act_own, pool_own = sem("front_own"), sem("scan_own"), sem("tail_own"), sem("act_own"), sem("pool_own")

        sp_passed, pool_passed, dve_passed = sem("sp_passed_a"), sem("pool_passed_a"), sem("dve_passed_a")
        block = ctx.enter_context(nc.Block())
        x_rows = X.rearrange("b (t p) d -> b p t d", p=P)
        x1_rows = x1_dram.rearrange("b (t p) d -> b p t d", p=P)

        def seg(pe, row, c):
            pe.wait_ge(ra_ready, row(4, c + 1))
            if c >= 2:
                pe.wait_ge(decay_ready, row(4, c - 1))
            nc.tensor.matmul(bank(4 + c % 2), after[:, :], ra[c % 2][:, :, :].rearrange("p h n -> p (h n)"),
                             start=True, stop=True).then_inc(seg_ps, 1)

        def intra(pe, row, c):
            pe.wait_ge(m_ready, row(4, c + 1))
            if c == 0:
                pe.wait_ge(dx_ready, row(1, 1))
            for h in range(MH):
                ins = nc.tensor.matmul(bank(0, 2)[:, c * DI + h * HD:c * DI + (h + 1) * HD], mm[c % 2][:, h, :],
                                       xdt[:, c, h * HD:(h + 1) * HD], start=True, stop=True)
            ins.then_inc(intra_ps, 1)

        @block.sync
        def _(sp):
            sp.dma_start(win[:, :, :], W_in[0:PROJ - MH, :].rearrange("(c p) d -> p c d", p=P)).then_inc(w_in_sem, 16)
            sp.dma_start(win_dt[:, :], W_in[PROJ - MH:PROJ, :]).then_inc(w_in_sem, 16)
            sp.dma_start(wout[:, :], W_out).then_inc(w_in_sem, 16)
            sp.dma_start(nw[:, :], norm_w.rearrange("(k p) -> p k", p=P), allow_slow_non_contiguous=True).then_inc(w_in_sem, 16)
            sp.dma_start(xin[0][:, :, :], x_rows[0]).then_inc(x_in[0], 16)
            sp.dma_start(cw[:, :, :], conv_w.rearrange("(c p) k -> p c k", p=P)).then_inc(w_in_sem, 16)
            sp.dma_start(cb[:, :], conv_b.rearrange("(c p) -> p c", p=P), allow_slow_non_contiguous=True).then_inc(w_in_sem, 16)
            sp.dma_start(dtb[:, :], over_partitions(dt_bias)).then_inc(w_in_sem, 16)
            sp.dma_start(a_log[:, :], over_partitions(A_log)).then_inc(w_in_sem, 16)
            sp.dma_start(dskip[:, :], over_partitions(Dskip)).then_inc(w_in_sem, 16)
            sp.dma_start(xin[1][:, :, :], x_rows[1]).then_inc(x_in[1], 16)

            def move_c(it, p):
                row, q = Row(it, p), p % 2
                wait_apart(sp, silu, row(3, 2), sp_passed)
                if not (isinstance(it, int) and it * 2 + p < 2):
                    sp.wait_ge(inter_ps, Row(it, p - 1)(3, 0))
                    sp.wait_ge(g_ps, Row(it, p - 1)(1, 0))
                sp.dma_start(cz[q][0:NS, :], bc[q][NS:P, :]).then_inc(c_moved[q], 16)
            move_c(0, 0)

            def body(it, p, first, load, last):
                row, before = Row(it, p), Row(it, p - 1)
                if load:
                    sp.wait_ge(xT_ps, row(1, 1))
                    sp.wait_ge(x2_ready, row(1, 1))
                    sp.dma_start(xin[p % 2][:, :, :], x_rows[it * 2 + p + 2]).then_inc(x_in[p % 2], 16)
                if not first:
                    sp.wait_ge(x1_ready, before(1, 1))
                    sp.dma_start(x1_rows[it * 2 + p - 1], x1[(p - 1) % 2][:, :, :]).then_inc(x1_used[(p - 1) % 2], 16)
                if not last:
                    move_c(it, p + 1)
            body(0, 0, True, True, False)
            with sp.Fori(0, BATCH // 2 - 2) as it:
                body(it, 1, False, True, False)
                body(it, 2, False, True, False)
            end = BATCH // 2 - 1
            body(end, -1, False, True, False)
            body(end, 0, False, False, False)
            body(end, 1, False, False, True)
            sp.wait_ge(x1_ready, BATCH)
            sp.dma_start(x1_rows[BATCH - 1], x1[1][:, :, :]).then_inc(x1_used[1], 16)
            for p in range(2):
                sp.wait_ge(x1_used[p], 16 * (BATCH // 2))

        @block.gpsimd
        def _(pool):
            nc.gpsimd.memset(ones[:, :], 1.0).then_inc(consts, 1)
            nc.gpsimd.memset(minus_half[:, :], -0.5).then_inc(consts, 1)
            for p in range(2):
                nc.gpsimd.memset(cz[p][:, :], 0.0).then_inc(consts, 1)
            nc.gpsimd.memset(hs[:, :, :], 0.0).then_inc(consts, 1)
            pool.wait_ge(consts, 5)
            nc.gpsimd.affine_select(out=ident[:, :], in_=ones[:, :], compare_op=ALU.is_equal, fill=0.0, base=0,
                                    pattern=[[-1, P]], channel_multiplier=1).then_inc(consts, 1)
            nc.gpsimd.affine_select(out=upto[:, :], in_=ones[:, :], compare_op=ALU.is_ge, fill=0.0, base=0,
                                    pattern=[[1, P]], channel_multiplier=-1).then_inc(consts, 1)
            nc.gpsimd.affine_select(out=after[:, :], in_=ones[:, :], compare_op=ALU.is_gt, fill=0.0, base=0,
                                    pattern=[[-1, P]], channel_multiplier=1).then_inc(consts, 1)
            own = Chain(pool, pool_own, 2)

            def ra_step(row, c):
                if c == 0:
                    pool.wait_ge(a_ready, row(1, 1))
                used = row(4, c - 1)
                if not (isinstance(used, int) and used <= 0):
                    pool.wait_ge(seg_ps, used)
                nc.gpsimd.tensor_tensor(ra[c % 2][:, :, :], upto[:, :].unsqueeze(1).broadcast_to([P, MH, P]),
                                        a[:, c, :].unsqueeze(2).broadcast_to([P, MH, P]),
                                        ALU.mult).then_inc(ra_ready, 1)

            def xw_step(row, c):
                if c == 0:
                    pool.wait_ge(xdt_ready, row(1, 1))
                    pool.wait_ge(hn_ps, row(3, 0))
                pool.wait_ge(decay_ready, row(4, c + 1))
                nc.gpsimd.tensor_tensor(xw[:, c, :].rearrange("p (h d) -> p h d", h=MH),
                                        xdt[:, c, :].rearrange("p (h d) -> p h d", h=MH),
                                        decay[c % 2][:, :, P - 1:P].broadcast_to([P, MH, HD]),
                                        ALU.mult).then_inc(xw_ready, 1)

            pool.wait_ge(consts, 8)
            for c in range(2):
                ra_step(Row(0, 0), c)

            def rms(row):
                pool.wait_ge(r_ready, row(1, 0))
                wait_apart(pool, ss_ready, row(4, 4), pool_passed)
                own.begin(row)
                own.add(nc.gpsimd.tensor_scalar(rstd[:, :], ss[:, :], 1.0 / DI, EPS, ALU.mult, ALU.add))
                own.wait()
                nc.gpsimd.tensor_tensor(rstd[:, :], rstd[:, :], minus_half[:, :], ALU.pow).then_inc(rstd_ready, 1)

            def norm(row):
                wait_apart(pool, var_ready, row(1, 1), pool_passed)
                own.add(nc.gpsimd.tensor_scalar(rstd2[:, :], mv[:, :, 1], EPS, None, ALU.add))
                own.wait()
                nc.gpsimd.tensor_tensor(rstd2[:, :], rstd2[:, :], minus_half[:, :], ALU.pow).then_inc(rstd2_ready, 1)
                own.end()

            def body(it, p, first, last):
                row, before, next_row = Row(it, p), Row(it, p - 1), Row(it, p + 1)
                if not first:
                    rms(before)
                xw_step(row, 0)
                ra_step(row, 2)
                if not first:
                    norm(before)
                xw_step(row, 1)
                ra_step(row, 3)
                xw_step(row, 2)
                pool.wait_ge(x_in[p % 2], (it + p // 2 + 1) * 16)
                pool.wait_ge(r_ready, row(1, 0))
                nc.gpsimd.tensor_tensor(x2[:, :, :], xin[p % 2][:, :, :], xin[p % 2][:, :, :], ALU.add).then_inc(x2_ready, 1)
                if not last:
                    for c in range(2):
                        ra_step(next_row, c)
            all_rows(pool, body)
            rms(Row(BATCH // 2 - 1, 1))
            norm(Row(BATCH // 2 - 1, 1))

        @block.scalar
        def _(act):
            act.wait_ge(w_in_sem, 16 * 9)
            nc.scalar.activation(a_neg[:, :], a_log[:, :], ACT.Exp).then_inc(setup_sb, 1)

            def xT_copy(row):
                act.wait_ge(xT_ps, row(1, 1))
                act.wait_ge(z_ps, row(1, 0))
                nc.scalar.activation(xT[:, :], bank(6), ACT.Copy).then_inc(xT_sb, 1)

            def newest_tap(row, c):
                act.wait_ge(conv_ps, row(3, c + 1))
                act.wait_ge(silu, row(3, 0))
                nc.scalar.activation(acc[:, c, :], bank(6 + c % 2), ACT.Identity, bias=cb[:, c:c + 1],
                                     scale=cw[:, c, TAPS - 1:TAPS]).then_inc(tap0, 1)

            def softplus_exp(row):
                act.wait_ge(u_ready, row(3, 2))
                nc.scalar.activation(eu[:, :, :], absu[:, :, :], ACT.Exp, scale=-1.0).then_inc(ln_ready, 1)

            def softplus_ln(row):
                act.wait_ge(u_ready, row(3, 3))
                nc.scalar.activation(lnu[:, :, :], one_e[:, :, :], ACT.Ln).then_inc(ln_ready, 1)

            def silus(it, p):
                row, before, q = Row(it, p), Row(it, p - 1), p % 2
                old = not (isinstance(it, int) and it * 2 + p < 2)
                act.wait_ge(conv_done, row(3, 2))
                if old:
                    act.wait_ge(xtr_ps, before(1, 0))
                nc.scalar.activation(xc[q][:, :, :], acc[:, 0:2, :], ACT.Silu).then_inc(silu, 1)
                act.wait_ge(conv_done, row(3, 3))
                if old:
                    act.wait_ge(c_moved[q], (it + p // 2) * 16)
                    act.wait_ge(bctr_ps, before(1, 0))
                    act.wait_ge(g_ps, before(1, 0))
                nc.scalar.activation(bc[q][:, :], acc[:, 2, :], ACT.Silu).then_inc(silu, 1)
                act.wait_ge(z_ps, row(1, 1))
                if old:
                    act.wait_ge(y_ready, before(1, 0))
                nc.scalar.activation(zs[q][:, :, :].rearrange("p t n -> p (t n)"), bank(6, 2), ACT.Silu).then_inc(silu, 1)

            def cumulative(row):
                act.wait_ge(cs_ps, row(1, 1))
                act.wait_ge(y_ready, row(1, 0))
                nc.scalar.activation(ecs[:, :, :].rearrange("p t h -> p (t h)"), bank(3)[:, 16:32], ACT.Exp).then_inc(act_own, 1)
                nc.scalar.activation(etot[:, :, :].rearrange("p t h -> p (t h)"), bank(3)[0:NS, 32:48], ACT.Exp).then_inc(ecs_ready, 1)

            def decays(row, c):
                act.wait_ge(seg_ps, row(4, c + 1))
                used = row(4, c - 1)
                if not (isinstance(used, int) and used <= 0):
                    act.wait_ge(m_ready, used)
                    act.wait_ge(xw_ready, row(3, max(c - 1, 0)))
                nc.scalar.activation(decay[c % 2][:, :, :].rearrange("p h n -> p (h n)"), bank(4 + c % 2),
                                     ACT.Exp).then_inc(decay_ready, 1)

            def b_copy(row):
                act.wait_ge(bctr_ps, row(1, 1))
                act.wait_ge(hn_ps, row(3, 0))
                nc.scalar.activation(btok[:, :, :], bank(2).rearrange("p (t n) -> p t n", t=TILES)[:, :, 0:NS],
                                     ACT.Copy).then_inc(btok_ready, 1)

            def squares(row):
                act.wait_ge(y_ready, row(1, 1))
                act.wait_ge(rstd_ready, row(1, 0))
                for t in range(TILES):
                    if t >= 1:
                        act.wait_ge(ss_ready, row(4, t))
                    nc.scalar.activation(sq[:, :], y[:, t, :], ACT.Square, accum_out=ss[:, t:t + 1]).then_inc(ss_ready, 1)

            def yT_copy(row):
                act.wait_ge(yT_ps, row(1, 1))
                act.wait_ge(o_ps, row(1, 0))
                nc.scalar.activation(yT[:, :, :].rearrange("p k n -> p (k n)"), bank(4, 2), ACT.Copy).then_inc(yT_sb, 1)

            start = Row(0, 0)
            xT_copy(start)
            for c in range(2):
                newest_tap(start, c)
            softplus_exp(start)
            newest_tap(start, 2)
            softplus_ln(start)
            silus(0, 0)

            def body(it, p, first, last):
                row, before, next_row = Row(it, p), Row(it, p - 1), Row(it, p + 1)
                if not first:
                    yT_copy(before)
                cumulative(row)
                if not last:
                    xT_copy(next_row)
                decays(row, 0)
                decays(row, 1)
                b_copy(row)
                if not last:
                    newest_tap(next_row, 0)
                    softplus_exp(next_row)
                decays(row, 2)
                if not last:
                    newest_tap(next_row, 1)
                decays(row, 3)
                if not last:
                    newest_tap(next_row, 2)
                    softplus_ln(next_row)
                if not last:
                    silus(it, p + 1)
                squares(row)
            all_rows(act, body)
            yT_copy(Row(BATCH // 2 - 1, 1))

        @block.vector
        def _(dve):
            dve.wait_ge(setup_ps, 1)
            nc.vector.tensor_copy(winT[:, :], bank(0, 2)[:, 0:PROJ]).then_inc(setup_sb, 1)
            dve.wait_ge(w_in_sem, 16 * 9)
            for k in range(2):
                nc.vector.tensor_scalar(woutT[:, k, :], bank(2)[:, k * P:(k + 1) * P], nw[:, k:k + 1], None,
                                        ALU.mult).then_inc(setup_sb, 1)
            dve.wait_ge(setup_sb, 4)
            nc.vector.tensor_scalar(a_neg[:, :], a_neg[:, :], -1.0, None, ALU.mult).then_inc(setup_sb, 1)
            dve.wait_ge(setup_sb, 5)
            front, scan, tail = Chain(dve, front_own, 13), Chain(dve, scan_own, 5), Chain(dve, tail_own, 4)

            def steps_u(row):
                front.begin(row)
                dve.wait_ge(dt_ps, row(1, 1))
                dve.wait_ge(a_ready, row(1, 0))
                nc.vector.tensor_tensor(u[:, :, :], bank(7)[:, 0:16].rearrange("p (t h) -> p t h", t=TILES),
                                        dtb[:, :].unsqueeze(1).broadcast_to([P, TILES, MH]), ALU.add).then_inc(u_ready, 1)
                dve.wait_ge(u_ready, row(3, 1))
                nc.vector.scalar_tensor_tensor(out=absu[:, :, :], in0=u[:, :, :], scalar=-1.0, in1=u[:, :, :],
                                               op0=ALU.mult, op1=ALU.max).then_inc(u_ready, 1)

            def taps(row, c):
                dve.wait_ge(tap0, row(3, c + 1))
                for k in range(TAPS - 1):
                    s = TAPS - 1 - k
                    if k:
                        front.wait()
                    ins = nc.vector.scalar_tensor_tensor(out=acc[:, c, s:SEQ], in0=bank(6 + c % 2)[:, 0:SEQ - s],
                                                         scalar=cw[:, c, k:k + 1], in1=acc[:, c, s:SEQ],
                                                         op0=ALU.mult, op1=ALU.add)
                    if k < TAPS - 2:
                        front.add(ins)
                    else:
                        ins.then_inc(conv_done, 1)

            def steps_e(row):
                dve.wait_ge(ln_ready, row(2, 1))
                nc.vector.tensor_scalar(one_e[:, :, :], eu[:, :, :], 1.0, None, ALU.add).then_inc(u_ready, 1)

            def steps_dt(row):
                dve.wait_ge(u_ready, row(3, 3))
                front.add(nc.vector.tensor_scalar(den[:, :, :], one_e[:, :, :], -1.0, 1e-30, ALU.add, ALU.max))
                front.wait()
                front.add(nc.vector.reciprocal(den[:, :, :], den[:, :, :]))
                front.wait()
                dve.wait_ge(ln_ready, row(2, 2))
                front.add(nc.vector.tensor_tensor(lnu[:, :, :], lnu[:, :, :], den[:, :, :], ALU.mult))
                front.wait()
                front.add(nc.vector.tensor_scalar(den[:, :, :], one_e[:, :, :], 1.0, None, ALU.is_equal))
                front.wait()
                front.add(nc.vector.tensor_tensor(lnu[:, :, :], lnu[:, :, :], den[:, :, :], ALU.add))
                front.wait()
                front.add(nc.vector.tensor_tensor(lnu[:, :, :], lnu[:, :, :], eu[:, :, :], ALU.mult))
                front.wait()
                dve.wait_ge(xdt_ready, row(1, 0))
                dve.wait_ge(ra_ready, row(4, 0))
                dve.wait_ge(cs_ps, row(1, 0))
                front.add(nc.vector.scalar_tensor_tensor(out=dt[:, :, :], in0=u[:, :, :], scalar=0.0, in1=lnu[:, :, :],
                                                         op0=ALU.max, op1=ALU.add))
                front.wait()
                nc.vector.scalar_tensor_tensor(out=a[:, :, :], in0=dt[:, :, :], scalar=1.0,
                                               in1=a_neg[:, :].unsqueeze(1).broadcast_to([P, TILES, MH]),
                                               op0=ALU.mult, op1=ALU.mult).then_inc(a_ready, 1)
                front.end()

            def x_by_token(row):
                dve.wait_ge(xtr_ps, row(1, 1))
                xtok = bank(0, 2).rearrange("p (t h d) -> p t h d", t=TILES, h=MH)
                dve.wait_ge(a_ready, row(1, 1))
                dve.wait_ge(intra_ps, row(4, 0))
                dve.wait_ge(xw_ready, row(3, 0))
                nc.vector.tensor_tensor(xdt[:, :, :].rearrange("p t (h d) -> p (t h) d", h=MH),
                                        bank(0, 2).rearrange("p (g d) -> p g d", d=HD),
                                        dt[:, :, :].rearrange("p t h -> p (t h)").unsqueeze(2).broadcast_to([P, TILES * MH, HD]),
                                        ALU.mult).then_inc(xdt_ready, 1)
                dve.wait_ge(y_ready, row(1, 0))
                nc.vector.tensor_tensor(dx[:, :, :].rearrange("p t (h d) -> p t h d", h=MH), xtok,
                                        dskip[:, :].unsqueeze(1).unsqueeze(3).broadcast_to([P, TILES, MH, HD]),
                                        ALU.mult).then_inc(dx_ready, 1)

            def masked_g(row):
                dve.wait_ge(g_ps, row(1, 1))
                dve.wait_ge(m_ready, row(4, 0))
                nc.vector.tensor_tensor(gm[:, :, :], bank(3).rearrange("p (t n) -> p t n", t=TILES),
                                        upto[:, :].unsqueeze(1).broadcast_to([P, TILES, P]), ALU.mult).then_inc(gm_ready, 1)

            def masked(row, c):
                dve.wait_ge(gm_ready, row(1, 1))
                dve.wait_ge(decay_ready, row(4, c + 1))
                used = row(4, c - 1)
                if not (isinstance(used, int) and used <= 0):
                    dve.wait_ge(intra_ps, used)
                nc.vector.tensor_tensor(mm[c % 2][:, :, :], decay[c % 2][:, :, :],
                                        gm[:, c, :].unsqueeze(1).broadcast_to([P, MH, P]), ALU.mult).then_inc(m_ready, 1)

            def states(row):
                scan.begin(row)
                dve.wait_ge(hn_ps, row(3, 3))
                dve.wait_ge(ecs_ready, row(1, 1))
                dve.wait_ge(act_own, row(1, 1))
                dve.wait_ge(inter_ps, row(3, 0))
                nc.vector.tensor_copy(hs[0:NS, 1, :], bank(2)[0:NS, 0:DI]).then_inc(h_ready, 1)
                for c in range(1, TILES - 1):
                    dve.wait_ge(h_ready, row(3, c))
                    scan.add(nc.vector.tensor_tensor(hs[0:NS, c + 1, :].rearrange("p (h d) -> p h d", h=MH),
                                                     hs[0:NS, c, :].rearrange("p (h d) -> p h d", h=MH),
                                                     etot[:, c, :].unsqueeze(2).broadcast_to([NS, MH, HD]), ALU.mult))
                    scan.wait()
                    src = bank(2)[0:NS, DI:2 * DI] if c == 1 else bank(3)[0:NS, 0:DI]
                    nc.vector.tensor_tensor(hs[0:NS, c + 1, :], hs[0:NS, c + 1, :], src, ALU.add).then_inc(h_ready, 1)

            def y_steps(row, p):
                dve.wait_ge(intra_ps, row(4, 4))
                dve.wait_ge(ss_ready, row(4, 0))
                dve.wait_ge(yT_ps, row(1, 0))
                scan.add(nc.vector.tensor_tensor(y[:, :, :].rearrange("p t n -> p (t n)"), bank(0, 2),
                                                 dx[:, :, :].rearrange("p t n -> p (t n)"), ALU.add))
                dve.wait_ge(inter_ps, row(3, 3))
                scan.add(nc.vector.tensor_tensor(t1[:, 1:TILES, :].rearrange("p t (h d) -> p (t h) d", h=MH),
                                                 bank(4, 2)[:, DI:TILES * DI].rearrange("p (g d) -> p g d", d=HD),
                                                 ecs[:, 1:TILES, :].rearrange("p t h -> p (t h)").unsqueeze(2).broadcast_to([P, 3 * MH, HD]),
                                                 ALU.mult))
                scan.wait()
                scan.add(nc.vector.tensor_tensor(y[:, 1:TILES, :], y[:, 1:TILES, :], t1[:, 1:TILES, :], ALU.add))
                scan.wait()
                dve.wait_ge(silu, row(3, 3))
                nc.vector.tensor_tensor(y[:, :, :], y[:, :, :], zs[p % 2][:, :, :], ALU.mult).then_inc(y_ready, 1)
                scan.end()

            def residual(row):
                tail.begin(row)
                dve.wait_ge(o_ps, row(1, 1))
                dve.wait_ge(rstd_ready, row(1, 1))
                dve.wait_ge(x2_ready, row(1, 1))
                dve.wait_ge(x1_ready, row(1, 0))
                for t in range(TILES):
                    ins = nc.vector.scalar_tensor_tensor(out=r[:, t, :], in0=bank(2)[:, t * P:(t + 1) * P],
                                                         scalar=rstd[:, t:t + 1], in1=x2[:, t, :],
                                                         op0=ALU.mult, op1=ALU.add)
                    if t == TILES - 1:
                        ins.then_inc(r_ready, 1)
                    else:
                        tail.add(ins)
                tail.wait()
                dve.wait_ge(r_ready, row(1, 1))
                for t in range(TILES):
                    ins = nc.vector.bn_stats(bst[:, t, :], r[:, t, :])
                tail.add(ins)
                dve.wait_ge(rstd2_ready, row(1, 0))
                tail.wait_apart(dve_passed)
                for t in range(TILES):
                    ins = nc.vector.bn_aggr(mv[:, t, :], bst[:, t, :])
                ins.then_inc(var_ready, 1)
                tail.end()

            def normalise(row, it, p):
                dve.wait_ge(var_ready, row(1, 1))
                dve.wait_ge(rstd2_ready, row(1, 1))
                dve.wait_ge(x1_used[p % 2], (it + p // 2) * 16)
                for t in range(TILES):
                    ins = nc.vector.tensor_scalar(x1[p % 2][:, t, :], r[:, t, :], mv[:, t, 0:1], rstd2[:, t:t + 1],
                                                  ALU.subtract, ALU.mult)
                ins.then_inc(x1_ready, 1)

            start = Row(0, 0)
            steps_u(start)
            taps(start, 0)
            steps_e(start)
            taps(start, 1)
            taps(start, 2)
            steps_dt(start)

            def body(it, p, first, last):
                row, before, next_row = Row(it, p), Row(it, p - 1), Row(it, p + 1)
                x_by_token(row)
                if not first:
                    residual(before)
                masked_g(row)
                masked(row, 0)
                if not last:
                    steps_u(next_row)
                masked(row, 1)
                if not first:
                    normalise(before, it, p - 1)
                if not last:
                    taps(next_row, 0)
                    steps_e(next_row)
                masked(row, 2)
                if not last:
                    taps(next_row, 1)
                masked(row, 3)
                states(row)
                if not last:
                    taps(next_row, 2)
                if not last:
                    steps_dt(next_row)
                y_steps(row, p)
            all_rows(dve, body)
            end = Row(BATCH // 2 - 1, 1)
            residual(end)
            normalise(end, BATCH // 2 - 1, 1)

        @block.tensor
        def _(pe):
            pe.wait_ge(w_in_sem, 16 * 9)
            pe.wait_ge(consts, 8)
            for c in range(PROJ // P):
                nc.tensor.transpose(bank(0, 2)[:, c * P:(c + 1) * P], win[:, c, :], ident[:, :])
            nc.tensor.transpose(bank(1)[:, P:P + MH], win_dt[:, :], ident[0:MH, 0:MH])
            for k in range(2):
                ins = nc.tensor.transpose(bank(2)[:, k * P:(k + 1) * P], wout[:, k * P:(k + 1) * P], ident[:, :])
            ins.then_inc(setup_ps, 1)

            def turn_x(it, p):
                row = Row(it, p)
                pe.wait_ge(x_in[p % 2], (it + p // 2 + 1) * 16)
                pe.wait_ge(silu, row(3, 0))
                for t in range(TILES):
                    ins = nc.tensor.transpose(bank(6)[:, t * P:(t + 1) * P], xin[p % 2][:, t, :], ident[:, :])
                ins.then_inc(xT_ps, 1)

            def conv(row, c):
                if c == 1:
                    pe.wait_ge(u_ready, row(3, 1))
                if c == 2:
                    pe.wait_ge(conv_done, row(3, 1))
                nc.tensor.matmul(bank(6 + c % 2), winT[:, DI + c * P:DI + (c + 1) * P], xT[:, :],
                                 start=True, stop=True).then_inc(conv_ps, 1)

            def project_dt(row):
                pe.wait_ge(xT_sb, row(1, 1))
                for t in range(TILES):
                    ins = nc.tensor.matmul(bank(7)[:, t * MH:(t + 1) * MH], xT[:, t * P:(t + 1) * P],
                                           winT[:, PROJ - MH:PROJ], start=True, stop=True)
                ins.then_inc(dt_ps, 1)

            def project_z(row):
                pe.wait_ge(conv_done, row(3, 3))
                for t in range(TILES):
                    ins = nc.tensor.matmul(bank(6, 2)[:, t * DI:(t + 1) * DI], xT[:, t * P:(t + 1) * P],
                                           winT[:, 0:DI], start=True, stop=True)
                ins.then_inc(z_ps, 1)

            def turn_xc(row, p):
                pe.wait_ge(silu, row(3, 1))
                pe.wait_ge(y_ready, row(1, 0))
                for t in range(TILES):
                    for k in range(2):
                        ins = nc.tensor.transpose(bank(0, 2)[:, t * DI + k * P:t * DI + (k + 1) * P],
                                                  xc[p % 2][:, k, t * P:(t + 1) * P], ident[:, :])
                ins.then_inc(xtr_ps, 1)

            def sums(row):
                pe.wait_ge(a_ready, row(1, 1))
                pe.wait_ge(h_ready, row(3, 0))
                nc.tensor.matmul(bank(3)[:, 16:32], upto[:, :], a[:, :, :].rearrange("p t h -> p (t h)"),
                                 start=True, stop=True)
                nc.tensor.matmul(bank(3)[0:NS, 32:48], ones[:, 0:NS], a[:, :, :].rearrange("p t h -> p (t h)"),
                                 start=True, stop=True).then_inc(cs_ps, 1)

            def c_by_b(row, it, p):
                q = p % 2
                pe.wait_ge(silu, row(3, 2))
                pe.wait_ge(c_moved[q], (it + p // 2 + 1) * 16)
                pe.wait_ge(ecs_ready, row(1, 1))
                for t in range(TILES):
                    ins = nc.tensor.matmul(bank(3)[:, t * P:(t + 1) * P], bc[q][:, t * P:(t + 1) * P],
                                           cz[q][:, t * P:(t + 1) * P], start=True, stop=True)
                ins.then_inc(g_ps, 1)

            def turn_bc(row, p):
                pe.wait_ge(r_ready, row(1, 0))
                for t in range(TILES):
                    ins = nc.tensor.transpose(bank(2)[:, t * P:(t + 1) * P], bc[p % 2][:, t * P:(t + 1) * P], ident[:, :])
                ins.then_inc(bctr_ps, 1)

            def state(row, c):
                pe.wait_ge(btok_ready, row(1, 1))
                pe.wait_ge(xw_ready, row(3, c + 1))
                if c == 2:
                    pe.wait_ge(gm_ready, row(1, 1))
                out = bank(2)[0:NS, c * DI:(c + 1) * DI] if c < 2 else bank(3)[0:NS, 0:DI]
                nc.tensor.matmul(out, btok[:, c, :], xw[:, c, :], start=True, stop=True).then_inc(hn_ps, 1)

            def from_states(row, p):
                pe.wait_ge(decay_ready, row(4, 4))
                for c in range(1, TILES):
                    pe.wait_ge(h_ready, row(3, c))
                    nc.tensor.matmul(bank(4, 2)[:, c * DI:(c + 1) * DI], cz[p % 2][:, c * P:(c + 1) * P], hs[:, c, :],
                                     start=True, stop=True).then_inc(inter_ps, 1)

            def turn_y(row):
                pe.wait_ge(y_ready, row(1, 1))
                for t in range(TILES):
                    for k in range(2):
                        ins = nc.tensor.transpose(bank(4 + k)[:, t * P:(t + 1) * P], y[:, t, k * P:(k + 1) * P], ident[:, :])
                ins.then_inc(yT_ps, 1)

            def out_projection(row):
                pe.wait_ge(yT_sb, row(1, 1))
                for t in range(TILES):
                    for k in range(2):
                        ins = nc.tensor.matmul(bank(2)[:, t * P:(t + 1) * P], yT[:, k, t * P:(t + 1) * P],
                                               woutT[:, k, :], start=(k == 0), stop=(k == 1))
                ins.then_inc(o_ps, 1)

            turn_x(0, 0)
            pe.wait_ge(setup_sb, 5)
            start = Row(0, 0)
            project_dt(start)
            for c in range(CH):
                conv(start, c)
            project_z(start)

            def body(it, p, first, last):
                row, before, next_row = Row(it, p), Row(it, p - 1), Row(it, p + 1)
                sums(row)
                turn_xc(row, p)
                if not first:
                    turn_y(before)
                if not last:
                    turn_x(it, p + 1)
                if not first:
                    out_projection(before)
                seg(pe, row, 0)
                seg(pe, row, 1)
                c_by_b(row, it, p)
                turn_bc(row, p)
                if not last:
                    project_dt(next_row)
                    conv(next_row, 0)
                state(row, 0)
                seg(pe, row, 2)
                intra(pe, row, 0)
                if not last:
                    conv(next_row, 1)
                state(row, 1)
                seg(pe, row, 3)
                intra(pe, row, 1)
                if not last:
                    conv(next_row, 2)
                state(row, 2)
                intra(pe, row, 2)
                intra(pe, row, 3)
                from_states(row, p)
                if not last:
                    project_z(next_row)
            all_rows(pe, body)
            turn_y(Row(BATCH // 2 - 1, 1))
            out_projection(Row(BATCH // 2 - 1, 1))
    end_stage(nc, sems)


AH, DH = 16, 8
PARTS = 3
QK_ROWS = PARTS * PARTS * DH
MAX_ROWS = QK_ROWS + PARTS
GROUPS = AH // 4
VW = 32


def qkv_projection(nc, x1_dram, w_qkv, q_parts, k_parts, v_dram):
    sems = []
    with ExitStack() as ctx:
        def sb(name, shape, dt=F32):
            return ctx.enter_context(nc.sbuf_tensor(name, shape, dt))

        def pair(name, shape, dt=F32):
            return [sb(f"{name}{p}", shape, dt) for p in range(2)]

        def sem(name):
            sems.append(nc.alloc_semaphore(name))
            return sems[-1]

        wqkv = sb("wqkv", [P, 3 * D])
        wqk = sb("wqk", [P, 2, DH, AH])
        ones = sb("ones_b", [P, P])
        ident = sb("ident_b", [P, P])
        x1 = pair("x1_b", [P, TILES, D])
        xT = pair("xT_b", [P, SEQ])
        part = {n: pair(f"{n}part", [P, PARTS, SEQ], BF16) for n in "qk"}
        rest = {n: pair(f"{n}rest", [P, SEQ]) for n in "qk"}
        v = pair("v_b", [P, TILES, D])
        ps = ctx.enter_context(nc.psum_tensor("psB0", [P, 8, 512], F32))
        w_loaded, consts, w_ordered = sem("wqkv_loaded"), sem("qkv_constants"), sem("wqk_ordered")
        x_loaded = [sem(f"x1_loaded{p}") for p in range(2)]
        stored = [sem(f"qkv_stored{p}") for p in range(2)]
        xT_ps, xT_sb = sem("x1T_ps"), sem("x1T_sb")
        proj_ps = sem("proj_ps")
        first_part, rest_ready, third_part, second_part = sem("first_part"), sem("rest_ready"), sem("third_part"), sem("second_part")
        v_sb = sem("v_sb")
        block = ctx.enter_context(nc.Block())
        x1_rows = x1_dram.rearrange("b (t p) d -> b p t d", p=P)
        v_rows = v_dram.rearrange("b (t p) d -> b p t d", p=P)
        SCALE = {"q": DH ** -0.5, "k": 1.0}

        @block.sync
        def _(sp):
            def load(it, p):
                sp.dma_start(x1[p % 2][:, :, :], x1_rows[it * 2 + p]).then_inc(x_loaded[p % 2], 16)

            def store(it, p):
                row = Row(it, p)
                for n, (name, dst) in enumerate((("q", q_parts), ("k", k_parts))):
                    sp.wait_ge(third_part, row(2, n + 1))
                    sp.dma_start(dst[it * 2 + p].rearrange("s c n -> c s n"), part[name][p][:, :, :]).then_inc(stored[p], 16)
                sp.wait_ge(v_sb, row(1, 1))
                sp.dma_start(v_rows[it * 2 + p], v[p][:, :, :]).then_inc(stored[p], 16)

            sp.dma_start(wqkv[:, :], w_qkv).then_inc(w_loaded, 16)
            load(0, 0)
            load(0, 1)
            with sp.Fori(0, BATCH // 2 - 1) as it:
                for p in range(2):
                    sp.wait_ge(xT_ps, Row(it, p)(1, 1))
                    load(it, p + 2)
                    store(it, p)
            for p in range(2):
                store(BATCH // 2 - 1, p)
            for p in range(2):
                sp.wait_ge(stored[p], 48 * (BATCH // 2))

        @block.gpsimd
        def _(pool):
            nc.gpsimd.memset(ones[:, :], 1.0).then_inc(consts, 1)
            pool.wait_ge(consts, 1)
            nc.gpsimd.affine_select(out=ident[:, :], in_=ones[:, :], compare_op=ALU.is_equal, fill=0.0, base=0,
                                    pattern=[[-1, P]], channel_multiplier=1).then_inc(consts, 1)

        @block.scalar
        def _(act):
            def xT_copy(it, p):
                q = p % 2
                act.wait_ge(xT_ps, Row(it, p)(1, 1))
                if not (isinstance(it, int) and it * 2 + p < 2):
                    act.wait_ge(proj_ps, Row(it, p - 2)(3, 3))
                nc.scalar.activation(xT[q][:, :], ps[:, 4 * q, :], ACT.Copy).then_inc(xT_sb, 1)

            def body(it, p, first, last):
                row, q = Row(it, p), p % 2
                if not last:
                    xT_copy(it, p + 1)
                act.wait_ge(stored[q], (it + p // 2) * 48)
                for n, name in enumerate("qk"):
                    act.wait_ge(proj_ps, row(3, n + 1))
                    nc.scalar.activation(part[name][q][:, 0, :], ps[:, 4 * q + 1 + n, :], ACT.Copy,
                                         scale=SCALE[name]).then_inc(first_part, 1)
                act.wait_ge(proj_ps, row(3, 3))
                nc.scalar.activation(v[q][:, :, :].rearrange("p t n -> p (t n)"), ps[:, 4 * q + 3, :], ACT.Copy).then_inc(v_sb, 1)
                for n, name in enumerate("qk"):
                    act.wait_ge(rest_ready, row(2, n + 1))
                    nc.scalar.activation(part[name][q][:, 1, :], rest[name][q][:, :], ACT.Copy).then_inc(second_part, 1)
            xT_copy(0, 0)
            all_rows(act, body)

        @block.vector
        def _(dve):
            dve.wait_ge(w_loaded, 16)
            for n in range(2):
                nc.vector.tensor_copy(wqk[:, n, :, :], wqkv[:, n * D:(n + 1) * D].rearrange("p (h d) -> p d h", d=DH)).then_inc(w_ordered, 1)
            with dve.Fori(0, BATCH // 2) as it:
                for p in range(2):
                    row = Row(it, p)
                    dve.wait_ge(third_part, it * 4)
                    for n, name in enumerate("qk"):
                        dve.wait_ge(first_part, row(2, n + 1))
                        nc.vector.scalar_tensor_tensor(out=rest[name][p][:, :], in0=ps[:, 4 * p + 1 + n, :], scalar=SCALE[name],
                                                       in1=part[name][p][:, 0, :], op0=ALU.mult, op1=ALU.subtract).then_inc(rest_ready, 1)
                    for n, name in enumerate("qk"):
                        dve.wait_ge(second_part, row(2, n + 1))
                        nc.vector.tensor_tensor(part[name][p][:, 2, :], rest[name][p][:, :], part[name][p][:, 1, :],
                                                ALU.subtract).then_inc(third_part, 1)

        @block.tensor
        def _(pe):
            pe.wait_ge(w_loaded, 16)
            pe.wait_ge(consts, 2)
            pe.wait_ge(w_ordered, 2)
            def turn(it, p):
                q = p % 2
                pe.wait_ge(x_loaded[q], (it + p // 2 + 1) * 16)
                if not (isinstance(it, int) and it * 2 + p < 2):
                    pe.wait_ge(xT_sb, Row(it, p - 2)(1, 1))
                for t in range(TILES):
                    ins = nc.tensor.transpose(ps[:, 4 * q, t * P:(t + 1) * P], x1[q][:, t, :], ident[:, :])
                ins.then_inc(xT_ps, 1)

            def body(it, p, first, last):
                row, q = Row(it, p), p % 2
                if not last:
                    turn(it, p + 1)
                pe.wait_ge(xT_sb, row(1, 1))
                if not (isinstance(it, int) and it * 2 + p < 2):
                    pe.wait_ge(rest_ready, Row(it, p - 2)(2, 2))
                    pe.wait_ge(v_sb, Row(it, p - 2)(1, 1))
                for n in range(2):
                    nc.tensor.matmul(ps[:, 4 * q + 1 + n, :], wqk[:, n, :, :].rearrange("p d h -> p (d h)"), xT[q][:, :],
                                     start=True, stop=True).then_inc(proj_ps, 1)
                for t in range(TILES):
                    ins = nc.tensor.matmul(ps[:, 4 * q + 3, t * P:(t + 1) * P], xT[q][:, t * P:(t + 1) * P],
                                           wqkv[:, 2 * D:3 * D], start=True, stop=True)
                ins.then_inc(proj_ps, 1)
            turn(0, 0)
            all_rows(pe, body)
    end_stage(nc, sems)


MAX_UNITS = [(qt, 4 * g + h, n) for g in range(GROUPS) for qt, n in ((0, 4), (1, 2), (2, 1), (3, 1)) for h in range(0, 4, n)]
EXP_UNITS = [(g, kt, h, n) for g in range(GROUPS) for kt, n in ((0, 2), (1, 2), (2, 4), (3, 4)) for h in range(0, 4, n)]
NMAX, NEXP, STEPS = len(MAX_UNITS), len(EXP_UNITS), GROUPS * TILES


LAG = 2
PBUF = 4
MAX_SHARE = [4] * 5 + [3] * 8 + [0] * 3


def schedule():
    extra = {2: [("last heads", GROUPS - 1), ("spread v", 0)], 3: [("last out", 0)], 4: [("last norm", 0)],
             5: [("last normalise", 0)], 6: [("heads", 0), ("last gain", 0)], 10: [("heads", 1)],
             12: [("max rows", 0)], 14: [("heads", 2)]}
    out, done = [], 0
    for step in range(STEPS):
        units = [u for u, (g, k, _, _) in enumerate(EXP_UNITS) if (g, k) == divmod(step, TILES)]
        n = MAX_SHARE[step]
        for i, u in enumerate(units):
            out.append(("exp", u))
            m = n // len(units) + (i < n % len(units))
            out += [("max", done + j) for j in range(m)]
            done += m
        out.append(("pv", step - LAG) if step >= LAG else ("last pv", STEPS - LAG + step))
        if step % TILES == TILES - 1:
            out.append(("group", step // TILES))
        out += extra.get(step, [])
    assert done == NMAX
    return out


SCHEDULE = schedule()


def repeated(ap, n):
    return bass.AP(tensor=ap.tensor, offset=ap.offset, ap=[[0, n]] + [list(x) for x in ap.ap])


def attention_layer(nc, x1_dram, q_parts, k_parts, v_dram, w_o, g1, b1, h_dram):
    sems = []
    with ExitStack() as ctx:
        def sb(name, shape, dt=F32):
            return ctx.enter_context(nc.sbuf_tensor(name, shape, dt))

        def pair(name, shape, dt=F32):
            return [sb(f"{name}{p}", shape, dt) for p in range(2)]

        def sem(name):
            sems.append(nc.alloc_semaphore(name))
            return sems[-1]

        wo = sb("wo", [P, D])
        g1b = sb("g1b", [P, D])
        b1b = sb("b1b", [P, D])
        ones = sb("ones_c", [P, P])
        ident = sb("ident_c", [P, P])
        ident16 = sb("ident16", [P, P], BF16)
        hide = sb("hide", [P, P], BF16)
        minus_half = sb("minus_half_c", [P, TILES])
        qx = pair("qx", [96, AH, SEQ], BF16)
        kx = pair("kx", [96, AH, SEQ], BF16)
        kones = sb("kones", [PARTS, SEQ], BF16)
        vtok = pair("vtok", [P, TILES, D])
        vx = pair("vx", [P, TILES, AH, VW])
        mx = sb("mx", [P, AH, TILES])
        mparts = sb("mparts", [AH * TILES, PARTS, P], BF16)
        mrest = sb("mrest", [TILES * AH, P])
        pb = [sb(f"pb{k}", [P, 4, SEQ]) for k in range(PBUF)]
        oT = sb("oT", [P, SEQ])
        rc = sb("rc", [P, TILES, 4, 1])
        otok = sb("otok", [P, TILES, D])
        oT2 = sb("oT2", [P, SEQ])
        x1r = sb("x1r", [P, TILES, D])
        r = sb("r_c", [P, TILES, D])
        bst = sb("bst_c", [P, TILES, 6])
        mv = sb("mv_c", [P, TILES, 2])
        rstd = sb("rstd_c", [P, TILES])
        nrm = sb("nrm", [P, TILES, D])
        h1 = sb("h1", [P, TILES, D])
        h = sb("h_c", [P, TILES, D])

        ps = ctx.enter_context(nc.psum_tensor("psB", [P, 8, 512], F32))
        S_BANK, E_BANK, PV_BANK, MISC = 0, 2, 6, 7

        w_loaded, consts, vx_made = sem("wo_loaded"), sem("att_constants"), sem("vx_made")
        kones_made, kones_loaded = sem("kones_made"), sem("kones_loaded")
        qk_loaded, v_loaded, vx_ready = [[sem(f"qk_loaded{p}_{g}") for g in range(GROUPS)] for p in range(2)], [sem(f"v_loaded{p}") for p in range(2)], sem("vx_ready")
        s_ps, mx_ready = sem("s_ps"), sem("mx_ready")
        mxT_ps, mpart_ready, mrows = sem("mxT_ps"), sem("mpart_ready"), [sem(f"mrows{p}") for p in range(2)]
        e_ps, exp_ready, masked, pv_ps = sem("e_ps"), sem("exp_ready"), sem("masked"), sem("pv_ps")
        oT_sb, oTt_ps, otok_ready = sem("oT_sb"), sem("oTt_ps"), sem("otok_ready")
        oT2_ps, oT2_sb, o_ps, x1r_loaded = sem("oT2_ps"), sem("oT2_sb"), sem("att_o_ps"), sem("x1r_loaded")
        r_ready, var_ready, rstd_ready, nrm_ready = sem("att_r"), sem("att_var"), sem("att_rstd"), sem("att_nrm")
        gain_done, h_ready, h_stored = sem("gain_done"), sem("att_h_ready"), sem("h_stored")
        dve_own = sem("dve_own_c")

        pool_passed, dve_passed, pe_passed = sem("pool_passed_c"), sem("dve_passed_c"), sem("pe_passed_c")
        block = ctx.enter_context(nc.Block())
        x1_rows = x1_dram.rearrange("b (t p) d -> b p t d", p=P)
        h_rows = h_dram.rearrange("b (t p) d -> b p t d", p=P)
        v_rows = v_dram.rearrange("b (t p) d -> b p t d", p=P)

        def times(it, p):
            return it + p // 2 + 1

        QK_LOADS = 2 * PARTS * 16

        def load_group(sp, it, p, g):
            q, src, heads = p % 2, it * 2 + p, slice(4 * g, 4 * g + 4)
            for s in range(PARTS):
                at = s * PARTS * DH
                sp.dma_start(qx[q][at:at + PARTS * DH, heads, :],
                             q_parts[src].rearrange("j (d h) n -> (j d) h n", d=DH)[:, heads, :]).then_inc(qk_loaded[q][g], 16)
                k = k_parts[src, s].rearrange("(d h) n -> d h n", d=DH)[:, heads, :]
                sp.dma_start(kx[q][at:at + PARTS * DH, heads, :], repeated(k, PARTS)).then_inc(qk_loaded[q][g], 16)

        def load_v(sp, it, p):
            sp.dma_start(vtok[p % 2][:, :, :], v_rows[it * 2 + p]).then_inc(v_loaded[p % 2], 16)

        def store_max(sp, it, p):
            row, q = Row(it, p), p % 2
            sp.wait_ge(mpart_ready, row(4, 4))
            for s in range(PARTS):
                sp.dma_start(qx[q][QK_ROWS + s:QK_ROWS + s + 1, :, :].rearrange("p h (t n) -> p (h t) n", n=P),
                             mparts[:, s, :]).then_inc(mrows[q], 16)

        @block.sync
        def _(sp):
            for g in range(GROUPS):
                load_group(sp, 0, 0, g)
            load_v(sp, 0, 0)
            sp.dma_start(wo[:, :], w_o).then_inc(w_loaded, 16)
            sp.dma_start(g1b[:, :], over_partitions(g1)).then_inc(w_loaded, 16)
            sp.dma_start(b1b[:, :], over_partitions(b1)).then_inc(w_loaded, 16)
            sp.wait_ge(kones_made, 1)
            for q in range(2):
                sp.dma_start(kx[q][QK_ROWS:MAX_ROWS, :, :], kones[:, :].unsqueeze(1).broadcast_to([PARTS, AH, SEQ])).then_inc(kones_loaded, 16)
            for g in range(GROUPS):
                load_group(sp, 0, 1, g)
            load_v(sp, 0, 1)
            store_max(sp, 0, 0)

            def body(it, p, first, loads, last):
                row = Row(it, p)
                if not first:
                    sp.wait_ge(r_ready, Row(it, p - 1)(1, 0))
                    sp.dma_start(x1r[:, :, :], x1_rows[it * 2 + p - 1]).then_inc(x1r_loaded, 16)
                if loads:
                    sp.wait_ge(vx_ready, row(1, 1))
                    load_v(sp, it, p + 2)
                for g in range(GROUPS):
                    if g == GROUPS - 1 and not last:
                        store_max(sp, it, p + 1)
                    if loads:
                        sp.wait_ge(e_ps, row(NEXP, (g + 1) * NEXP // GROUPS))
                        load_group(sp, it, p + 2, g)
            body(0, 0, True, True, False)
            with sp.Fori(0, BATCH // 2 - 2) as it:
                body(it, 1, False, True, False)
                body(it, 2, False, True, False)
            last = BATCH // 2 - 1
            body(last, -1, False, True, False)
            body(last, 0, False, False, False)
            body(last, 1, False, False, True)
            sp.wait_ge(r_ready, BATCH - 1)
            sp.dma_start(x1r[:, :, :], x1_rows[BATCH - 1]).then_inc(x1r_loaded, 16)

        def spread_v(pool, it, p):
            row, q = Row(it, p), p % 2
            wait_apart(pool, v_loaded[q], times(it, p) * 16, pool_passed)
            nc.gpsimd.tensor_copy(vx[q][:, :, :, 0:DH], vtok[q][:, :, :].rearrange("p t (h d) -> p t h d", d=DH)).then_inc(vx_ready, 1)

        @block.gpsimd
        def _(pool):
            nc.gpsimd.memset(ones[:, :], 1.0).then_inc(consts, 1)
            nc.gpsimd.memset(minus_half[:, :], -0.5).then_inc(consts, 1)
            nc.gpsimd.memset(hide[:, :], -3e38).then_inc(consts, 1)
            pool.wait_ge(consts, 3)
            nc.gpsimd.affine_select(out=ident[:, :], in_=ones[:, :], compare_op=ALU.is_equal, fill=0.0, base=0,
                                    pattern=[[-1, P]], channel_multiplier=1).then_inc(consts, 1)
            nc.gpsimd.affine_select(out=ident16[:, :], in_=ones[:, :], compare_op=ALU.is_equal, fill=0.0, base=0,
                                    pattern=[[-1, P]], channel_multiplier=1).then_inc(consts, 1)
            nc.gpsimd.affine_select(out=hide[:, :], in_=hide[:, :], compare_op=ALU.is_gt, fill=0.0, base=0,
                                    pattern=[[1, P]], channel_multiplier=-1).then_inc(consts, 1)
            pool.wait_ge(vx_made, 2)
            spread_v(pool, 0, 0)

            def norm(it, p):
                row = Row(it, p)
                wait_apart(pool, var_ready, row(1, 1), pool_passed)
                nc.gpsimd.tensor_scalar(rstd[:, :], mv[:, :, 1], EPS, None, ALU.add).then_inc(rstd_ready, 1)
                pool.wait_ge(rstd_ready, row(2, 1))
                nc.gpsimd.tensor_tensor(rstd[:, :], rstd[:, :], minus_half[:, :], ALU.pow).then_inc(rstd_ready, 1)

            def gain(it, p):
                row = Row(it, p)
                pool.wait_ge(nrm_ready, row(1, 1))
                nc.gpsimd.tensor_tensor(h1[:, :, :], nrm[:, :, :], g1b[:, :].unsqueeze(1).broadcast_to([P, TILES, D]),
                                        ALU.mult).then_inc(gain_done, 1)
                pool.wait_ge(gain_done, row(1, 1))
                pool.wait_ge(h_stored, row(16, 0))
                nc.gpsimd.tensor_tensor(h[:, :, :], h1[:, :, :], b1b[:, :].unsqueeze(1).broadcast_to([P, TILES, D]),
                                        ALU.add).then_inc(h_ready, 1)
                pool.wait_ge(h_ready, row(1, 1))
                pool.dma_start(h_rows[it * 2 + p], h[:, :, :]).then_inc(h_stored, 16)

            def body(it, p, first, last):
                row = Row(it, p)
                for what, n in SCHEDULE:
                    if what == "exp":
                        g, kt, h0, heads = EXP_UNITS[n]
                        if h0 + heads == 4:
                            step = g * TILES + kt
                            wait_apart(pool, exp_ready, row(NEXP, n + 2), pool_passed)
                            nc.gpsimd.affine_select(out=pb[step % PBUF][:, :, 0:P], in_=pb[step % PBUF][:, :, 0:P],
                                                    compare_op=ALU.is_ge, fill=0.0, base=0,
                                                    pattern=[[0, 4], [1, P]], channel_multiplier=-1).then_inc(masked, 1)
                    elif what == "spread v" and not last:
                        if not first:
                            pool.wait_ge(pv_ps, row(STEPS, 0))
                        spread_v(pool, it, p + 1)
                    elif what == "last norm" and not first:
                        norm(it, p - 1)
                    elif what == "last gain" and not first:
                        gain(it, p - 1)
            all_rows(pool, body)
            norm(BATCH // 2 - 1, 1)
            gain(BATCH // 2 - 1, 1)
            pool.wait_ge(h_stored, 16 * BATCH)

        @block.scalar
        def _(act):
            act.sem_inc(exp_ready, 1)

            def exp_unit(row, u):
                g, kt, h0, heads = EXP_UNITS[u]
                step, width = g * TILES + kt, SEQ - kt * P
                stride = 512 if width > 256 else width
                src = ps[:, E_BANK + 2 * (u % 2):E_BANK + 2 * (u % 2) + 2, :].rearrange("p k n -> p (k n)")
                src = src[:, 0:heads * stride].rearrange("p (h n) -> p h n", n=stride)[:, :, 0:width]
                act.wait_ge(e_ps, row(NEXP, u + 1))
                used = row(STEPS, step + 1 - PBUF)
                if not (isinstance(used, int) and used <= 0):
                    act.wait_ge(pv_ps, used)
                nc.scalar.activation(pb[step % PBUF][:, h0:h0 + heads, 0:width], src, ACT.Exp).then_inc(exp_ready, 1)

            def oT_copy(row, g):
                act.wait_ge(pv_ps, row(STEPS, TILES * g + TILES))
                act.wait_ge(oTt_ps, row(GROUPS, g))
                nc.scalar.activation(oT[:, :], ps[:, PV_BANK, :], ACT.Copy).then_inc(oT_sb, 1)

            def oT2_copy(row):
                act.wait_ge(oT2_ps, row(1, 1))
                act.wait_ge(o_ps, row(1, 0))
                nc.scalar.activation(oT2[:, :], ps[:, MISC, :], ACT.Copy).then_inc(oT2_sb, 1)

            def body(it, p, first, last):
                row, before = Row(it, p), Row(it, p - 1)
                for what, n in SCHEDULE:
                    if what == "exp":
                        exp_unit(row, n)
                    elif what == "pv" and n % TILES == TILES - 1:
                        oT_copy(row, n // TILES)
                    elif what == "last pv" and n == STEPS - 1 and not first:
                        oT_copy(before, GROUPS - 1)
                    elif what == "last out" and not first:
                        oT2_copy(before)
            all_rows(act, body)
            end = Row(BATCH // 2 - 1, 1)
            oT_copy(end, GROUPS - 1)
            oT2_copy(end)

        @block.vector
        def _(dve):
            nc.vector.memset(kones[:, :], 1.0).then_inc(kones_made, 1)
            for q in range(2):
                nc.vector.memset(vx[q][:, :, :, :], 0.0).then_inc(vx_made, 1)
            dve.wait_ge(vx_made, 2)
            for q in range(2):
                nc.vector.memset(vx[q][:, :, :, DH:DH + 1], 1.0).then_inc(vx_made, 1)

            def max_unit(row, u):
                qt, h0, heads = MAX_UNITS[u]
                width = (qt + 1) * P
                dve.wait_ge(s_ps, row(NMAX, u + 1))
                nc.vector.tensor_reduce(mx[:, h0:h0 + heads, qt],
                                        ps[:, S_BANK + u % 2, 0:heads * width].rearrange("p (h n) -> p h n", n=width),
                                        AX.X, ALU.max).then_inc(mx_ready, 1)

            def max_rows(row, it, p):
                q = p % 2
                src = ps[0:TILES * AH, MISC, 0:P]
                dve.wait_ge(mxT_ps, row(1, 1))
                if not (isinstance(it, int) and times(it, p - 1) <= 0):
                    dve.wait_ge(mrows[1 - q], times(it, p - 1) * 16 * PARTS)
                nc.vector.tensor_scalar(mparts[:, 0, :], src, -1.0, None, ALU.mult).then_inc(mpart_ready, 1)
                dve.wait_ge(mpart_ready, row(4, 1))
                nc.vector.scalar_tensor_tensor(out=mrest[:, :], in0=src, scalar=-1.0, in1=mparts[:, 0, :],
                                               op0=ALU.mult, op1=ALU.subtract).then_inc(mpart_ready, 1)
                dve.wait_ge(mpart_ready, row(4, 2))
                nc.vector.tensor_copy(mparts[:, 1, :], mrest[:, :]).then_inc(mpart_ready, 1)
                dve.wait_ge(mpart_ready, row(4, 3))
                nc.vector.tensor_tensor(mparts[:, 2, :], mrest[:, :], mparts[:, 1, :], ALU.subtract).then_inc(mpart_ready, 1)

            def heads(row, g):
                src = ps[:, MISC, :].rearrange("p (t r n) -> p t r n", t=TILES, r=4)
                dve.wait_ge(oTt_ps, row(GROUPS, g + 1))
                dve.wait_ge(otok_ready, row(2 * GROUPS, 2 * g))
                nc.vector.reciprocal(rc[:, :, :, :], src[:, :, :, DH:DH + 1]).then_inc(otok_ready, 1)
                dve.wait_ge(otok_ready, row(2 * GROUPS, 2 * g + 1))
                if g == 0:
                    dve.wait_ge(oT2_ps, row(1, 0))
                nc.vector.tensor_tensor(otok[:, :, g * 32:(g + 1) * 32].rearrange("p t (r d) -> p t r d", r=4),
                                        src[:, :, :, 0:DH], rc[:, :, :, :].broadcast_to([P, TILES, 4, DH]),
                                        ALU.mult).then_inc(otok_ready, 1)

            def residual(row):
                dve.wait_ge(o_ps, row(1, 1))
                dve.wait_ge(x1r_loaded, row(16, 16))
                dve.wait_ge(nrm_ready, row(1, 0))
                nc.vector.tensor_tensor(r[:, :, :].rearrange("p t n -> p (t n)"), ps[:, MISC, :],
                                        x1r[:, :, :].rearrange("p t n -> p (t n)"), ALU.add).then_inc(r_ready, 1)
                dve.wait_ge(r_ready, row(1, 1))
                for t in range(TILES):
                    ins = nc.vector.bn_stats(bst[:, t, :], r[:, t, :])
                ins.then_inc(dve_own, 1)
                dve.wait_ge(rstd_ready, row(2, 0))
                wait_apart(dve, dve_own, row(1, 1), dve_passed)
                for t in range(TILES):
                    ins = nc.vector.bn_aggr(mv[:, t, :], bst[:, t, :])
                ins.then_inc(var_ready, 1)

            def normalise(row):
                dve.wait_ge(var_ready, row(1, 1))
                dve.wait_ge(rstd_ready, row(2, 2))
                dve.wait_ge(gain_done, row(1, 0))
                for t in range(TILES):
                    ins = nc.vector.tensor_scalar(nrm[:, t, :], r[:, t, :], mv[:, t, 0:1], rstd[:, t:t + 1],
                                                  ALU.subtract, ALU.mult)
                ins.then_inc(nrm_ready, 1)

            for u in range(NMAX):
                max_unit(Row(0, 0), u)
            max_rows(Row(0, 0), 0, 0)

            def body(it, p, first, last):
                row, before, after = Row(it, p), Row(it, p - 1), Row(it, p + 1)
                for what, n in SCHEDULE:
                    if what == "max" and not last:
                        max_unit(after, n)
                    elif what == "max rows" and not last:
                        max_rows(after, it, p + 1)
                    elif what == "heads":
                        heads(row, n)
                    elif what == "last heads" and not first:
                        heads(before, n)
                    elif what == "last norm" and not first:
                        residual(before)
                    elif what == "last normalise" and not first:
                        normalise(before)
            all_rows(dve, body)
            end = Row(BATCH // 2 - 1, 1)
            heads(end, GROUPS - 1)
            residual(end)
            normalise(end)

        @block.tensor
        def _(pe):
            pe.wait_ge(consts, 6)

            def max_unit(row, it, p, u):
                qt, h0, heads = MAX_UNITS[u]
                q, width = p % 2, (qt + 1) * P
                if u % (NMAX // GROUPS) == 0:
                    pe.wait_ge(qk_loaded[q][h0 // 4], times(it, p) * QK_LOADS)
                n = row(NMAX, u - 1)
                if not isinstance(n, int) or n > 0:
                    pe.wait_ge(mx_ready, n)
                for j in range(heads):
                    out = ps[:, S_BANK + u % 2, j * width:(j + 1) * width]
                    nc.tensor.matmul(out, qx[q][0:QK_ROWS, h0 + j, qt * P:(qt + 1) * P],
                                     kx[q][0:QK_ROWS, h0 + j, 0:width], start=True, stop=False)
                    ins = nc.tensor.matmul(out[:, qt * P:width], ident16[:, :], hide[:, :], start=False, stop=True)
                ins.then_inc(s_ps, 1)

            def max_rows(row):
                wait_apart(pe, mx_ready, row(NMAX, NMAX), pe_passed)
                nc.tensor.transpose(ps[0:TILES * AH, MISC, 0:P], mx[:, :, :].rearrange("p h t -> p (h t)"),
                                    ident[:, :]).then_inc(mxT_ps, 1)

            def exp_unit(row, it, p, u):
                g, kt, h0, heads = EXP_UNITS[u]
                q, width = p % 2, SEQ - kt * P
                stride = 512 if width > 256 else width
                if u == 0:
                    pe.wait_ge(mrows[q], times(it, p) * 16 * PARTS)
                pe.wait_ge(exp_ready, row(NEXP, u))
                for j in range(heads):
                    at = (E_BANK + 2 * (u % 2)) * 512 + j * stride
                    ins = nc.tensor.matmul(ps[:, at // 512, at % 512:at % 512 + width],
                                           kx[q][0:MAX_ROWS, 4 * g + h0 + j, kt * P:(kt + 1) * P],
                                           qx[q][0:MAX_ROWS, 4 * g + h0 + j, kt * P:SEQ], start=True, stop=True)
                ins.then_inc(e_ps, 1)

            def pv(row, it, p, step):
                g, kt = divmod(step, TILES)
                q, width = p % 2, SEQ - kt * P
                if step == 0:
                    pe.wait_ge(vx_ready, row(1, 1))
                if kt == 0:
                    pe.wait_ge(oT_sb, row(GROUPS, g))
                pe.wait_ge(masked, row(STEPS, step + 1))
                for j in range(4):
                    ins = nc.tensor.matmul(ps[32 * j:32 * (j + 1), PV_BANK, kt * P:SEQ], vx[q][:, kt, 4 * g + j, :],
                                           pb[step % PBUF][:, j, 0:width], start=(kt == 0), stop=(kt == TILES - 1))
                ins.then_inc(pv_ps, 1)

            def heads(row, g):
                pe.wait_ge(oT_sb, row(GROUPS, g + 1))
                pe.wait_ge(otok_ready, row(2 * GROUPS, 2 * g))
                for t in range(TILES):
                    ins = nc.tensor.transpose(ps[:, MISC, t * P:(t + 1) * P], oT[:, t * P:(t + 1) * P], ident[:, :])
                ins.then_inc(oTt_ps, 1)

            def out_proj(row):
                pe.wait_ge(otok_ready, row(2 * GROUPS, 2 * GROUPS))
                for t in range(TILES):
                    ins = nc.tensor.transpose(ps[:, MISC, t * P:(t + 1) * P], otok[:, t, :], ident[:, :])
                ins.then_inc(oT2_ps, 1)

            def out_proj2(row):
                pe.wait_ge(oT2_sb, row(1, 1))
                for t in range(TILES):
                    ins = nc.tensor.matmul(ps[:, MISC, t * P:(t + 1) * P], oT2[:, t * P:(t + 1) * P], wo[:, :],
                                           start=True, stop=True)
                ins.then_inc(o_ps, 1)

            for u in range(NMAX):
                max_unit(Row(0, 0), 0, 0, u)
            max_rows(Row(0, 0))
            pe.wait_ge(w_loaded, 48)
            pe.wait_ge(kones_loaded, 32)
            pe.wait_ge(vx_made, 4)

            def body(it, p, first, last):
                row, before, after = Row(it, p), Row(it, p - 1), Row(it, p + 1)
                for what, n in SCHEDULE:
                    if what == "exp":
                        exp_unit(row, it, p, n)
                    elif what == "max" and not last:
                        max_unit(after, it, p + 1, n)
                    elif what == "max rows" and not last:
                        pe.wait_ge(otok_ready, row(2 * GROUPS, 2 * 2))
                        max_rows(after)
                    elif what == "pv":
                        pv(row, it, p, n)
                    elif what == "last pv" and not first:
                        pv(before, it, p - 1, n)
                    elif what == "heads":
                        if n == 0:
                            if not first:
                                pe.wait_ge(r_ready, before(1, 1))
                        elif n == 2 and not last:
                            pe.wait_ge(mpart_ready, after(4, 2))
                        heads(row, n)
                    elif what == "last heads" and not first:
                        heads(before, n)
                    elif what == "last out" and not first:
                        out_proj(before)
                    elif what == "last norm" and not first:
                        out_proj2(before)
            all_rows(pe, body)
            end = Row(BATCH // 2 - 1, 1)
            for n in range(STEPS - LAG, STEPS):
                pv(end, BATCH // 2 - 1, 1, n)
            heads(end, GROUPS - 1)
            out_proj(end)
            out_proj2(end)
    end_stage(nc, sems)


E, TOPK, F = 8, 2, 512
FC = F // P
TOKENS = BATCH * SEQ
ALL_TILES = TOKENS // P
REGION = TOKENS + P
SLOTS = E * REGION + P
PAY = D + 1
RESULTS = TOPK * TOKENS
NOWHERE = 1 << 20
SLOT_TILES = RESULTS // P + E
ROUTE_STEPS = 29


def route(nc, h_dram, wg, slots, gates, table, w1, w2, w1s, w2s):
    sems = []
    with ExitStack() as ctx:
        def sb(name, shape, dt=F32):
            return ctx.enter_context(nc.sbuf_tensor(name, shape, dt))

        def pair(name, shape, dt=F32):
            return [sb(f"{name}{p}", shape, dt) for p in range(2)]

        def sem(name):
            sems.append(nc.alloc_semaphore(name))
            return sems[-1]

        wgs = sb("wgs", [P, E])
        count = sb("count", [P, E])
        ones = sb("ones_r", [P, P])
        ident = sb("ident_r", [P, P])
        before = sb("before", [P, P])
        rank = sb("rank", [P, E])
        region = sb("region", [P, E])
        fill_at = sb("fill_at", [P, E])
        fill_idx = sb("fill_idx", [P, E], U32)
        filler = sb("filler", [P, PAY])
        rows_of = sb("rows_of", [P, TOPK, ALL_TILES], U32)
        pay = [pair(f"pay{k}_", [P, TILES, PAY]) for k in range(TOPK)]
        hT = pair("hT_r", [P, SEQ])
        lg = sb("lg", [P, TILES, E])
        lg2 = sb("lg2", [P, TILES, E])
        m = [sb(f"m{k}", [P, TILES, 1]) for k in range(TOPK)]
        key = sb("key", [P, TILES, E])
        kmax = sb("kmax", [P, TILES, 1])
        sel = pair("sel", [P, TOPK, TILES, E])
        cnt = pair("cnt", [P, TILES, E])
        ex = sb("ex", [P, TILES])
        den = sb("den_r", [P, TILES])
        base = sb("base", [P, TILES, E])
        pos = sb("pos", [P, TILES, E])
        pick = sb("pick", [P, TILES, E])
        at = sb("at", [P, TILES])
        idx = [pair(f"idx{k}_", [P, TILES], U32) for k in range(TOPK)]
        ps = ctx.enter_context(nc.psum_tensor("psR", [P, 8, 512], F32))
        J, M = SLOT_TILES, TOKENS // P
        full = sb("full", [1, E, M])
        passed = sb("passed", [1, E, M])
        need = sb("need", [1, E, 1])
        upto = sb("upto_p", [1, E + 1])
        number = sb("number", [1, J])
        ids = sb("ids", [1, E])
        cmp = sb("cmp", [1, J, E])
        whose = sb("whose", [1, J, 1])
        begin = sb("begin", [1, J, 1])
        live = sb("live", [1, J, 1])
        slot = sb("slot", [1, J, 1])
        plan_own, moe_loaded = sem("plan_steps"), sem("moe_loaded_early")
        w_loaded, consts = sem("wg_loaded"), sem("route_constants")
        h_loaded = [sem(f"h_loaded{p}") for p in range(2)]
        scattered = [sem(f"scattered{p}") for p in range(2)]
        hT_ps, hT_sb, lg_ps, diff_ready, exp_ready = sem("hT_ps"), sem("hT_sb"), sem("lg_ps"), sem("diff_ready"), sem("rexp_ready")
        cnt_ready, pos_ps, idx_ready, fill_ready, filled = sem("cnt_ready"), sem("pos_ps"), sem("idx_ready"), sem("fill_ready"), sem("filled")
        dve_own = sem("dve_own_r")
        pool_passed, sp_passed = sem("pool_passed_r"), sem("sp_passed_r")
        block = ctx.enter_context(nc.Block())
        h_rows = h_dram.rearrange("b (t p) d -> b p t d", p=P)

        @block.sync
        def _(sp):
            sp.dma_start(wgs[:, :], wg).then_inc(w_loaded, 16)
            with sp.Fori(0, BATCH // 2) as it:
                for p in range(2):
                    wait_apart(sp, hT_ps, it * 2, sp_passed)
                    sp.wait_ge(scattered[p], it * (16 * TOPK * TILES))
                    for k in range(TOPK):
                        sp.dma_start(pay[k][p][:, :, 0:D], h_rows[it * 2 + p]).then_inc(h_loaded[p], 16)
            for e in range(E):
                sp.dma_start(w1s[:, e * F:(e + 1) * F], w1[e]).then_inc(moe_loaded, 16)
                sp.dma_start(w2s[:, e * F:(e + 1) * F].rearrange("p (c d) -> p c d", c=FC),
                             w2[e].rearrange("(c p) d -> p c d", p=P)).then_inc(moe_loaded, 16)
            sp.wait_ge(moe_loaded, 2 * E * 16)

        @block.gpsimd
        def _(pool):
            nc.gpsimd.memset(ones[:, :], 1.0).then_inc(consts, 1)
            nc.gpsimd.memset(filler[:, :], 0.0).then_inc(consts, 1)
            pool.wait_ge(consts, 2)
            nc.gpsimd.affine_select(out=ident[:, :], in_=ones[:, :], compare_op=ALU.is_equal, fill=0.0, base=0,
                                    pattern=[[-1, P]], channel_multiplier=1).then_inc(consts, 1)
            nc.gpsimd.affine_select(out=before[:, :], in_=ones[:, :], compare_op=ALU.is_gt, fill=0.0, base=0,
                                    pattern=[[1, P]], channel_multiplier=-1).then_inc(consts, 1)
            nc.gpsimd.iota(rank[:, :], pattern=[[-1, E]], base=E, channel_multiplier=0,
                           allow_small_or_imprecise_dtypes=True).then_inc(consts, 1)
            nc.gpsimd.iota(region[:, :], pattern=[[REGION, E]], base=0, channel_multiplier=0,
                           allow_small_or_imprecise_dtypes=True).then_inc(consts, 1)
            nc.gpsimd.iota(fill_at[:, :], pattern=[[REGION, E]], base=0, channel_multiplier=1,
                           allow_small_or_imprecise_dtypes=True).then_inc(consts, 1)
            nc.gpsimd.iota(rows_of[:, :, :], pattern=[[TOKENS, TOPK], [P, ALL_TILES]], base=0,
                           channel_multiplier=1).then_inc(consts, 1)
            nc.gpsimd.iota(filler[:, D:PAY].bitcast(U32), pattern=[[0, 1]], base=NOWHERE, channel_multiplier=0).then_inc(consts, 1)
            nc.gpsimd.iota(full[:, :, :], pattern=[[0, E], [P, M]], base=0, channel_multiplier=0,
                           allow_small_or_imprecise_dtypes=True).then_inc(consts, 1)
            nc.gpsimd.iota(number[:, :], pattern=[[1, J]], base=0, channel_multiplier=0,
                           allow_small_or_imprecise_dtypes=True).then_inc(consts, 1)
            nc.gpsimd.iota(ids[:, :], pattern=[[1, E]], base=0, channel_multiplier=0,
                           allow_small_or_imprecise_dtypes=True).then_inc(consts, 1)
            with pool.Fori(0, BATCH // 2) as it:
                for p in range(2):
                    row = Row(it, p)
                    for k in range(TOPK):
                        wait_apart(pool, idx_ready, row(TOPK, k + 1), pool_passed)
                        for t in range(TILES):
                            nc.gpsimd.indirect_dma_start(out=slots, out_offset=bass.IndirectOffsetOnAxis(ap=idx[k][p][:, t:t + 1], axis=0),
                                                         in_=pay[k][p][:, t, :], in_offset=None, bounds_check=SLOTS - 1,
                                                         oob_is_err=False).then_inc(scattered[p], 16)
            pool.wait_ge(fill_ready, 1)
            pool.dma_start(slots[E * REGION:SLOTS, :], filler[:, :]).then_inc(filled, 16)
            for e in range(E):
                nc.gpsimd.indirect_dma_start(out=slots, out_offset=bass.IndirectOffsetOnAxis(ap=fill_idx[:, e:e + 1], axis=0),
                                             in_=filler[:, :], in_offset=None, bounds_check=SLOTS - 1,
                                             oob_is_err=False).then_inc(filled, 16)
            for p in range(2):
                pool.wait_ge(scattered[p], 16 * TOPK * TILES * (BATCH // 2))
            pool.wait_ge(filled, 16 * (E + 1))

        @block.scalar
        def _(act):
            with act.Fori(0, BATCH // 2) as it:
                for p in range(2):
                    row = Row(it, p)
                    act.wait_ge(hT_ps, row(1, 1))
                    act.wait_ge(lg_ps, it * 2)
                    nc.scalar.activation(hT[p][:, :], ps[:, p, :], ACT.Copy).then_inc(hT_sb, 1)
                    act.wait_ge(diff_ready, row(1, 1))
                    nc.scalar.activation(ex[:, :], den[:, :], ACT.Exp).then_inc(exp_ready, 1)

        @block.vector
        def _(dve):
            nc.vector.memset(count[:, :], 0.0).then_inc(dve_own, 1)
            dve.wait_ge(dve_own, 1)
            dve.wait_ge(consts, 9)
            own = Chain(dve, dve_own, ROUTE_STEPS)
            with dve.Fori(0, BATCH // 2) as it:
                for p in range(2):
                    row = Row(it, p)
                    own.begin(lambda per, k, row=row: row(per, k) + 1)

                    def step(ins):
                        own.add(ins)
                        own.wait()

                    def bc(x, n=E):
                        return x.broadcast_to([P, TILES, n])
                    tiles = bass.ds(it * (2 * TILES) + p * TILES, TILES)
                    dve.wait_ge(scattered[p], it * (16 * TOPK * TILES))
                    for k in range(TOPK):
                        step(nc.vector.tensor_copy(pay[k][p][:, :, D:PAY].bitcast(U32), rows_of[:, k, tiles].unsqueeze(2)))
                    dve.wait_ge(lg_ps, row(1, 1))
                    step(nc.vector.tensor_copy(lg[:, :, :].rearrange("p t e -> p (t e)"), ps[:, 2 + p, 0:TILES * E]))
                    dve.wait_ge(pos_ps, it * 2)
                    src = lg
                    for k in range(TOPK):
                        step(nc.vector.tensor_reduce(m[k][:, :, :], src[:, :, :], AX.X, ALU.max))
                        step(nc.vector.tensor_tensor(key[:, :, :], src[:, :, :], bc(m[k][:, :, :]), ALU.is_equal))
                        step(nc.vector.tensor_tensor(key[:, :, :], key[:, :, :], rank[:, :].unsqueeze(1).broadcast_to([P, TILES, E]), ALU.mult))
                        step(nc.vector.tensor_reduce(kmax[:, :, :], key[:, :, :], AX.X, ALU.max))
                        step(nc.vector.tensor_tensor(sel[p][:, k, :, :], key[:, :, :], bc(kmax[:, :, :]), ALU.is_equal))
                        if k == 0:
                            step(nc.vector.scalar_tensor_tensor(out=lg2[:, :, :], in0=sel[p][:, 0, :, :], scalar=-3e38,
                                                                in1=lg[:, :, :], op0=ALU.mult, op1=ALU.add))
                            src = lg2
                    nc.vector.tensor_tensor(cnt[p][:, :, :], sel[p][:, 0, :, :], sel[p][:, 1, :, :], ALU.add).then_inc(cnt_ready, 1)
                    nc.vector.tensor_tensor(den[:, :], m[1][:, :, 0], m[0][:, :, 0], ALU.subtract).then_inc(diff_ready, 1)
                    dve.wait_ge(exp_ready, row(1, 1))
                    step(nc.vector.tensor_scalar(den[:, :], ex[:, :], 1.0, None, ALU.add))
                    step(nc.vector.reciprocal(den[:, :], den[:, :]))
                    step(nc.vector.tensor_copy(gates[:, 0, tiles], den[:, :]))
                    step(nc.vector.tensor_tensor(gates[:, 1, tiles], den[:, :], ex[:, :], ALU.mult))
                    dve.wait_ge(pos_ps, row(1, 1))
                    step(nc.vector.tensor_copy(base[:, 0, :], count[:, :]))
                    for t in range(1, TILES):
                        step(nc.vector.tensor_tensor(base[:, t, :], ps[:, 6 + p, (t - 1) * E:t * E], base[:, t - 1, :], ALU.add))
                    step(nc.vector.tensor_tensor(count[:, :], ps[:, 6 + p, (TILES - 1) * E:TILES * E], base[:, TILES - 1, :], ALU.add))
                    step(nc.vector.tensor_tensor(pos[:, :, :], ps[:, 4 + p, 0:TILES * E].rearrange("p (t e) -> p t e", e=E), base[:, :, :], ALU.add))
                    step(nc.vector.tensor_tensor(pos[:, :, :], pos[:, :, :], region[:, :].unsqueeze(1).broadcast_to([P, TILES, E]), ALU.add))
                    for k in range(TOPK):
                        step(nc.vector.tensor_tensor(pick[:, :, :], sel[p][:, k, :, :], pos[:, :, :], ALU.mult))
                        step(nc.vector.tensor_reduce(at[:, :], pick[:, :, :], AX.X, ALU.add))
                        nc.vector.tensor_copy(idx[k][p][:, :], at[:, :]).then_inc(idx_ready, 1)
                        dve.wait_ge(idx_ready, row(TOPK, k + 1))
                    own.end()
            nc.vector.tensor_tensor(fill_at[:, :], fill_at[:, :], count[:, :], ALU.add).then_inc(dve_own, 1)
            dve.wait_ge(dve_own, 2 + ROUTE_STEPS * BATCH)
            nc.vector.tensor_copy(fill_idx[:, :], fill_at[:, :]).then_inc(fill_ready, 1)

            planned = [0]

            def step(ins):
                planned[0] += 1
                ins.then_inc(plan_own, 1)
                dve.wait_ge(plan_own, planned[0])
            v = nc.vector
            dve.wait_ge(consts, 12)
            step(v.tensor_tensor(passed[:, :, :], count[0:1, :].unsqueeze(2).broadcast_to([1, E, M]), full[:, :, :], ALU.is_gt))
            step(v.tensor_reduce(need[:, :, :], passed[:, :, :], AX.X, ALU.add))
            step(v.memset(upto[:, 0:1], 0.0))
            for e in range(E):
                step(v.tensor_tensor(upto[:, e + 1:e + 2], upto[:, e:e + 1], need[:, e, :], ALU.add))
            num = number[:, :].unsqueeze(2).broadcast_to([1, J, E])
            step(v.tensor_tensor(cmp[:, :, :], upto[:, 1:E + 1].unsqueeze(1).broadcast_to([1, J, E]), num, ALU.is_le))
            step(v.tensor_reduce(whose[:, :, :], cmp[:, :, :], AX.X, ALU.add))
            step(v.tensor_tensor(cmp[:, :, :], ids[:, :].unsqueeze(1).broadcast_to([1, J, E]), whose[:, :, :].broadcast_to([1, J, E]), ALU.is_equal))
            step(v.tensor_tensor(cmp[:, :, :], cmp[:, :, :], upto[:, 0:E].unsqueeze(1).broadcast_to([1, J, E]), ALU.mult))
            step(v.tensor_reduce(begin[:, :, :], cmp[:, :, :], AX.X, ALU.add))
            step(v.tensor_scalar(live[:, :, :], whose[:, :, :], float(E), float(P), ALU.is_lt, ALU.mult))
            step(v.tensor_tensor(slot[:, :, 0], number[:, :], begin[:, :, 0], ALU.subtract))
            step(v.tensor_tensor(slot[:, :, :], slot[:, :, :], live[:, :, :], ALU.mult))
            step(v.scalar_tensor_tensor(out=slot[:, :, :], in0=whose[:, :, :], scalar=float(REGION), in1=slot[:, :, :],
                                        op0=ALU.mult, op1=ALU.add))
            step(v.tensor_copy(table[:, 0, :], slot[:, :, 0]))
            step(v.tensor_scalar(whose[:, :, :], whose[:, :, :], float(E - 1), None, ALU.min))
            step(v.tensor_scalar(table[:, 1, :], whose[:, :, 0], float(D + FC), None, ALU.mult))
            step(v.tensor_scalar(table[:, 2, :], whose[:, :, 0], float(F), None, ALU.mult))

        @block.tensor
        def _(pe):
            pe.wait_ge(w_loaded, 16)
            pe.wait_ge(consts, 9)
            with pe.Fori(0, BATCH // 2) as it:
                for p in range(2):
                    row = Row(it, p)
                    pe.wait_ge(h_loaded[p], it * (16 * TOPK) + 16 * TOPK)
                    pe.wait_ge(hT_sb, it * 2)
                    for t in range(TILES):
                        ins = nc.tensor.transpose(ps[:, p, t * P:(t + 1) * P], pay[0][p][:, t, 0:D], ident[:, :])
                    ins.then_inc(hT_ps, 1)
                    pe.wait_ge(hT_sb, row(1, 1))
                    pe.wait_ge(cnt_ready, it * 2)
                    for t in range(TILES):
                        ins = nc.tensor.matmul(ps[:, 2 + p, t * E:(t + 1) * E], hT[p][:, t * P:(t + 1) * P], wgs[:, :],
                                               start=True, stop=True)
                    ins.then_inc(lg_ps, 1)
                    pe.wait_ge(cnt_ready, row(1, 1))
                    pe.wait_ge(idx_ready, it * (2 * TOPK))
                    nc.tensor.matmul(ps[:, 4 + p, 0:TILES * E], before[:, :], cnt[p][:, :, :].rearrange("p t e -> p (t e)"),
                                     start=True, stop=True)
                    nc.tensor.matmul(ps[:, 6 + p, 0:TILES * E], ones[:, :], cnt[p][:, :, :].rearrange("p t e -> p (t e)"),
                                     start=True, stop=True).then_inc(pos_ps, 1)
    end_stage(nc, sems)


RING = 4
BIAS = D + FC


class Tile:

    def __init__(self, it, p):
        self.it, self.p = it, p
        self.j = it * RING + p
        self.turn = it + p // RING
        self.ring, self.pair = p % RING, p % 2

    def shift(self, d):
        if isinstance(self.it, int) and not 0 <= self.j + d < SLOT_TILES:
            return None
        return Tile(self.it, self.p + d)

    def done(self, before=0):
        if isinstance(self.it, int) and self.j + 1 - before <= 0:
            return None
        return self.it * RING + (self.p + 1 - before)


def all_tiles(eng, body):
    for p in range(RING):
        body(Tile(0, p))
    with eng.Fori(1, SLOT_TILES // RING - 1) as it:
        for p in range(RING):
            body(Tile(it, p))
    for p in range(RING):
        body(Tile(SLOT_TILES // RING - 1, p))


def experts(nc, slots, w1s, bb1, w2s, bb2, table, results):
    sems = []
    with ExitStack() as ctx:
        def sb(name, shape, dt=F32):
            return ctx.enter_context(nc.sbuf_tensor(name, shape, dt))

        def ring(name, n, shape, dt=F32):
            return [sb(f"{name}{p}", shape, dt) for p in range(n)]

        def sem(name):
            sems.append(nc.alloc_semaphore(name))
            return sems[-1]

        b1s = sb("b1s", [E * FC, P])
        biases = sb("biases", [P, E, BIAS])
        ones = sb("ones_e", [P, P])
        ident = sb("ident_e", [P, P])
        hin = ring("hin", RING, [P, PAY])
        dest = ring("dest", RING, [P, 1], U32)
        y = ring("y_e", RING, [P, D])
        w1t = ring("w1t", 2, [P, F])
        hT = ring("hT_e", 2, [P, P])
        pre = ring("pre", 2, [P, FC, P])
        gT = ring("gT", 2, [P, FC, P])
        ps = ctx.enter_context(nc.psum_tensor("psE", [P, 8, 512], F32))
        HT_BANK, UP_BANK, Y_BANK = 0, 2, 4
        w_loaded, consts = sem("moe_biases"), sem("moe_constants")
        b1_ps, b1_ready = sem("b1_ps"), sem("b1_ready")
        h_loaded = [sem(f"slots_loaded{p}") for p in range(RING)]
        stored = [sem(f"results_stored{p}") for p in range(RING)]
        hT_ps, hT_sb, w1_ready, up_ps, pre_ready, g_ready = sem("ehT_ps"), sem("ehT_sb"), sem("w1_ready"), sem("up_ps"), sem("pre_ready"), sem("g_ready")
        y_ps, y_ready, dest_ready = sem("y_ps"), sem("ey_ready"), sem("dest_ready")
        pool_passed = sem("pool_passed_e")
        block = ctx.enter_context(nc.Block())

        def offset(eng, row, tile, bound):
            cell = table[0:1, row, tile.j:tile.j + 1] if isinstance(tile.j, int) else table[0:1, row, bass.ds(tile.j, 1)]
            return eng.value_load(cell, min_val=0, max_val=bound)

        def wait(eng, sem, value):
            if value is not None:
                eng.wait_ge(sem, value)

        @block.sync
        def _(sp):
            def load(tile):
                at = offset(sp, 0, tile, SLOTS - P)
                wait(sp, hT_ps, tile.done(RING))
                wait(sp, dest_ready, tile.done(RING))
                sp.dma_start(hin[tile.ring][:, :], slots[bass.ds(at, P), :]).then_inc(h_loaded[tile.ring], 16)

            for p in range(RING - 1):
                load(Tile(0, p))
            sp.dma_start(b1s[:, :], bb1.rearrange("e (c p) -> (e c) p", p=P)).then_inc(w_loaded, 16)
            sp.dma_start(biases[:, :, 0:D], over_partitions(bb2)).then_inc(w_loaded, 16)

            def body(tile):
                if tile.shift(RING - 1):
                    load(tile.shift(RING - 1))
            all_tiles(sp, body)

        @block.gpsimd
        def _(pool):
            nc.gpsimd.memset(ones[:, :], 1.0).then_inc(consts, 1)
            pool.wait_ge(consts, 1)
            nc.gpsimd.affine_select(out=ident[:, :], in_=ones[:, :], compare_op=ALU.is_equal, fill=0.0, base=0,
                                    pattern=[[-1, P]], channel_multiplier=1).then_inc(consts, 1)

            def body(tile):
                wait_apart(pool, y_ready, tile.done(), pool_passed)
                nc.gpsimd.indirect_dma_start(out=results, out_offset=bass.IndirectOffsetOnAxis(ap=dest[tile.ring][:, 0:1], axis=0),
                                             in_=y[tile.ring][:, :], in_offset=None, bounds_check=RESULTS - 1,
                                             oob_is_err=False).then_inc(stored[tile.ring], 16)
            all_tiles(pool, body)
            for q in range(RING):
                pool.wait_ge(stored[q], 16 * (SLOT_TILES // RING))

        @block.scalar
        def _(act):
            def weights(tile):
                at = offset(act, 2, tile, (E - 1) * F)
                wait(act, up_ps, tile.done(2))
                nc.scalar.activation(w1t[tile.pair][:, :], w1s[:, bass.ds(at, F)], ACT.Copy).then_inc(w1_ready, 1)

            def turned(tile):
                act.wait_ge(hT_ps, tile.done())
                wait(act, up_ps, tile.done(2))
                nc.scalar.activation(hT[tile.pair][:, :], ps[:, HT_BANK + tile.pair, 0:P], ACT.Copy).then_inc(hT_sb, 1)

            def gelu(tile):
                act.wait_ge(pre_ready, tile.done())
                wait(act, y_ps, tile.done(2))
                nc.scalar.activation(gT[tile.pair][:, :, :], pre[tile.pair][:, :, :], ACT.Gelu_apprx_tanh).then_inc(g_ready, 1)

            act.wait_ge(w_loaded, 32)
            for p in range(2):
                weights(Tile(0, p))
                turned(Tile(0, p))

            def body(tile):
                gelu(tile)
                if tile.shift(2):
                    weights(tile.shift(2))
                    turned(tile.shift(2))
            all_tiles(act, body)

        @block.vector
        def _(dve):
            dve.wait_ge(w_loaded, 32)
            dve.wait_ge(b1_ps, 1)
            nc.vector.tensor_copy(biases[:, :, D:BIAS], ps[:, Y_BANK, 0:E * FC].rearrange("p (e c) -> p e c", c=FC)).then_inc(b1_ready, 1)
            dve.wait_ge(b1_ready, 1)
            flat = biases[:, :, :].rearrange("p e n -> p (e n)")

            def rows(tile):
                dve.wait_ge(h_loaded[tile.ring], (tile.turn + 1) * 16)
                dve.wait_ge(stored[tile.ring], tile.turn * 16)
                nc.vector.tensor_copy(dest[tile.ring][:, :], hin[tile.ring][:, D:PAY].bitcast(U32)).then_inc(dest_ready, 1)

            def bias(tile, at):
                dve.wait_ge(up_ps, tile.done())
                wait(dve, g_ready, tile.done(2))
                nc.vector.tensor_tensor(pre[tile.pair][:, :, :], ps[:, UP_BANK + tile.pair, :].rearrange("p (c n) -> p c n", c=FC),
                                        flat[:, bass.ds(at + D, FC)].unsqueeze(2).broadcast_to([P, FC, P]),
                                        ALU.add).then_inc(pre_ready, 1)

            def result(tile, at):
                dve.wait_ge(y_ps, tile.done())
                dve.wait_ge(dest_ready, tile.done())
                nc.vector.tensor_tensor(y[tile.ring][:, :], ps[:, Y_BANK + tile.pair, 0:D], flat[:, bass.ds(at, D)],
                                        ALU.add).then_inc(y_ready, 1)

            def body(tile):
                at = offset(dve, 1, tile, (E - 1) * BIAS)
                rows(tile)
                bias(tile, at)
                before = tile.shift(-1)
                if before:
                    result(before, offset(dve, 1, before, (E - 1) * BIAS))
            all_tiles(dve, body)
            last = Tile(SLOT_TILES // RING - 1, RING - 1)
            result(last, offset(dve, 1, last, (E - 1) * BIAS))

        @block.tensor
        def _(pe):
            pe.wait_ge(w_loaded, 32)
            pe.wait_ge(consts, 2)
            nc.tensor.transpose(ps[:, Y_BANK, 0:E * FC], b1s[:, :], ident[0:E * FC, 0:E * FC]).then_inc(b1_ps, 1)
            pe.wait_ge(b1_ready, 1)

            def turn(tile):
                pe.wait_ge(h_loaded[tile.ring], (tile.turn + 1) * 16)
                wait(pe, hT_sb, tile.done(2))
                nc.tensor.transpose(ps[:, HT_BANK + tile.pair, 0:P], hin[tile.ring][:, 0:D], ident[:, :]).then_inc(hT_ps, 1)

            def up(tile):
                pe.wait_ge(hT_sb, tile.done())
                pe.wait_ge(w1_ready, tile.done())
                wait(pe, pre_ready, tile.done(2))
                for c in range(FC):
                    ins = nc.tensor.matmul(ps[:, UP_BANK + tile.pair, c * P:(c + 1) * P], w1t[tile.pair][:, c * P:(c + 1) * P],
                                           hT[tile.pair][:, :], start=True, stop=True)
                ins.then_inc(up_ps, 1)

            def down(tile, at):
                pe.wait_ge(g_ready, tile.done())
                wait(pe, y_ready, tile.done(2))
                for c in range(FC):
                    ins = nc.tensor.matmul(ps[:, Y_BANK + tile.pair, 0:D], gT[tile.pair][:, c, :], w2s[:, bass.ds(at + c * D, D)],
                                           start=(c == 0), stop=(c == FC - 1))
                ins.then_inc(y_ps, 1)

            turn(Tile(0, 0))
            turn(Tile(0, 1))
            up(Tile(0, 0))

            def body(tile):
                at = offset(pe, 2, tile, (E - 1) * F)
                if tile.shift(1):
                    up(tile.shift(1))
                if tile.shift(2):
                    turn(tile.shift(2))
                down(tile, at)
            all_tiles(pe, body)
    end_stage(nc, sems)


def last_norms(nc, x1_dram, h_dram, results, gates, g2, b2, out):
    sems = []
    with ExitStack() as ctx:
        def sb(name, shape, dt=F32):
            return ctx.enter_context(nc.sbuf_tensor(name, shape, dt))

        def pair(name, shape, dt=F32):
            return [sb(f"{name}{p}", shape, dt) for p in range(2)]

        def sem(name):
            sems.append(nc.alloc_semaphore(name))
            return sems[-1]
        g2b, b2b = sb("g2b", [P, D]), sb("b2b", [P, D])
        minus_half = sb("minus_half_l", [P, TILES])
        x1, h = pair("x1_l", [P, TILES, D]), pair("h_l", [P, TILES, D])
        ys = pair("ys", [P, TOPK, TILES, D])
        s = [sb(f"s{k}", [P, TILES, D]) for k in range(TOPK)]
        bst, mv, rs = [[sb(f"{n}{k}_l", sh) for k in range(2)] for n, sh in (("bst", [P, TILES, 6]), ("mv", [P, TILES, 2]), ("rs", [P, TILES]))]
        n1, n2, n3 = sb("n1", [P, TILES, D]), sb("n2", [P, TILES, D]), sb("n3", [P, TILES, D])
        r = sb("r_l", [P, TILES, D])
        o = pair("o_l", [P, TILES, D])
        loaded = [sem(f"moe_loaded{p}") for p in range(2)]
        x1_loaded = [sem(f"x1_loaded_l{p}") for p in range(2)]
        stored = [sem(f"out_stored{p}") for p in range(2)]
        w_loaded, consts = sem("g2_loaded"), sem("last_constants")
        sum_ready, var_ready, rstd_ready = sem("moe_sum"), [sem(f"lvar_ready{k}") for k in range(2)], [sem(f"lrstd_ready{k}") for k in range(2)]
        stats_ready = [sem(f"lstats{k}") for k in range(2)]
        n1_ready, gain_ready, r_ready, o_ready = sem("ln1_ready"), sem("lgain_ready"), sem("lr_ready"), sem("o_ready")
        pool_passed, dve_passed = sem("pool_passed_l"), sem("dve_passed_l")
        block = ctx.enter_context(nc.Block())
        MOE_LOADS = 16 * (TOPK + 1)

        def by_tile(x):
            return x.rearrange("b (t p) d -> b p t d", p=P)

        @block.sync
        def _(sp):
            res = results.rearrange("(k b t p) d -> k b p t d", k=TOPK, b=BATCH, p=P)

            def load_moe(it, p):
                q, b = p % 2, it * 2 + p
                sp.dma_start(h[q][:, :, :], by_tile(h_dram)[b]).then_inc(loaded[q], 16)
                for k in range(TOPK):
                    sp.dma_start(ys[q][:, k, :, :], res[k, b]).then_inc(loaded[q], 16)

            def load_x1(it, p):
                sp.dma_start(x1[p % 2][:, :, :], by_tile(x1_dram)[it * 2 + p]).then_inc(x1_loaded[p % 2], 16)

            def store(it, p):
                sp.wait_ge(o_ready, Row(it, p)(1, 1))
                sp.dma_start(by_tile(out)[it * 2 + p], o[p % 2][:, :, :]).then_inc(stored[p % 2], 16)

            load_moe(0, 0)
            sp.dma_start(g2b[:, :], over_partitions(g2)).then_inc(w_loaded, 16)
            sp.dma_start(b2b[:, :], over_partitions(b2)).then_inc(w_loaded, 16)
            load_x1(0, 0)
            load_moe(0, 1)
            load_x1(0, 1)
            with sp.Fori(0, BATCH // 2 - 1) as it:
                for p in range(2):
                    row = Row(it, p)
                    sp.wait_ge(sum_ready, row(TOPK, TOPK))
                    load_moe(it, p + 2)
                    sp.wait_ge(r_ready, row(1, 1))
                    load_x1(it, p + 2)
                    store(it, p)
            for p in range(2):
                store(BATCH // 2 - 1, p)
            for p in range(2):
                sp.wait_ge(stored[p], 16 * (BATCH // 2))

        @block.gpsimd
        def _(pool):
            nc.gpsimd.memset(minus_half[:, :], -0.5).then_inc(consts, 1)
            pool.wait_ge(consts, 1)
            pool.wait_ge(w_loaded, 32)

            def rstd(row, k):
                wait_apart(pool, var_ready[k], row(1, 1), pool_passed)
                nc.gpsimd.tensor_scalar(rs[k][:, :], mv[k][:, :, 1], EPS, None, ALU.add).then_inc(rstd_ready[k], 1)
                pool.wait_ge(rstd_ready[k], row(2, 1))
                nc.gpsimd.tensor_tensor(rs[k][:, :], rs[k][:, :], minus_half[:, :], ALU.pow).then_inc(rstd_ready[k], 1)

            def gain(row):
                pool.wait_ge(n1_ready, row(1, 1))
                nc.gpsimd.tensor_tensor(n2[:, :, :], n1[:, :, :], g2b[:, :].unsqueeze(1).broadcast_to([P, TILES, D]),
                                        ALU.mult).then_inc(gain_ready, 1)
                pool.wait_ge(gain_ready, row(2, 1))
                pool.wait_ge(r_ready, row(1, 0))
                nc.gpsimd.tensor_tensor(n3[:, :, :], n2[:, :, :], b2b[:, :].unsqueeze(1).broadcast_to([P, TILES, D]),
                                        ALU.add).then_inc(gain_ready, 1)

            def body(it, p, first, last):
                rstd(Row(it, p), 0)
                if not first:
                    rstd(Row(it, p - 1), 1)
                gain(Row(it, p))
            all_rows(pool, body)
            rstd(Row(BATCH // 2 - 1, 1), 1)

        @block.vector
        def _(dve):
            def moments(row, x, k):
                for t in range(TILES):
                    ins = nc.vector.bn_stats(bst[k][:, t, :], x[:, t, :])
                ins.then_inc(stats_ready[k], 1)
                wait_apart(dve, stats_ready[k], row(1, 1), dve_passed)
                for t in range(TILES):
                    ins = nc.vector.bn_aggr(mv[k][:, t, :], bst[k][:, t, :])
                ins.then_inc(var_ready[k], 1)

            def moe_sum(row, it, p):
                q = p % 2
                dve.wait_ge(loaded[q], (it + p // 2 + 1) * MOE_LOADS)
                dve.wait_ge(n1_ready, row(1, 0))
                src = h[q]
                for k in range(TOPK):
                    for t in range(TILES):
                        ins = nc.vector.scalar_tensor_tensor(out=s[k][:, t, :], in0=ys[q][:, k, t, :],
                                                             scalar=gates[:, k, bass.ds(it * (2 * TILES) + (p * TILES + t), 1)],
                                                             in1=src[:, t, :], op0=ALU.mult, op1=ALU.add)
                    ins.then_inc(sum_ready, 1)
                    dve.wait_ge(sum_ready, row(TOPK, k + 1))
                    src = s[k]
                moments(row, src, 0)

            def residual(row, p, it):
                q = p % 2
                dve.wait_ge(gain_ready, row(2, 2))
                dve.wait_ge(x1_loaded[q], (it + p // 2 + 1) * 16)
                dve.wait_ge(o_ready, row(1, 0))
                nc.vector.tensor_tensor(r[:, :, :], n3[:, :, :], x1[q][:, :, :], ALU.add).then_inc(r_ready, 1)
                dve.wait_ge(r_ready, row(1, 1))
                moments(row, r, 1)

            def first_norm(row):
                dve.wait_ge(var_ready[0], row(1, 1))
                dve.wait_ge(rstd_ready[0], row(2, 2))
                dve.wait_ge(gain_ready, row(2, 0))
                for t in range(TILES):
                    ins = nc.vector.tensor_scalar(n1[:, t, :], s[TOPK - 1][:, t, :], mv[0][:, t, 0:1], rs[0][:, t:t + 1],
                                                  ALU.subtract, ALU.mult)
                ins.then_inc(n1_ready, 1)

            def second_norm(row, it, p):
                dve.wait_ge(var_ready[1], row(1, 1))
                dve.wait_ge(rstd_ready[1], row(2, 2))
                dve.wait_ge(stored[p % 2], (it + p // 2) * 16)
                for t in range(TILES):
                    ins = nc.vector.tensor_scalar(o[p % 2][:, t, :], r[:, t, :], mv[1][:, t, 0:1], rs[1][:, t:t + 1],
                                                  ALU.subtract, ALU.mult)
                ins.then_inc(o_ready, 1)

            def body(it, p, first, last):
                row, before = Row(it, p), Row(it, p - 1)
                moe_sum(row, it, p)
                if not first:
                    residual(before, p - 1, it)
                first_norm(row)
                if not first:
                    second_norm(before, it, p - 1)
            all_rows(dve, body)
            end = Row(BATCH // 2 - 1, 1)
            residual(end, 1, BATCH // 2 - 1)
            second_norm(end, BATCH // 2 - 1, 1)
    end_stage(nc, sems)


def layer(nc, X, W_in, conv_w, conv_b, dt_bias, A_log, Dskip, norm_w, W_out,
          w_qkv, w_o, g1, b1, wg, w1, bb1, w2, bb2, g2, b2, out):
    def dram(name, shape, dt=F32):
        return nc.dram_tensor(name, shape, dt, kind="Internal").ap()

    x1 = dram("x1_rows", (BATCH, SEQ, D))
    q_parts = dram("q_parts", (BATCH, PARTS, D, SEQ), BF16)
    k_parts = dram("k_parts", (BATCH, PARTS, D, SEQ), BF16)
    v = dram("v_rows", (BATCH, SEQ, D))
    h = dram("h_rows", (BATCH, SEQ, D))
    slots = dram("slots", (SLOTS, PAY))
    results = dram("results", (RESULTS, D))

    mamba_layer(nc, X, W_in, conv_w, conv_b, dt_bias, A_log, Dskip, norm_w, W_out, x1)
    qkv_projection(nc, x1, w_qkv, q_parts, k_parts, v)
    attention_layer(nc, x1, q_parts, k_parts, v, w_o, g1, b1, h)
    with nc.sbuf_tensor("gates", [P, TOPK, ALL_TILES], F32) as gates, \
            nc.sbuf_tensor("table", [1, 3, SLOT_TILES], U32) as table:
        with nc.sbuf_tensor("w1s", [P, E * F], F32) as w1s, nc.sbuf_tensor("w2s", [P, E * F], F32) as w2s:
            route(nc, h, wg, slots, gates, table, w1, w2, w1s, w2s)
            experts(nc, slots, w1s, bb1, w2s, bb2, table, results)
        last_norms(nc, x1, h, results, gates, g2, b2, out)


INPUTS = ["L0_attn_X", "L0_attn_W_in", "L0_attn_conv_w", "L0_attn_conv_b", "L0_attn_dt_bias", "L0_attn_A_log",
          "L0_attn_D", "L0_attn_norm_w", "L0_attn_W_out", "L0_ffn_w_qkv", "L0_ffn_w_o", "L0_ffn_g1", "L0_ffn_b1",
          "L0_ffn_wg", "L0_ffn_w1", "L0_ffn_bb1", "L0_ffn_w2", "L0_ffn_bb2", "L0_ffn_g2", "L0_ffn_b2"]


def kernel(**inputs):
    import numpy as np
    import concourse.bacc as bacc
    from concourse.bass_utils import run_bass_kernel_spmd

    nc = bacc.Bacc("TRN2", target_bir_lowering=False, num_devices=1)
    arrays, args = {}, []
    for name in INPUTS:
        a = np.ascontiguousarray(inputs[name])
        arrays[f"in_{name}"] = a
        args.append(nc.dram_tensor(f"in_{name}", a.shape, mybir.dt.from_np(a.dtype), kind="ExternalInput").ap())
    out = nc.dram_tensor("out_rows", (BATCH, SEQ, D), F32, kind="ExternalOutput").ap()
    layer(nc, *args, out)
    result = run_bass_kernel_spmd(nc, [arrays], core_ids=[0])
    return result.results[0]["out_rows"]
```
